# Optimizing a Trainium2 kernel written in Bass

```python
import numpy as np
import jax
import jax.numpy as jnp

def _softmax(x, axis=-1):
    return jax.nn.softmax(x, axis=axis)

def _gelu(x):
    return jax.nn.gelu(x, approximate=True)

def _silu(x):
    return jax.nn.silu(x)

def _sigmoid(x):
    return jax.nn.sigmoid(x)

def _layernorm(x, axis=-1, eps=1e-05):
    m = jnp.mean(x, axis=axis, keepdims=True)
    v = jnp.var(x, axis=axis, keepdims=True)
    return (x - m) / jnp.sqrt(v + eps)

def _scatter_add(tgt, idx, src, axis=0):
    return tgt.at[idx].add(src)

def _segment_sum(src, seg, n):
    return jax.ops.segment_sum(src, seg, n)
kernel_name = 'mk_sandwich_d1_jaxref_r8_b5ac5e'

def setup_inputs(seed: int=0):
    np.random.seed(seed)
    _w = jnp.asarray

    def _L0_attn_setup():
        import jax, jax.numpy as jnp
        import numpy as np
        N_HIDDEN = 128
        N_HEADS = 16
        HEAD_DIM = N_HIDDEN // N_HEADS
        KERNEL = 4
        GN_EPS = 1e-05

        def _short_conv_1d(x, weight):
            F, K = weight.shape
            xp = jnp.pad(x, ((0, 0), (K - 1, 0), (0, 0)))
            shifts = jnp.stack([xp[:, i:i + x.shape[1], :] for i in range(K)], axis=-1)
            return jnp.sum(shifts * weight[None, None, :, :], axis=-1)
        key = jax.random.key(seed)
        ks = jax.random.split(key, 16)
        B, S = (4, 512)
        H, Hd = (N_HEADS, N_HIDDEN)
        sc = 0.02
        inp = {'x': jax.random.normal(ks[0], (B, S, Hd), dtype=jnp.float32), 'Wq': jax.random.normal(ks[1], (Hd, Hd), dtype=jnp.float32) * sc, 'bq': jnp.zeros((Hd,), jnp.float32), 'Wk': jax.random.normal(ks[2], (Hd, Hd), dtype=jnp.float32) * sc, 'bk': jnp.zeros((Hd,), jnp.float32), 'Wv': jax.random.normal(ks[3], (Hd, Hd), dtype=jnp.float32) * sc, 'bv': jnp.zeros((Hd,), jnp.float32), 'q_conv': jax.random.normal(ks[4], (Hd, KERNEL), dtype=jnp.float32) * sc, 'k_conv': jax.random.normal(ks[5], (Hd, KERNEL), dtype=jnp.float32) * sc, 'v_conv': jax.random.normal(ks[6], (Hd, KERNEL), dtype=jnp.float32) * sc, 'Wa': jax.random.normal(ks[7], (Hd, H), dtype=jnp.float32) * sc, 'ba': jnp.zeros((H,), jnp.float32), 'Wb': jax.random.normal(ks[8], (Hd, H), dtype=jnp.float32) * sc, 'bb': jnp.zeros((H,), jnp.float32), 'Wg': jax.random.normal(ks[9], (Hd, Hd), dtype=jnp.float32) * sc, 'bg': jnp.zeros((Hd,), jnp.float32), 'gn_scale': jnp.ones((Hd,), jnp.float32), 'gn_bias': jnp.zeros((Hd,), jnp.float32), 'Wo': jax.random.normal(ks[10], (Hd, Hd), dtype=jnp.float32) * sc, 'bo': jnp.zeros((Hd,), jnp.float32)}
        return inp
    _L0_attn_in = _L0_attn_setup()

    def _L0_ffn_setup():
        import jax, jax.numpy as jnp
        import numpy as np
        DIM = 128
        HID = 352
        E = 8
        TOP_K = 2
        EPS = 1e-06

        def _rmsnorm(x, w):
            var = jnp.mean(jnp.square(x), axis=-1, keepdims=True)
            return x * jax.lax.rsqrt(var + EPS) * w
        key = jax.random.key(seed)
        ks = jax.random.split(key, 5)
        x = jax.random.normal(ks[0], (4, 256, DIM), dtype=jnp.float32)
        norm_weight = jnp.ones((DIM,), dtype=jnp.float32)
        router_weight = jax.random.normal(ks[1], (E, DIM), dtype=jnp.float32) * 0.02
        gate_up_weight = jax.random.normal(ks[2], (E, 2 * HID, DIM), dtype=jnp.float32) * (0.02 / np.sqrt(E))
        down_weight = jax.random.normal(ks[3], (E, DIM, HID), dtype=jnp.float32) * (0.02 / np.sqrt(E))
        residual_alpha = jnp.float32(1.0)
        return {'x': x, 'norm_weight': norm_weight, 'router_weight': router_weight, 'gate_up_weight': gate_up_weight, 'down_weight': down_weight, 'residual_alpha': residual_alpha}
    _L0_ffn_in = _L0_ffn_setup()
    _d = {'L0_attn_x': _L0_attn_in['x'], 'L0_attn_Wq': _L0_attn_in['Wq'], 'L0_attn_bq': _L0_attn_in['bq'], 'L0_attn_Wk': _L0_attn_in['Wk'], 'L0_attn_bk': _L0_attn_in['bk'], 'L0_attn_Wv': _L0_attn_in['Wv'], 'L0_attn_bv': _L0_attn_in['bv'], 'L0_attn_q_conv': _L0_attn_in['q_conv'], 'L0_attn_k_conv': _L0_attn_in['k_conv'], 'L0_attn_v_conv': _L0_attn_in['v_conv'], 'L0_attn_Wa': _L0_attn_in['Wa'], 'L0_attn_ba': _L0_attn_in['ba'], 'L0_attn_Wb': _L0_attn_in['Wb'], 'L0_attn_bb': _L0_attn_in['bb'], 'L0_attn_Wg': _L0_attn_in['Wg'], 'L0_attn_bg': _L0_attn_in['bg'], 'L0_attn_gn_scale': _L0_attn_in['gn_scale'], 'L0_attn_gn_bias': _L0_attn_in['gn_bias'], 'L0_attn_Wo': _L0_attn_in['Wo'], 'L0_attn_bo': _L0_attn_in['bo'], 'L0_ffn_norm_weight': _L0_ffn_in['norm_weight'], 'L0_ffn_router_weight': _L0_ffn_in['router_weight'], 'L0_ffn_gate_up_weight': _L0_ffn_in['gate_up_weight'], 'L0_ffn_down_weight': _L0_ffn_in['down_weight'], 'L0_ffn_residual_alpha': _L0_ffn_in['residual_alpha']}
    _x0 = _d['L0_attn_x']
    _d['L0_attn_x'] = jax.random.normal(jax.random.fold_in(jax.random.key(seed), 1), (8, 256, 128), dtype=_x0.dtype)
    del _x0
    return _d

def reference(L0_attn_x, L0_attn_Wq, L0_attn_bq, L0_attn_Wk, L0_attn_bk, L0_attn_Wv, L0_attn_bv, L0_attn_q_conv, L0_attn_k_conv, L0_attn_v_conv, L0_attn_Wa, L0_attn_ba, L0_attn_Wb, L0_attn_bb, L0_attn_Wg, L0_attn_bg, L0_attn_gn_scale, L0_attn_gn_bias, L0_attn_Wo, L0_attn_bo, L0_ffn_norm_weight, L0_ffn_router_weight, L0_ffn_gate_up_weight, L0_ffn_down_weight, L0_ffn_residual_alpha):

    def _L0_attn_ref(x, Wq, bq, Wk, bk, Wv, bv, q_conv, k_conv, v_conv, Wa, ba, Wb, bb, Wg, bg, gn_scale, gn_bias, Wo, bo):
        import jax, jax.numpy as jnp
        import numpy as np
        N_HIDDEN = 128
        N_HEADS = 16
        HEAD_DIM = N_HIDDEN // N_HEADS
        KERNEL = 4
        GN_EPS = 1e-05

        def _short_conv_1d(x, weight):
            F, K = weight.shape
            xp = jnp.pad(x, ((0, 0), (K - 1, 0), (0, 0)))
            shifts = jnp.stack([xp[:, i:i + x.shape[1], :] for i in range(K)], axis=-1)
            return jnp.sum(shifts * weight[None, None, :, :], axis=-1)
        B, S, _ = x.shape
        h, d = (N_HEADS, HEAD_DIM)
        q = jax.nn.silu(_short_conv_1d(x @ Wq + bq, q_conv)).reshape(B, S, h, d)
        q = q / (jnp.linalg.norm(q, axis=-1, keepdims=True) + 1e-06)
        k = jax.nn.silu(_short_conv_1d(x @ Wk + bk, k_conv)).reshape(B, S, h, d)
        k = k / (jnp.linalg.norm(k, axis=-1, keepdims=True) + 1e-06)
        v = jax.nn.silu(_short_conv_1d(x @ Wv + bv, v_conv)).reshape(B, S, h, d)
        alpha = jax.nn.sigmoid(x @ Wa + ba)
        beta = jax.nn.sigmoid(x @ Wb + bb)
        out_gate = jax.nn.silu(x @ Wg + bg)
        qT = jnp.transpose(q, (1, 0, 2, 3))
        kT = jnp.transpose(k, (1, 0, 2, 3))
        vT = jnp.transpose(v, (1, 0, 2, 3))
        aT = jnp.transpose(alpha, (1, 0, 2))
        bT = jnp.transpose(beta, (1, 0, 2))

        def _step(Sst, inputs):
            q_t, k_t, v_t, a_t, b_t = inputs
            a = a_t[:, :, None, None]
            b = b_t[:, :, None, None]
            Sk = jnp.einsum('bhde,bhe->bhd', Sst, k_t)
            delta_gated = v_t - a_t[:, :, None] * Sk
            update = b * jnp.einsum('bhd,bhe->bhde', delta_gated, k_t)
            Sst = a * Sst + update
            o_t = jnp.einsum('bhde,bhe->bhd', Sst, q_t)
            return (Sst, o_t)
        S0 = jnp.zeros((B, h, d, d), dtype=x.dtype)
        _, outs = jax.lax.scan(_step, S0, (qT, kT, vT, aT, bT))
        outs = jnp.transpose(outs, (1, 0, 2, 3)).reshape(B, S, N_HIDDEN)
        g = outs.reshape(B, S, h, d)
        mu = jnp.mean(g, axis=(1, 3), keepdims=True)
        var = jnp.mean(jnp.square(g), axis=(1, 3), keepdims=True) - jnp.square(mu)
        g = (g - mu) * jax.lax.rsqrt(var + GN_EPS)
        y = g.reshape(B, S, N_HIDDEN) * gn_scale + gn_bias
        return out_gate * y @ Wo + bo

    def _L0_ffn_ref(x, norm_weight, router_weight, gate_up_weight, down_weight, residual_alpha):
        import jax, jax.numpy as jnp
        import numpy as np
        DIM = 128
        HID = 352
        E = 8
        TOP_K = 2
        EPS = 1e-06

        def _rmsnorm(x, w):
            var = jnp.mean(jnp.square(x), axis=-1, keepdims=True)
            return x * jax.lax.rsqrt(var + EPS) * w
        normed = _rmsnorm(x, norm_weight)
        logits = jnp.einsum('bsd,ed->bse', normed, router_weight)
        probs = jax.nn.softmax(logits, axis=-1)
        topk_w, topk_idx = jax.lax.top_k(probs, TOP_K)
        topk_w = topk_w / jnp.sum(topk_w, axis=-1, keepdims=True)
        combine = jnp.sum(jax.nn.one_hot(topk_idx, E, dtype=normed.dtype) * topk_w[..., None], axis=-2)
        moe_out = jnp.zeros_like(x)
        for e in range(E):
            gu = jnp.einsum('bsd,hd->bsh', normed, gate_up_weight[e])
            gate, up = (gu[..., :HID], gu[..., HID:])
            hidden = jax.nn.silu(gate) * up
            out_e = jnp.einsum('bsh,dh->bsd', hidden, down_weight[e])
            moe_out = moe_out + combine[..., e, None] * out_e
        alpha = jnp.clip(residual_alpha, -0.5, 2.0)
        return x + alpha * moe_out
    x = L0_attn_x
    x = x + _layernorm(_L0_attn_ref(_layernorm(x, axis=-1), L0_attn_Wq, L0_attn_bq, L0_attn_Wk, L0_attn_bk, L0_attn_Wv, L0_attn_bv, L0_attn_q_conv, L0_attn_k_conv, L0_attn_v_conv, L0_attn_Wa, L0_attn_ba, L0_attn_Wb, L0_attn_bb, L0_attn_Wg, L0_attn_bg, L0_attn_gn_scale, L0_attn_gn_bias, L0_attn_Wo, L0_attn_bo), axis=-1)
    x = x + _layernorm(_L0_ffn_ref(_layernorm(x, axis=-1), L0_ffn_norm_weight, L0_ffn_router_weight, L0_ffn_gate_up_weight, L0_ffn_down_weight, L0_ffn_residual_alpha), axis=-1)
    return x

_drawn_inputs = setup_inputs


def setup_inputs(seed=0):
    import zlib

    import numpy as np

    out = dict(_drawn_inputs(seed))
    spreads = {'L0_attn_bq': (0.0, 0.331),
     'L0_attn_bk': (0.0, 0.1),
     'L0_attn_bv': (0.0, 0.308),
     'L0_attn_ba': (0.0, 0.8),
     'L0_attn_bb': (0.0, 0.8),
     'L0_attn_bg': (0.0, 0.334),
     'L0_attn_gn_scale': (1.0, 0.6),
     'L0_attn_gn_bias': (0.0, 0.47),
     'L0_attn_bo': (0.0, 0.1),
     'L0_ffn_norm_weight': (1.0, 0.6)}
    factors = {'L0_attn_Wa': 8.0,
     'L0_attn_Wb': 8.0,
     'L0_ffn_router_weight': 8.0,
     'L0_ffn_gate_up_weight': 8.0,
     'L0_ffn_down_weight': 8.0}
    for name, (base, spread) in spreads.items():
        noise = np.random.default_rng([zlib.crc32(name.encode()), seed]).standard_normal(out[name].shape)
        drawn = base * np.exp(spread * noise) if base else spread * noise
        out[name] = jnp.asarray(drawn.astype(out[name].dtype))
    for name, factor in factors.items():
        out[name] = (out[name] * factor).astype(out[name].dtype)
    return out
```

```python
import concourse.bass as bass
from concourse import mybir
from contextlib import ExitStack

F32 = mybir.dt.float32
ALU = mybir.AluOpType
ACT = mybir.ActivationFunctionType
AX = mybir.AxisListType

P = 128
B, S = 8, 256
H, D = 16, 8
NE, HID = 8, 352
C = 4
NH = 2
SH = S // NH
CH = SH // C
NC = S // C
T = B * S // P
G = 4
TG = T // G
N = TG * P
KW = 4
PAD = S + KW - 1
LN_EPS, GN_EPS, RMS_EPS, QK_EPS = 1e-5, 1e-5, 1e-6, 1e-6
HC = [(0, 128), (128, 128), (256, 96)]
LOW = {0: 0, 1: 3, 2: 5}
DIAG = {0: 0, 1: 4, 2: 7, 3: 9}
NLOW, NDIAG = 6, 10
DB = 64
NB = S // DB
CB = DB // C
N_SLOT = D * C + NDIAG
SLOTS = D + C


class Steps:

    def __init__(self, eng, sem):
        self.eng, self.sem, self.n = eng, sem, 0

    def step(self, ins):
        ins.then_inc(self.sem, 1)
        self.n = self.n + 1

    def link(self, ins):
        self.step(ins)
        self.eng.wait_ge(self.sem, self.n)

    def wait(self):
        self.eng.wait_ge(self.sem, self.n)


def build(nc, x, Wq, bq, Wk, bk, Wv, bv, q_conv, k_conv, v_conv, Wa, ba, Wb, bb, Wg, bg,
          gn_scale, gn_bias, Wo, bo, norm_w, router_t, gu_t, down_t, res_alpha, out):
    ctx = ExitStack()
    with ctx:
        def sb(name, shape):
            return ctx.enter_context(nc.sbuf_tensor(name, shape, F32))

        def sem(name):
            return ctx.enter_context(nc.semaphore(name))

        qkv_d = nc.dram_tensor("qkv_scratch", [NH, 3, B, P, SH], F32, kind="Internal").ap()
        ab_d = nc.dram_tensor("ab_scratch", [NH, 2, B, H, SH], F32, kind="Internal").ap()
        o_d = nc.dram_tensor("o_scratch", [B, P, S], F32, kind="Internal").ap()

        w_proj = sb("w_proj", [P, 4, P])
        w_ab = sb("w_ab", [P, 2 * H])
        w_o = sb("w_o", [P, P])
        w_router = sb("w_router", [P, NE])
        conv_w = sb("conv_w", [P, 3, KW])
        bias_qkvg = sb("bias_qkvg", [P, 4])
        bias_ab = sb("bias_ab", [2 * H, 1])
        gn_sb = sb("gn_sb", [P, 2])
        normw_sb = sb("normw_sb", [P, 1])
        alpha_sb = sb("alpha_sb", [P, 1])
        bo_row = sb("bo_row", [P, P])
        ident = sb("ident", [P, P])
        halves = sb("halves", [P, 2 * SH])
        mhalf = sb("mhalf", [P, TG])
        ranks = sb("ranks", [P, NE])

        x_all = sb("x_all", [P, T, P])
        xn = sb("xn", [P, 2, TG, P])
        gateT = sb("gateT", [P, T * P])
        conv_in = sb("conv_in", [P, 3 * B * PAD])
        conv_v = conv_in[:, :].rearrange("p (w b t) -> p w b t", w=3, b=B)
        qs = sb("qs", [P, 2, 3, TG, P])
        ab_sb = sb("ab_sb", [2 * H, T * P])
        raw = sb("raw", [P, 3, D, SH])
        ab_bh = sb("ab_bh", [P, NH, 2, SH])
        work = sb("work", [P, NDIAG * CH * D])
        kn = sb("kn", [P, S, D])
        qn = sb("qn", [P, S, D])
        kd = sb("kd", [P, S, D])
        wx = sb("wx", [P, S, D])
        us = sb("us", [P, S, D])
        ws_buf = sb("ws_buf", [P, CH * C * D * (D + 1)])
        ws = ws_buf[:, :].rearrange("p (c r d e) -> p c r d e", c=CH, r=C, d=D)
        states = sb("states", [P, NC + 1, D * D])
        outer = sb("outer", [P, 2, D * D, C + 1])
        ss = sb("ss", [P, 2, SH])
        rn = sb("rn", [P, 2, SH])
        gram = sb("gram", [P, NLOW, NC])
        aq = sb("aq", [P, NDIAG, NC])
        dec = sb("dec", [P, NLOW, NC])
        gc = sb("gc", [P, C, NC])
        bg_neg = sb("bg_neg", [P, C, CH])
        sub_u = sb("sub_u", [P, (C - 1) * CH * D])
        stats = sb("stats", [P, TG, 6])
        mv = sb("mv", [P, 2, TG, 2])
        rstd = sb("rstd", [P, 2, TG])
        gn_part = sb("gn_part", [P, 2, NB])
        gn_s = sb("gn_s", [P, 8])
        moe_in = sb("moe_in", [P, T, NE])
        r_a = sb("r_a", [P, T, NE])
        r_b = sb("r_b", [P, T, NE])
        r_one = sb("r_one", [P, T, NE])
        r_two = sb("r_two", [P, T, NE])
        comb = sb("comb", [P, T, NE])
        r_s = sb("r_s", [P, 6, T])

        slots = conv_in[:, 0:SLOTS * DB * D].rearrange("p (s t d) -> p s t d", s=SLOTS, t=DB)
        gu_w = ws_buf[:, 0:NE * 2 * HID].rearrange("p (e n) -> p e n", e=NE)
        down_w = states[:, :, :].rearrange("p c n -> p (c n)")[:, 0:NE * 3 * P].rearrange(
            "p (e j n) -> p e j n", e=NE, j=3)
        gated = work[:, 0:2 * N].rearrange("p (k n) -> p k n", k=2)
        hidden = qs[:, :, :, :, :].rearrange("p k w j t -> p k w (j t)")
        xgT = work[:, 0:2 * N].rearrange("p (k n) -> p k n", k=2)
        xnT = us[:, :, :].rearrange("p t d -> p (t d)")
        og = kn[:, :, :].rearrange("p t d -> p (t d)").rearrange("p (d t) -> p d t", d=D)
        gT = qn[:, :, :].rearrange("p t d -> p (t d)").rearrange("p (b t) -> p b t", b=B)
        yT = wx[:, :, :].rearrange("p t d -> p (t d)")
        h_all = kd[:, :, :].rearrange("p t d -> p (t d)").rearrange("p (i f) -> p i f", i=T)

        banks = ctx.enter_context(nc.psum_tensor("banks", [P, 8, N], F32))

        x_in = [sem(f"x_in{g}") for g in range(G)]
        w_in = sem("w_in")
        gu_in, down_in = sem("gu_in"), sem("down_in")
        qs_out = [sem(f"qs_out{g}") for g in range(G)]
        ab_out = sem("ab_out")
        raw_in = [sem(f"raw_in{h}") for h in range(NH)]
        ab_in = sem("ab_in")
        og_out, gT_in = sem("og_out"), sem("gT_in")
        out_done = sem("out_done")
        vec, pool_s, act_s = sem("vec_steps"), sem("pool_steps"), sem("act_steps")
        const_ready = sem("const_ready")
        var_ready, rstd_ready = sem("var_ready"), sem("rstd_ready")
        xn_ready, xT_psum, xnT_ready = sem("xn_ready"), sem("xT_psum"), sem("xnT_ready")
        proj_psum, proj_out = sem("proj_psum"), sem("proj_out")
        ab_sig = sem("ab_sig")
        conv_ready, silu_ready = sem("conv_ready"), sem("silu_ready")
        sq_ready, ss_ready, root_ready = sem("sq_ready"), sem("ss_ready"), sem("root_ready")
        norm_ready, raw_free = sem("norm_ready"), sem("raw_free")
        decay_ready, mk_ready, u_ready, kd_ready = (sem("decay_ready"), sem("mk_ready"), sem("u_ready"), sem("kd_ready"))
        aq_ready, qg_ready = sem("aq_ready"), sem("qg_ready")
        state_ready, carry_ready = sem("state_ready"), sem("carry_ready")
        slots_ready, slots_used = sem("slots_ready"), sem("slots_used")
        o_sum, o_sq = sem("o_sum"), sem("o_sq")
        gn_var, gn_rstd, og_ready = sem("gn_var"), sem("gn_rstd"), sem("og_ready")
        y_aff, y_ready = sem("y_aff"), sem("y_ready")
        wo_psum = sem("wo_psum")
        logit_psum, exp_in, exp_done, comb_ready = sem("logit_psum"), sem("exp_in"), sem("exp_done"), sem("comb_ready")
        gu_psum, gate_done, hid_ready = sem("gu_psum"), sem("gate_done"), sem("hid_ready")
        down_psum, acc_done = sem("down_psum"), sem("acc_done")
        result_ready = sem("result_ready")

        block = ctx.enter_context(nc.Block())

        N_W = 22
        x_v = x.rearrange("(b h p) f -> h p b f", h=NH, p=P)

        def tiles(g):
            return g * TG, (g + 1) * TG

        @block.sync
        def _(sp):
            for g in range(G):
                h, b0 = g // 2, TG * (g % 2)
                sp.dma_start(x_all[:, g * TG:(g + 1) * TG, :], x_v[h, :, b0:b0 + TG, :]).then_inc(x_in[g], 16)
                if g == 0:
                    for i, w in enumerate((Wq, Wk, Wv, Wg)):
                        sp.dma_start(w_proj[:, i, :], w).then_inc(w_in, 16)
                    sp.dma_start(w_ab[:, 0:H], Wa).then_inc(w_in, 16)
                    sp.dma_start(w_ab[:, H:2 * H], Wb).then_inc(w_in, 16)
            for g in range(G):
                h, b0 = g // 2, TG * (g % 2)
                sp.wait_ge(silu_ready, g + 1)
                for w in range(3):
                    sp.dma_start(qkv_d[h, w, b0:b0 + TG].rearrange("b p t -> p b t"),
                                 qs[:, g % 2, w, :, :]).then_inc(qs_out[g], 16)
                if g % 2:
                    for k in (g - 1, g):
                        sp.wait_ge(qs_out[k], 3 * 16)
                    if h:
                        sp.wait_ge(raw_free, 2 * h)
                        sp.wait_ge(u_ready, h)
                    for w in (1, 0, 2):
                        sp.dma_start(raw[:, w, :, :], qkv_d[h, w].rearrange("b (h d) t -> (b h) d t", h=H)
                                     ).then_inc(raw_in[h], 16)
            sp.wait_ge(state_ready, NC + 1)
            sp.dma_start(gu_w, gu_t).then_inc(gu_in, 16)
            sp.wait_ge(slots_ready, NB * N_SLOT)
            for q, (h0, m) in enumerate(HC):
                sp.dma_start(down_w[0:m, :, q, :], down_t[:, h0:h0 + m, :].rearrange("e p n -> p e n")).then_inc(down_in, 16)
            sp.wait_ge(og_ready, 1)
            sp.dma_start(o_d.rearrange("b (h d) t -> (b h) d t", h=H), og).then_inc(og_out, 16)
            sp.wait_ge(og_out, 16)
            sp.dma_start(gT, o_d.rearrange("b p t -> p b t")).then_inc(gT_in, 16)
            for g in range(G):
                h, b0 = g // 2, TG * (g % 2)
                sp.wait_ge(result_ready, g + 1)
                sp.dma_start(out.rearrange("(b h p) f -> h p b f", h=NH, p=P)[h, :, b0:b0 + TG, :],
                             x_all[:, g * TG:(g + 1) * TG, :]).then_inc(out_done, 16)
            sp.wait_ge(out_done, G * 16)

        @block.scalar
        def _(act):
            col = lambda v: v.rearrange("(p a) -> p a", a=1)
            for i, v in enumerate((bq, bk, bv, bg)):
                act.dma_start(bias_qkvg[:, i:i + 1], col(v)).then_inc(w_in, 16)
            act.dma_start(bias_ab[0:H, :], col(ba)).then_inc(w_in, 16)
            act.dma_start(bias_ab[H:2 * H, :], col(bb)).then_inc(w_in, 16)
            for i, v in enumerate((q_conv, k_conv, v_conv)):
                act.dma_start(conv_w[:, i, :], v).then_inc(w_in, 16)
            act.dma_start(gn_sb[:, 0:1], col(gn_scale)).then_inc(w_in, 16)
            act.dma_start(gn_sb[:, 1:2], col(gn_bias)).then_inc(w_in, 16)
            act.dma_start(w_o[:, :], Wo).then_inc(w_in, 16)
            act.dma_start(normw_sb[:, :], col(norm_w)).then_inc(w_in, 16)
            act.dma_start(w_router[:, :], router_t).then_inc(w_in, 16)
            act.dma_start(bo_row[:, :], bo.partition_broadcast(P)).then_inc(w_in, 16)
            act.dma_start(alpha_sb[:, :], res_alpha.partition_broadcast(P)).then_inc(w_in, 16)
            act.wait_ge(w_in, N_W * 16)
            for g in range(G):
                h, b0 = g // 2, TG * (g % 2)
                act.wait_ge(xT_psum, g + 1)
                nc.scalar.copy(xgT[:, g % 2, :], banks[:, 0, :]).then_inc(xnT_ready, 1)
                act.wait_ge(proj_psum, g + 1)
                for w in range(3):
                    nc.scalar.activation(conv_v[:, w, b0:b0 + TG, KW - 1 + h * SH:KW - 1 + (h + 1) * SH],
                                         banks[:, 1 + w, :].rearrange("p (b t) -> p b t", b=TG), ACT.Identity,
                                         bias=bias_qkvg[:, w:w + 1]).then_inc(proj_out, 1)
                nc.scalar.activation(ab_sb[:, g * N:(g + 1) * N], banks[0:2 * H, 5, :], ACT.Sigmoid,
                                     bias=bias_ab[:, 0:1]).then_inc(ab_sig, 1)
                nc.scalar.activation(gateT[:, g * N:(g + 1) * N], banks[:, 4, :], ACT.Silu,
                                     bias=bias_qkvg[:, 3:4]).then_inc(proj_out, 1)
                act.wait_ge(conv_ready, g + 1)
                nc.scalar.activation(qs[:, g % 2], qs[:, g % 2], ACT.Silu).then_inc(silu_ready, 1)
                if g % 2:
                    act.wait_ge(ab_sig, g + 1)
                    for k in range(2):
                        act.dma_start(ab_d[h, k].rearrange("b h t -> h b t"),
                                      ab_sb[k * H:(k + 1) * H, h * B * SH:(h + 1) * B * SH]
                                      .rearrange("h (b t) -> h b t", b=B)).then_inc(ab_out, 16)
                    act.wait_ge(ab_out, (h + 1) * 32)
                    act.dma_start(ab_bh[:, h, :, :], ab_d[h].rearrange("k b h t -> (b h) k t")).then_inc(ab_in, 16)
            for h in range(NH):
                act.wait_ge(raw_in[h], 3 * 16)
                nc.scalar.activation(work[:, 0:2 * D * SH], raw[:, 0:2].rearrange("p w d t -> p (w d t)"),
                                     ACT.Square).then_inc(sq_ready, 1)
                act.wait_ge(decay_ready, h + 1)
                with act.Fori(0, CH // 2) as i:
                    for k in range(2):
                        c = i * 2 + (h * CH + k)
                        act.wait_ge(state_ready, c + 1)
                        nc.scalar.activation(outer[:, k, :, C], states[:, bass.ds(c, 1), :].rearrange("p a n -> p (a n)"),
                                             ACT.Copy, scale=gc[:, C - 1, bass.ds(c, 1)]).then_inc(carry_ready, 1)
            for n in range(NB):
                act.wait_ge(slots_used, (n + 1) * SLOTS)
                nc.scalar.activation(og[:, :, n * DB:(n + 1) * DB], banks[:, n, :].rearrange("p (t d) -> p d t", d=D),
                                     ACT.Copy, accum_out=gn_part[:, 0, n:n + 1]).then_inc(o_sum, 1)
                if n >= 2:
                    act.wait_ge(o_sq, n - 1)
                nc.scalar.activation(gated[:, n % 2, :], banks[:, n, :], ACT.Square,
                                     accum_out=gn_part[:, 1, n:n + 1]).then_inc(o_sq, 1)
            act.wait_ge(gT_in, 16)
            nc.scalar.activation(yT.rearrange("p (h b t) -> p b h t", h=NH, b=B),
                                 gT.rearrange("p b (h t) -> p b h t", h=NH),
                                 ACT.Identity, scale=gn_sb[:, 0:1], bias=gn_sb[:, 1:2]).then_inc(y_aff, 1)
            for g in range(G):
                act.wait_ge(xT_psum, G + g + 1)
                nc.scalar.activation(xnT[:, g * N:(g + 1) * N], banks[:, g, :], ACT.Copy,
                                     scale=normw_sb[:, 0:1]).then_inc(xnT_ready, 1)
            act.wait_ge(exp_in, 1)
            nc.scalar.activation(r_b[:, :, :], r_a[:, :, :], ACT.Exp).then_inc(exp_done, 1)
            with act.Fori(0, G) as blk:
                for e in range(NE):
                    for j, (_, m) in enumerate(HC):
                        k = 3 * e + j
                        act.wait_ge(gu_psum, blk * 3 * NE + (k + 1))
                        act.wait_ge(hid_ready, blk * 3 * NE + max(k, 1))
                        nc.scalar.activation(gated[0:m, k % 2, :], banks[0:m, 2 * (k % 2), :],
                                             ACT.Silu).then_inc(gate_done, 1)

        @block.gpsimd
        def _(pool):
            own = Steps(pool, pool_s)
            own.step(nc.gpsimd.memset(halves[:, :], 0.5))
            own.step(nc.gpsimd.memset(mhalf[:, :], -0.5))
            own.link(nc.gpsimd.memset(ident[:, :], 0.0))
            nc.gpsimd.affine_select(out=ident[:, :], in_=ident[:, :], compare_op=ALU.not_equal, fill=1.0, base=0,
                                    pattern=[[-1, P]], channel_multiplier=1).then_inc(const_ready, 1)
            nc.gpsimd.memset(states[:, 0, :], 0.0).then_inc(state_ready, 1)
            nc.gpsimd.iota(ranks[:, :], pattern=[[-1, NE]], base=NE, channel_multiplier=0,
                           allow_small_or_imprecise_dtypes=True).then_inc(const_ready, 1)
            nc.gpsimd.memset(conv_v[:, :, :, 0:KW - 1], 0.0).then_inc(const_ready, 1)

            def root(n):
                pool.wait_ge(var_ready, n + 1)
                nc.gpsimd.tensor_tensor(rstd[:, n % 2, :], mv[:, n % 2, :, 1], mhalf[:, :], ALU.pow).then_inc(rstd_ready, 1)

            for g in range(G):
                root(g)
            q4 = qn[:, :, :].rearrange("p (c r) e -> p r c e", r=C)

            def prepare(h):
                c0, c1 = h * CH, (h + 1) * CH
                al = ab_bh[:, h, 0, :].rearrange("p (c r) -> p r c", r=C)
                be = ab_bh[:, h, 1, :].rearrange("p (c r) -> p r c", r=C)
                pool.wait_ge(ab_in, (h + 1) * 16)
                d = lambda k: dec[:, k, c0:c1]
                own.step(nc.gpsimd.tensor_copy(d(0), al[:, 1, :]))
                own.step(nc.gpsimd.tensor_copy(d(3), al[:, 2, :]))
                own.step(nc.gpsimd.tensor_copy(d(5), al[:, 3, :]))
                own.step(nc.gpsimd.tensor_copy(gc[:, 0, c0:c1], al[:, 0, :]))
                own.step(nc.gpsimd.tensor_tensor(d(1), al[:, 1, :], al[:, 2, :], ALU.mult))
                own.link(nc.gpsimd.tensor_tensor(d(4), al[:, 2, :], al[:, 3, :], ALU.mult))
                own.link(nc.gpsimd.tensor_tensor(d(2), d(1), al[:, 3, :], ALU.mult))
                nc.gpsimd.tensor_tensor(gc[:, 1:C, c0:c1], dec[:, 0:C - 1, c0:c1],
                                        al[:, 0:1, :].broadcast_to([P, C - 1, CH]), ALU.mult).then_inc(decay_ready, 1)
                pool.wait_ge(ss_ready, h + 1)
                nc.gpsimd.tensor_tensor(rn[:, :, :], ss[:, :, :],
                                        halves[:, :].rearrange("p (w t) -> p w t", w=2), ALU.pow).then_inc(root_ready, 1)
                if h:
                    pool.wait_ge(state_ready, h * CH + 1)
                for r in range(C):
                    own.step(nc.gpsimd.tensor_tensor(
                        ws[:, :, r, :, D], raw[:, 2].rearrange("p d (c r) -> p r c d", r=C)[:, r],
                        be[:, r, :].unsqueeze(2).broadcast_to([P, CH, D]), ALU.mult))
                pool.wait_ge(mk_ready, h + 1)
                own.wait()
                for i in range(C - 1):
                    n = C - 1 - i
                    tmp = sub_u[:, 0:n * CH * D].rearrange("p (r c d) -> p r c d", r=n, c=CH)
                    for q in range(n):
                        own.step(nc.gpsimd.tensor_tensor(
                            tmp[:, q], ws[:, :, i, :, D],
                            gram[:, LOW[i] + q, c0:c1].unsqueeze(2).broadcast_to([P, CH, D]), ALU.mult))
                    own.wait()
                    for q in range(n):
                        dst = ws[:, :, i + 1 + q, :, D]
                        ins = nc.gpsimd.tensor_tensor(dst, dst, tmp[:, q], ALU.subtract)
                        if i < C - 2:
                            own.step(ins)
                        else:
                            ins.then_inc(u_ready, 1)
                    own.wait()
                pool.wait_ge(aq_ready, (h + 1) * (C - 1))
                pool.wait_ge(decay_ready, h + 1)
                for r in range(C):
                    nc.gpsimd.tensor_tensor(q4[:, r, c0:c1], q4[:, r, c0:c1],
                                            gc[:, r, c0:c1].unsqueeze(2).broadcast_to([P, CH, D]),
                                            ALU.mult).then_inc(qg_ready, 1)

            def outputs(h):
                pool.wait_ge(state_ready, (h + 1) * CH + 1)
                pool.wait_ge(qg_ready, (h + 1) * C)
                own.wait()
                for n in range(h * NB // NH, (h + 1) * NB // NH):
                    t0, cc = n * DB, n * CB
                    for s in range(SLOTS):
                        if n:
                            pool.wait_ge(slots_used, (n - 1) * SLOTS + s + 1)
                        if s < D:
                            for r in range(C):
                                ins = nc.gpsimd.tensor_tensor(
                                    slots[:, s].rearrange("p (c r) d -> p c r d", r=C)[:, :, r],
                                    states[:, cc:cc + CB, :].rearrange("p c (d e) -> p c d e", d=D)[:, :, :, s],
                                    q4[:, r, cc:cc + CB, s:s + 1].broadcast_to([P, CB, D]), ALU.mult)
                                ins.then_inc(slots_ready, 1)
                        else:
                            i = s - D
                            for r in range(i, C):
                                nc.gpsimd.tensor_tensor(
                                    slots[:, s].rearrange("p (c r) d -> p c r d", r=C)[:, :, r],
                                    us[:, :, :].rearrange("p (c r) d -> p c r d", r=C)[:, cc:cc + CB, i],
                                    aq[:, DIAG[i] + r - i, cc:cc + CB].unsqueeze(2).broadcast_to([P, CB, D]),
                                    ALU.mult).then_inc(slots_ready, 1)

            prepare(0)
            pool.wait_ge(conv_ready, G)
            for i in range(1, C):
                own.step(nc.gpsimd.memset(slots[:, D + i].rearrange("p (c r) d -> p c r d", r=C)[:, :, 0:i], 0.0))
            prepare(1)
            outputs(0)
            outputs(1)
            pool.wait_ge(gn_var, 1)
            nc.gpsimd.tensor_tensor(gn_s[:, 4:5], gn_s[:, 3:4], mhalf[:, 0:1], ALU.pow).then_inc(gn_rstd, 1)
            for n in range(G, 5 * G):
                root(n)

        @block.vector
        def _(dve):
            own = Steps(dve, vec)
            v = nc.vector
            lns = [0]

            def statistics(src, square=False):
                n = lns[0] % 2
                for j in range(TG):
                    own.step(v.bn_stats(stats[:, j, :], src(j)))
                own.wait()
                for j in range(TG):
                    own.step(v.bn_aggr(mv[:, n, j, :], stats[:, j, :]))
                own.wait()
                return n

            def normalise(src, dst, eps, signal=None):
                n = statistics(src)
                v.tensor_scalar(mv[:, n, :, 1], mv[:, n, :, 1], eps, None, ALU.add).then_inc(var_ready, 1)
                lns[0] += 1
                dve.wait_ge(rstd_ready, lns[0])
                for j in range(TG):
                    ins = v.tensor_scalar(dst(j), src(j), mv[:, n, j, 0:1], rstd[:, n, j:j + 1],
                                          ALU.subtract, ALU.mult)
                    if signal is None or j < TG - 1:
                        own.step(ins)
                    else:
                        ins.then_inc(signal, 1)
                if signal is None:
                    own.wait()

            def rms_scale(src, dst, eps, signal):
                n = statistics(src)
                own.link(v.tensor_tensor(mv[:, n, :, 0], mv[:, n, :, 0], mv[:, n, :, 0], ALU.mult))
                v.scalar_tensor_tensor(mv[:, n, :, 1], mv[:, n, :, 1], eps, mv[:, n, :, 0], ALU.add,
                                       ALU.add).then_inc(var_ready, 1)
                lns[0] += 1
                dve.wait_ge(rstd_ready, lns[0])
                for j in range(TG):
                    ins = v.tensor_scalar(dst(j), src(j), rstd[:, n, j:j + 1], None, ALU.mult)
                    if j < TG - 1:
                        own.step(ins)
                    else:
                        ins.then_inc(signal, 1)

            def ln_in(g):
                dve.wait_ge(x_in[g], 16)
                if g >= 2:
                    dve.wait_ge(xT_psum, g - 1)
                normalise(lambda j: x_all[:, g * TG + j, :], lambda j: xn[:, g % 2, j, :], LN_EPS, xn_ready)

            def conv(g):
                h, b0 = g // 2, TG * (g % 2)
                dve.wait_ge(proj_out, 4 * g + 4)
                if g >= 2:
                    dve.wait_ge(qs_out[g - 2], 3 * 16)
                for tap in range(KW):
                    for w in range(3):
                        src = conv_v[:, w, b0:b0 + TG, tap + h * SH:tap + (h + 1) * SH]
                        dst = qs[:, g % 2, w]
                        if tap == 0:
                            own.step(v.tensor_scalar(dst, src, conv_w[:, w, 0:1], None, ALU.mult))
                            continue
                        ins = v.scalar_tensor_tensor(dst, src, conv_w[:, w, tap:tap + 1], dst, ALU.mult, ALU.add)
                        if tap < KW - 1 or w < 2:
                            own.step(ins)
                        else:
                            ins.then_inc(conv_ready, 1)
                    if tap < KW - 1:
                        own.wait()
                    else:
                        own.wait()

            dve.wait_ge(const_ready, 3)
            dve.wait_ge(w_in, N_W * 16)
            ln_in(0)
            for g in range(G):
                if g + 1 < G:
                    ln_in(g + 1)
                conv(g)

            for h in range(NH):
                c0, c1 = h * CH, (h + 1) * CH
                t0, t1 = h * SH, (h + 1) * SH
                dve.wait_ge(sq_ready, h + 1)
                v.tensor_reduce(ss[:, :, :], work[:, 0:2 * D * SH].rearrange("p (w d t) -> p w t d", w=2, d=D),
                                AX.X, ALU.add).then_inc(ss_ready, 1)
                dve.wait_ge(root_ready, h + 1)
                own.link(v.tensor_scalar(rn[:, :, :], rn[:, :, :], QK_EPS, None, ALU.add))
                own.link(v.reciprocal(rn[:, :, :], rn[:, :, :]))
                for w, dst in ((1, kn), (0, qn)):
                    v.tensor_tensor(dst[:, t0:t1, :].rearrange("p t d -> p d t"), raw[:, w],
                                    rn[:, w:w + 1, :].broadcast_to([P, D, SH]), ALU.mult).then_inc(raw_free, 1)
                dve.wait_ge(raw_free, 2 * (h + 1))
                k4 = kn[:, :, :].rearrange("p (c r) e -> p r c e", r=C)
                q4 = qn[:, :, :].rearrange("p (c r) e -> p r c e", r=C)
                w4 = wx[:, :, :].rearrange("p (c r) e -> p r c e", r=C)
                d4 = kd[:, :, :].rearrange("p (c r) e -> p r c e", r=C)
                prod = work[:, 0:NLOW * CH * D].rearrange("p (m c e) -> p m c e", m=NLOW, c=CH)
                for i in range(C - 1):
                    n = C - 1 - i
                    own.step(v.tensor_tensor(prod[:, LOW[i]:LOW[i] + n], k4[:, i + 1:C, c0:c1],
                                             k4[:, i:i + 1, c0:c1].broadcast_to([P, n, CH, D]), ALU.mult))
                own.wait()
                own.link(v.tensor_reduce(gram[:, :, c0:c1], prod, AX.X, ALU.add))
                dve.wait_ge(decay_ready, h + 1)
                own.link(v.tensor_tensor(gram[:, :, c0:c1], gram[:, :, c0:c1], dec[:, :, c0:c1], ALU.mult))
                be = ab_bh[:, h, 1, :].rearrange("p (c r) -> p r c", r=C)
                for i in range(C - 1):
                    n = C - 1 - i
                    g_ = gram[:, LOW[i]:LOW[i] + n, c0:c1]
                    ins = v.tensor_tensor(g_, g_, be[:, i + 1:C], ALU.mult)
                    if i < C - 2:
                        own.step(ins)
                    else:
                        ins.then_inc(mk_ready, 1)
                own.link(v.scalar_tensor_tensor(bg_neg[:, :, :], be, -1.0, gc[:, :, c0:c1], ALU.mult, ALU.mult))
                own.step(v.tensor_tensor(w4[:, :, c0:c1], k4[:, :, c0:c1],
                                         bg_neg[:, :, :].unsqueeze(3).broadcast_to([P, C, CH, D]), ALU.mult))
                own.step(v.tensor_copy(d4[:, C - 1, c0:c1], k4[:, C - 1, c0:c1]))
                for i, m in ((0, 2), (1, 4), (2, 5)):
                    own.step(v.tensor_tensor(d4[:, i, c0:c1], k4[:, i, c0:c1],
                                             dec[:, m, c0:c1].unsqueeze(2).broadcast_to([P, CH, D]), ALU.mult))
                dve.wait_ge(mk_ready, h + 1)
                own.wait()
                for i in range(C - 1):
                    n = C - 1 - i
                    tmp = work[:, 0:n * CH * D].rearrange("p (r c e) -> p r c e", r=n, c=CH)
                    own.link(v.tensor_tensor(tmp, gram[:, LOW[i]:LOW[i] + n, c0:c1].unsqueeze(3).broadcast_to([P, n, CH, D]),
                                             w4[:, i:i + 1, c0:c1].broadcast_to([P, n, CH, D]), ALU.mult))
                    own.link(v.tensor_tensor(w4[:, i + 1:C, c0:c1], w4[:, i + 1:C, c0:c1], tmp, ALU.subtract))
                prod = work[:, 0:NDIAG * CH * D].rearrange("p (m c e) -> p m c e", m=NDIAG, c=CH)
                for i in range(C):
                    n = C - i
                    own.step(v.tensor_tensor(prod[:, DIAG[i]:DIAG[i] + n], q4[:, i:C, c0:c1],
                                             k4[:, i:i + 1, c0:c1].broadcast_to([P, n, CH, D]), ALU.mult))
                own.wait()
                own.link(v.tensor_reduce(aq[:, :, c0:c1], prod, AX.X, ALU.add))
                for i in range(C - 1):
                    n = C - 1 - i
                    a_ = aq[:, DIAG[i] + 1:DIAG[i] + 1 + n, c0:c1]
                    v.tensor_tensor(a_, a_, dec[:, LOW[i]:LOW[i] + n, c0:c1], ALU.mult).then_inc(aq_ready, 1)
                dve.wait_ge(u_ready, h + 1)
                dve.wait_ge(state_ready, h * CH + 1)
                n0 = own.n
                with dve.Fori(0, CH // 2) as it:
                    for k in range(2):
                        c = it * 2 + (h * CH + k)
                        cl = it * 2 + k
                        st = states[:, bass.ds(c, 1), :].rearrange("p a (d e) -> p a d e", d=D)
                        own.n = it * 6 + (n0 + 3 * k)
                        own.link(v.tensor_tensor(
                            ws[:, bass.ds(cl, 1), :, :, 0:D].rearrange("p a r d e -> p (a r) d e"),
                            wx[:, bass.ds(c * C, C), :].unsqueeze(2).broadcast_to([P, C, D, D]),
                            st.broadcast_to([P, C, D, D]), ALU.mult))
                        u = us[:, bass.ds(c * C, C), :]
                        own.link(v.tensor_reduce(
                            u, ws[:, bass.ds(cl, 1)].rearrange("p a r d e -> p (a r) d e"), AX.X, ALU.add))
                        own.link(v.tensor_tensor(
                            outer[:, k, :, 0:C].rearrange("p (d e) i -> p d e i", d=D),
                            kd[:, bass.ds(c * C, C), :].rearrange("p i e -> p e i").unsqueeze(1).broadcast_to([P, D, D, C]),
                            u.rearrange("p i d -> p d i").unsqueeze(2).broadcast_to([P, D, D, C]), ALU.mult))
                        dve.wait_ge(carry_ready, c + 1)
                        v.tensor_reduce(states[:, bass.ds(c + 1, 1), :].rearrange("p a n -> p (a n)"), outer[:, k, :, :],
                                        AX.X, ALU.add).then_inc(state_ready, 1)
                        dve.wait_ge(state_ready, c + 2)
                own.n = n0 + 3 * CH

            dve.wait_ge(o_sum, NB)
            dve.wait_ge(o_sq, NB)
            own.link(v.tensor_reduce(gn_s[:, 0:2], gn_part[:, :, :], AX.X, ALU.add))
            own.link(v.tensor_scalar(gn_s[:, 0:2], gn_s[:, 0:2], 1.0 / (S * D), None, ALU.mult))
            own.link(v.tensor_tensor(gn_s[:, 2:3], gn_s[:, 0:1], gn_s[:, 0:1], ALU.mult))
            v.scalar_tensor_tensor(gn_s[:, 3:4], gn_s[:, 1:2], GN_EPS, gn_s[:, 2:3], ALU.add,
                                   ALU.subtract).then_inc(gn_var, 1)
            dve.wait_ge(gn_rstd, 1)
            v.tensor_scalar(og, og, gn_s[:, 0:1], gn_s[:, 4:5], ALU.subtract, ALU.mult).then_inc(og_ready, 1)
            dve.wait_ge(y_aff, 1)
            v.tensor_tensor(yT, yT, gateT[:, :], ALU.mult).then_inc(y_ready, 1)

            for g in range(G):
                tl = slice(g * TG, (g + 1) * TG)
                dve.wait_ge(wo_psum, g + 1)
                own.link(v.tensor_tensor(xn[:, 0], banks[:, 4 + g, :].rearrange("p (j f) -> p j f", j=TG),
                                         bo_row[:, :].unsqueeze(1).broadcast_to([P, TG, P]), ALU.add))
                normalise(lambda j: xn[:, 0, j, :], lambda j: xn[:, 0, j, :], LN_EPS)
                own.link(v.tensor_tensor(x_all[:, tl, :], x_all[:, tl, :], xn[:, 0], ALU.add))
                normalise(lambda j: x_all[:, g * TG + j, :], lambda j: h_all[:, g * TG + j, :], LN_EPS)
                if g:
                    dve.wait_ge(xT_psum, G + g)
                rms_scale(lambda j: h_all[:, g * TG + j, :], lambda j: xn[:, 1, j, :], RMS_EPS, xn_ready)

            dve.wait_ge(logit_psum, 1)
            lg = banks[:, 4, 0:T * NE].rearrange("p (i e) -> p i e", e=NE)
            bc = lambda k: r_s[:, k, :].unsqueeze(2).broadcast_to([P, T, NE])
            own.link(v.tensor_reduce(r_s[:, 0, :], lg, AX.X, ALU.max))
            v.tensor_tensor(r_a[:, :, :], lg, bc(0), ALU.subtract).then_inc(exp_in, 1)
            dve.wait_ge(exp_done, 1)
            own.link(v.tensor_reduce(r_s[:, 1, :], r_b[:, :, :], AX.X, ALU.add))
            own.link(v.reciprocal(r_s[:, 1, :], r_s[:, 1, :]))
            own.link(v.tensor_tensor(r_b[:, :, :], r_b[:, :, :], bc(1), ALU.mult))
            for one, k in ((r_one, 2), (r_two, 3)):
                own.link(v.tensor_reduce(r_s[:, k, :], r_b[:, :, :], AX.X, ALU.max))
                own.link(v.tensor_tensor(r_a[:, :, :], r_b[:, :, :], bc(k), ALU.is_equal))
                own.link(v.tensor_tensor(r_a[:, :, :], r_a[:, :, :],
                                         ranks[:, :].unsqueeze(1).broadcast_to([P, T, NE]), ALU.mult))
                own.link(v.tensor_reduce(r_s[:, 4, :], r_a[:, :, :], AX.X, ALU.max))
                own.link(v.tensor_tensor(one[:, :, :], r_a[:, :, :], bc(4), ALU.is_equal))
                if k == 2:
                    own.link(v.scalar_tensor_tensor(r_b[:, :, :], one[:, :, :], -2.0, r_b[:, :, :], ALU.mult, ALU.add))
            own.link(v.tensor_tensor(r_s[:, 4, :], r_s[:, 2, :], r_s[:, 3, :], ALU.add))
            own.link(v.reciprocal(r_s[:, 4, :], r_s[:, 4, :]))
            own.link(v.tensor_scalar(alpha_sb[:, :], alpha_sb[:, :], -0.5, 2.0, ALU.max, ALU.min))
            own.link(v.tensor_scalar(r_s[:, 4, :], r_s[:, 4, :], alpha_sb[:, 0:1], None, ALU.mult))
            for k in (2, 3):
                own.step(v.tensor_tensor(r_s[:, k, :], r_s[:, k, :], r_s[:, 4, :], ALU.mult))
            own.wait()
            own.step(v.tensor_tensor(r_one[:, :, :], r_one[:, :, :], bc(2), ALU.mult))
            own.link(v.tensor_tensor(r_two[:, :, :], r_two[:, :, :], bc(3), ALU.mult))
            v.tensor_tensor(comb[:, :, :], r_one[:, :, :], r_two[:, :, :], ALU.add).then_inc(acc_done, 1)
            dve.wait_ge(acc_done, 1)
            v.memset(r_a[:, :, :], 0.0).then_inc(hid_ready, 1)

            with dve.Fori(0, G) as blk:
                def accumulate(e):
                    dve.wait_ge(down_psum, blk * NE + (e + 1))
                    for j in range(TG):
                        acc = h_all[:, bass.ds(blk * TG + j, 1), :].rearrange("p a f -> p (a f)")
                        ins = v.scalar_tensor_tensor(
                            acc, banks[:, 4 + e % 2, j * P:(j + 1) * P],
                            comb[:, bass.ds(blk * TG + j, 1), e], acc, ALU.mult, ALU.add)
                        ins.then_inc(acc_done, 1)

                for e in range(NE):
                    for j, (_, m) in enumerate(HC):
                        k = 3 * e + j
                        dve.wait_ge(gate_done, blk * 3 * NE + (k + 1))
                        v.tensor_tensor(hidden[0:m, e % 2, j, :], gated[0:m, k % 2, :],
                                        banks[0:m, 2 * (k % 2) + 1, :], ALU.mult).then_inc(hid_ready, 1)
                    if e >= 1:
                        accumulate(e - 1)
                        dve.wait_ge(acc_done, blk * NE * TG + (e * TG + 1))
                accumulate(NE - 1)
                dve.wait_ge(acc_done, blk * NE * TG + (NE * TG + 1))

            for g in range(G):
                tl = slice(g * TG, (g + 1) * TG)
                normalise(lambda j: h_all[:, g * TG + j, :], lambda j: h_all[:, g * TG + j, :], LN_EPS)
                v.tensor_tensor(x_all[:, tl, :], x_all[:, tl, :], h_all[:, tl, :], ALU.add).then_inc(result_ready, 1)

        @block.tensor
        def _(pe):
            mm = nc.tensor.matmul
            pe.wait_ge(const_ready, 3)
            pe.wait_ge(w_in, N_W * 16)
            for g in range(G):
                pe.wait_ge(xn_ready, g + 1)
                if g:
                    pe.wait_ge(xnT_ready, g)
                for j in range(TG):
                    ins = nc.tensor.transpose(banks[:, 0, j * P:(j + 1) * P], xn[:, g % 2, j, :], ident[:, :])
                ins.then_inc(xT_psum, 1)
                pe.wait_ge(xnT_ready, g + 1)
                if g:
                    pe.wait_ge(proj_out, 4 * g)
                    pe.wait_ge(ab_sig, g)
                rhs = xgT[:, g % 2, :]
                for w in range(4):
                    mm(banks[:, 1 + w, :], w_proj[:, w, :], rhs, start=True, stop=True)
                mm(banks[0:2 * H, 5, :], w_ab[:, :], rhs, start=True, stop=True).then_inc(proj_psum, 1)
            pe.wait_ge(xnT_ready, G)
            pe.wait_ge(proj_out, 4 * G)
            for n in range(NB):
                done = n * N_SLOT
                for s in range(SLOTS):
                    done += C if s < D else C - (s - D)
                    pe.wait_ge(slots_ready, done)
                    mm(banks[:, n, :], ident[:, :], slots[:, s].rearrange("p t d -> p (t d)"),
                       start=(s == 0), stop=(s == SLOTS - 1)).then_inc(slots_used, 1)
            pe.wait_ge(y_ready, 1)
            pe.wait_ge(ab_sig, G)
            for g in range(G):
                for j in range(TG):
                    i = g * TG + j
                    ins = mm(banks[:, 4 + g, j * P:(j + 1) * P], yT[:, i * P:(i + 1) * P], w_o[:, :], start=True, stop=True)
                ins.then_inc(wo_psum, 1)
            for g in range(G):
                pe.wait_ge(xn_ready, G + g + 1)
                for j in range(TG):
                    ins = nc.tensor.transpose(banks[:, g, j * P:(j + 1) * P], xn[:, 1, j, :], ident[:, :])
                ins.then_inc(xT_psum, 1)
            pe.wait_ge(xnT_ready, 2 * G)
            for i in range(T):
                ins = mm(banks[:, 4, i * NE:(i + 1) * NE], xnT[:, i * P:(i + 1) * P], w_router[:, :], start=True, stop=True)
            ins.then_inc(logit_psum, 1)
            pe.wait_ge(gu_in, 16)
            pe.wait_ge(down_in, 48)
            pe.wait_ge(exp_in, 1)
            with pe.Fori(0, G) as blk:
                rhs = xnT[:, bass.ds(blk * N, N)]

                def down(e):
                    pe.wait_ge(hid_ready, blk * 3 * NE + (3 * (e + 1) + 1))
                    pe.wait_ge(acc_done, blk * NE * TG + (max(e - 1, 0) * TG + 1))
                    for j in range(TG):
                        for q, (_, m) in enumerate(HC):
                            ins = mm(banks[:, 4 + e % 2, j * P:(j + 1) * P], hidden[0:m, e % 2, q, j * P:(j + 1) * P],
                                     down_w[0:m, e, q, :], start=(q == 0), stop=(q == 2))
                    ins.then_inc(down_psum, 1)

                for e in range(NE):
                    for j, (h0, m) in enumerate(HC):
                        k = 3 * e + j
                        pe.wait_ge(hid_ready, blk * 3 * NE + max(k, 1))
                        mm(banks[0:m, 2 * (k % 2), :], gu_w[:, e, h0:h0 + m], rhs, start=True, stop=True)
                        mm(banks[0:m, 2 * (k % 2) + 1, :], gu_w[:, e, HID + h0:HID + h0 + m], rhs,
                           start=True, stop=True).then_inc(gu_psum, 1)
                    if e >= 1:
                        down(e - 1)
                down(NE - 1)


_INS = ['L0_attn_x', 'L0_attn_Wq', 'L0_attn_bq', 'L0_attn_Wk', 'L0_attn_bk', 'L0_attn_Wv', 'L0_attn_bv',
        'L0_attn_q_conv', 'L0_attn_k_conv', 'L0_attn_v_conv', 'L0_attn_Wa', 'L0_attn_ba', 'L0_attn_Wb', 'L0_attn_bb',
        'L0_attn_Wg', 'L0_attn_bg', 'L0_attn_gn_scale', 'L0_attn_gn_bias', 'L0_attn_Wo', 'L0_attn_bo',
        'L0_ffn_norm_weight', 'L0_ffn_router_weight', 'L0_ffn_gate_up_weight', 'L0_ffn_down_weight',
        'L0_ffn_residual_alpha']


def kernel(**inputs):
    import numpy as _np
    import concourse.bacc as _bacc
    from concourse import mybir as _mybir
    from concourse.bass_utils import run_bass_kernel_spmd as _run

    nc = _bacc.Bacc("TRN2", target_bir_lowering=False, num_devices=1)
    laid = {n: _np.asarray(inputs[n]) for n in _INS}
    laid['L0_attn_x'] = laid['L0_attn_x'].reshape(B * S, P)
    laid['L0_ffn_router_weight'] = laid['L0_ffn_router_weight'].T
    laid['L0_ffn_gate_up_weight'] = laid['L0_ffn_gate_up_weight'].transpose(2, 0, 1)
    laid['L0_ffn_down_weight'] = laid['L0_ffn_down_weight'].transpose(0, 2, 1)
    laid['L0_ffn_residual_alpha'] = laid['L0_ffn_residual_alpha'].reshape(1)
    arrays, args = {}, []
    for name in _INS:
        a = _np.ascontiguousarray(laid[name])
        arrays[f"in_{name}_dram"] = a
        args.append(nc.dram_tensor(f"in_{name}_dram", a.shape, _mybir.dt.from_np(a.dtype), kind="ExternalInput").ap())
    res = nc.dram_tensor("out_0_dram", (B * S, P), F32, kind="ExternalOutput").ap()
    build(nc, *args, res)
    r = _run(nc, [arrays], core_ids=[0])
    return r.results[0]["out_0_dram"].reshape(B, S, P)
```

```python
import concourse.bass as bass
from concourse import mybir
from contextlib import ExitStack

F32 = mybir.dt.float32
I32 = mybir.dt.int32
BF16 = mybir.dt.bfloat16
ALU = mybir.AluOpType
ACT = mybir.ActivationFunctionType
AX = mybir.AxisListType

P = 128
B, S = 8, 256
H, D = 16, 8
NE, HID = 8, 352
C = 8
NH = 2
SH = S // NH
CH = SH // C
NC = S // C
T = B * S // P
G = 4
TG = T // G
N = TG * P
KW = 4
PAD = S + KW - 1
LN_EPS, GN_EPS, RMS_EPS, QK_EPS = 1e-5, 1e-5, 1e-6, 1e-6
HC = [(0, 128), (128, 128), (256, 96)]
NLOW = C * (C - 1) // 2
LOW = [sum(C - 1 - k for k in range(i)) for i in range(C)]
DB = 32
NB = S // DB
CB = DB // C
SLOTS = D + C
RING = 4
DL = D // 2
ROUND = 1.5 * 2 ** 23
NT = (B * S * 2 + NE * (P - 1)) // P
RG = 8
SLOTS_DVE = [1, 3, 5, 7, 8, 9, 10, 11, 12]


class Steps:

    def __init__(self, eng, sem):
        self.eng, self.sem, self.n = eng, sem, 0

    def step(self, ins):
        ins.then_inc(self.sem, 1)
        self.n = self.n + 1

    def link(self, ins):
        self.step(ins)
        self.eng.wait_ge(self.sem, self.n)

    def wait(self):
        self.eng.wait_ge(self.sem, self.n)


def group(g):
    return g // 2, TG * (g % 2)


def out_product(eng, slots, s, n, qn, states, us, aq_low, aq_diag, signal):
    dst = slots[:, s].rearrange("p (c r) d -> p r c d", r=C)
    c0, c1 = n * CB, (n + 1) * CB
    if s < D:
        eng.tensor_tensor(
            slots[:, s].rearrange("p (c r) d -> p c r d", r=C),
            states[:, c0:c1, :].rearrange("p c (d e) -> p c d e", d=D)[:, :, :, s].unsqueeze(2).broadcast_to([P, CB, C, D]),
            qn[:, n * DB:(n + 1) * DB, s:s + 1].rearrange("p (c r) a -> p c r a", r=C).broadcast_to([P, CB, C, D]),
            ALU.mult).then_inc(signal, 1)
        return
    i = s - D
    u = us[:, n * DB:(n + 1) * DB, :].rearrange("p (c r) d -> p r c d", r=C)
    eng.tensor_tensor(dst[:, i], u[:, i], aq_diag[:, i, c0:c1].unsqueeze(2).broadcast_to([P, CB, D]),
                      ALU.mult).then_inc(signal, 1)
    if i < C - 1:
        m = C - 1 - i
        eng.tensor_tensor(dst[:, i + 1:C], u[:, i:i + 1].broadcast_to([P, m, CB, D]),
                          aq_low[:, LOW[i]:LOW[i] + m, c0:c1].unsqueeze(3).broadcast_to([P, m, CB, D]),
                          ALU.mult).then_inc(signal, 1)


def products(s):
    return 2 if D <= s < SLOTS - 1 else 1


def build(nc, x, Wq, bq, Wk, bk, Wv, bv, q_conv, k_conv, v_conv, Wa, ba, Wb, bb, Wg, bg,
          gn_scale, gn_bias, Wo, bo, norm_w, router_t, gu_t, down_t, res_alpha, conv_rows, head_mask, batch_mask, out):
    ctx = ExitStack()
    with ctx:
        def sb(name, shape):
            return ctx.enter_context(nc.sbuf_tensor(name, shape, F32))

        def sem(name):
            return ctx.enter_context(nc.semaphore(name))

        qkv_d = nc.dram_tensor("qkv_scratch", [NH, 3, B, P, SH], F32, kind="Internal").ap()
        ab_d = nc.dram_tensor("ab_scratch", [NH, 2, B, H, SH], F32, kind="Internal").ap()
        o_d = nc.dram_tensor("o_scratch", [NB, B, P, DB], F32, kind="Internal").ap()

        nm_d = nc.dram_tensor("expert_inputs", [B * S, P], F32, kind="Internal").ap()
        y_d = nc.dram_tensor("expert_rows", [2 * B * S + NT * P, P], F32, kind="Internal").ap()

        w_proj = sb("w_proj", [P, 4, P])
        w_tap = sb("w_tap", [P, 3, KW, P])
        w_ab = sb("w_ab", [P, 2 * H])
        w_o = sb("w_o", [P, P])
        w_router = sb("w_router", [P, NE])
        conv_w = sb("conv_w", [P, 3, KW])
        conv_b = sb("conv_b", [P, 3, KW])
        bias_qkvg = sb("bias_qkvg", [P, 4])
        bias_ab = sb("bias_ab", [2 * H, 1])
        gn_sb = sb("gn_sb", [P, 2])
        normw_sb = sb("normw_sb", [P, 1])
        alpha_sb = sb("alpha_sb", [P, 1])
        bo_all = sb("bo_all", [P, P])
        zeros = sb("zeros", [P, P])
        ident = sb("ident", [P, P])
        h_mask = sb("h_mask", [P, P])
        b_mask = sb("b_mask", [P, B])
        mhalf = sb("mhalf", [P, TG])
        ranks = sb("ranks", [P, NE])

        x_all = sb("x_all", [P, T, P])
        x_bh = x_all[:, :, :].rearrange("p (b h) f -> p b h f", h=NH)
        xn = sb("xn", [P, 2, TG, P])
        x_pad = sb("x_pad", [P, B, PAD])
        gateT = sb("gateT", [P, B, S])
        qs = sb("qs", [P, 2, 3, TG, P])
        ab_sb = sb("ab_sb", [2 * H, B, SH])
        raw = sb("raw", [P, NH, 3, D, SH])
        ab_bh = sb("ab_bh", [P, NH, 2, SH])
        kn = sb("kn", [P, S, D])
        qn = sb("qn", [P, S, D])
        wx = sb("wx", [P, S, D])
        us = sb("us", [P, S, D])
        ring = sb("ring", [P, 2 * RING * C * D * (D + 1)])
        ws = ring[:, :].rearrange("p (c r d e) -> p c r d e", c=2 * RING, r=C, d=D)
        states = sb("states", [P, NC + 1, D * D])
        outer = sb("outer", [P, 2, D * D, C + 1])
        slots_buf = sb("slots_buf", [P, 8192])
        slots = slots_buf[:, 0:SLOTS * DB * D].rearrange("p (s t d) -> p s t d", s=SLOTS, t=DB)
        ss = sb("ss", [P, 2, SH])
        rn = sb("rn", [P, 2, SH])
        gram = sb("gram", [P, NLOW, CH])
        aq_low = sb("aq_low", [P, NLOW, NC])
        aq_diag = sb("aq_diag", [P, C, NC])
        dec = sb("dec", [P, NLOW, NC])
        gc = sb("gc", [P, C, NC])
        gc_neg = sb("gc_neg", [P, C, CH])
        tail = sb("tail", [P, C - 1, CH])
        stats = sb("stats", [P, T, 6])
        mv = sb("mv", [P, T, 2])
        rstd = sb("rstd", [P, T])
        shift = sb("shift", [P, T])
        spread = sb("spread", [P, 2, T])
        factor = sb("factor", [P, 2, T])
        gn_part = sb("gn_part", [P, 2, NB])
        gn_s = sb("gn_s", [P, 8])
        gn_rhs = sb("gn_rhs", [P, 2, B])
        gn_ab = sb("gn_ab", [P, 2, B])
        l_tri = ctx.enter_context(nc.sbuf_tensor("l_tri", [P, P], BF16))
        all_ones = sb("all_ones", [P, 2 * P])
        ones_16 = ctx.enter_context(nc.sbuf_tensor("ones_16", [P, P], BF16))
        col_no = sb("col_no", [P, P])
        column_no = sb("column_no", [P, T, 2])
        in_column = sb("in_column", [P, T, 2])
        past_no = sb("past_no", [P, NT])
        tile_e = sb("tile_e", [P, NT + 1])
        tile_no = col_no[:, 0:NT + 1]
        tile_cmp = sb("tile_cmp", [P, NT + 1, NE])
        onehot = ctx.enter_context(nc.sbuf_tensor("onehot", [P, NE, T, 2], BF16))
        incl = sb("incl", [P, NE, T, 2])
        place = sb("place", [P, NE, T, 2])
        r_e = sb("r_e", [P, 6, NE])
        weight = sb("weight", [P, T, 2])
        slot_f = sb("slot_f", [P, T, 2])
        tile_ei = ctx.enter_context(nc.sbuf_tensor("tile_ei", [P, NT + 1], I32))
        tile_of = sb("tile_of", [P, T, 2])
        row_of = sb("row_of", [P, T, 2])
        dest_f = sb("dest_f", [P, NT])
        src_f = sb("src_f", [P, NT])
        dest = ctx.enter_context(nc.sbuf_tensor("dest", [P, NT], I32))
        src = ctx.enter_context(nc.sbuf_tensor("src", [P, NT], I32))
        r_a = sb("r_a", [P, T, NE])
        r_b = sb("r_b", [P, T, NE])
        r_c = sb("r_c", [P, T, NE])
        r_p = sb("r_p", [P, T, NE])
        r_s = sb("r_s", [P, 6, T])

        conv_r = slots_buf[:, 0:3 * KW * P].rearrange("p (w k f) -> p w k f", w=3, k=KW)
        QK = (NLOW + C) * CH * D
        square = slots_buf[:, QK:QK + 2 * D * SH]
        kk = ring[:, 0:NLOW * CH * D].rearrange("p (m c e) -> p m c e", m=NLOW, c=CH)
        TMP = (C - 1) * CH * D
        w_tmp, u_tmp = ring[:, 0:TMP], ring[:, TMP:2 * TMP]
        qk = slots_buf[:, 0:QK].rearrange("p (m c e) -> p m c e", m=NLOW + C, c=CH)
        og = qs[:, :, :, :, :].rearrange("p a w j t -> p (a w j t)")[:, 0:S * D].rearrange(
            "p (n d t) -> p n d t", n=NB, d=D)
        sq_dump = xn[:, :, :, :].rearrange("p a j t -> p a (j t)")
        gu_w = raw[:, :, :, :, :].rearrange("p a w d t -> p (a w d t)")[:, 0:NE * 2 * HID].rearrange("p (e n) -> p e n", e=NE)
        down_w = ring[:, 0:NE * 3 * P].rearrange("p (e j n) -> p e j n", e=NE, j=3)
        gT = slots_buf[:, SLOTS * DB * D:SLOTS * DB * D + B * S].rearrange("p (n b t) -> p n b t", n=NB, b=B)
        yT = wx[:, :, :].rearrange("p t d -> p (t d)").rearrange("p (b t) -> p b t", b=B)
        h_all = kn[:, :, :].rearrange("p t d -> p (t d)").rearrange("p (i f) -> p i f", i=T)
        nm = qs[:, :, :, :, :].rearrange("p a w j t -> p (a w j t)")[:, 0:T * P].rearrange("p (i f) -> p i f", i=T)
        nm_all = us[:, :, :].rearrange("p t d -> p (t d)").rearrange("p (i f) -> p i f", i=T)
        xnT = qn[:, :, :].rearrange("p t d -> p (t d)")
        GU = 2 * HID
        FT = 2 * T
        row_hot = slots_buf[:, 0:FT * P // 2].bitcast(BF16).rearrange("p (c r) -> p c r", c=FT)
        tile_hot = slots_buf[:, FT * P // 2:FT * (P // 2 + NT)].bitcast(BF16).rearrange("p (c w t) -> p c w t", c=FT, w=2)
        tile_one = slots_buf[:, FT * (P // 2 + NT):FT * (P // 2 + 2 * NT)].rearrange("p (c t) -> p c t", c=FT)
        o1 = FT * (P // 2 + 2 * NT)
        hidden = slots_buf[:, o1:o1 + 6 * P].rearrange("p (k n) -> p k n", k=2)
        states_flat = states[:, :, :].rearrange("p c f -> p (c f)")
        xgT = states_flat[:, 0:2 * P].rearrange("p (k n) -> p k n", k=2)
        gu_cur = states_flat[:, 2 * P:2 * P + 2 * GU].rearrange("p (k n) -> p k n", k=2)
        down_cur = wx[:, :, :].rearrange("p t d -> p (t d)")[:, 0:6 * P].rearrange("p (k j n) -> p k j n", k=2, j=3)
        y_sb = wx[:, :, :].rearrange("p t d -> p (t d)")[:, 6 * P:8 * P].rearrange("p (k n) -> p k n", k=2)
        xg = us[:, :, :].rearrange("p t d -> p (t d)")[:, 0:RG * P].rearrange("p (k f) -> p k f", k=RG)
        y_in = [m.rearrange("p (j k f) -> p j k f", j=TG, k=2) for m in (
            gateT[:, :, :].rearrange("p b t -> p (b t)")[:, 0:2 * N], gateT[:, :, :].rearrange("p b t -> p (b t)")[:, 2 * N:4 * N],
            xnT[:, 0:2 * N], xnT[:, 2 * N:4 * N])]

        banks = ctx.enter_context(nc.psum_tensor("banks", [P, 8, N], F32))

        x_in = [sem(f"x_in{g}") for g in range(G)]
        w_conv, w_bias = sem("w_conv"), sem("w_bias")
        w_early, w_in, row_in = sem("w_early"), sem("w_in"), sem("row_in")
        gu_in, down_in = sem("gu_in"), sem("down_in")
        qs_out = [sem(f"qs_out{g}") for g in range(G)]
        ab_out = [sem(f"ab_out{h}") for h in range(NH)]
        raw_in = [sem(f"raw_in{h}") for h in range(NH)]
        v_in = [sem(f"v_in{h}") for h in range(NH)]
        ab_in = [sem(f"ab_in{h}") for h in range(NH)]
        og_out = [sem(f"og_out{n}") for n in range(NB)]
        gT_in = sem("gT_in")
        out_done = sem("out_done")
        vec, pool_s, act_s = sem("vec_steps"), sem("pool_steps"), sem("act_steps")
        const_ready, tap_ready, biases_ready = sem("const_ready"), sem("tap_ready"), sem("biases_ready")
        var_ready, rstd_ready = sem("var_ready"), sem("rstd_ready")
        xn_ready, xT_psum, xnT_ready = sem("xn_ready"), sem("xT_psum"), sem("xnT_ready")
        proj_psum, edge_ready, silu_ready = sem("proj_psum"), sem("edge_ready"), sem("silu_ready")
        gate_psum, gram_psum, kk_ready = sem("gate_psum"), sem("gram_psum"), sem("kk_ready")
        v_scaled, gram_used = sem("v_scaled"), sem("gram_used")
        gate_ready, ab_moved, ab_sig = sem("gate_ready"), sem("ab_moved"), sem("ab_sig")
        sq_ready, ss_ready, root_ready = sem("sq_ready"), sem("ss_ready"), sem("root_ready")
        kq_ready = sem("kq_ready")
        decay_ready, kd_ready, qg_ready = sem("decay_ready"), sem("kd_ready"), sem("qg_ready")
        qk_ready, qk_psum, aq_moved = sem("qk_ready"), sem("qk_psum"), sem("aq_moved")
        u_ready, aq_ready, ln_used = sem("u_ready"), sem("aq_ready"), sem("ln_used")
        ring_ready, carry_ready, scan = sem("ring_ready"), sem("carry_ready"), sem("scan_steps")
        slots_pool, slots_dve, slots_used = sem("slots_pool"), sem("slots_dve"), sem("slots_used")
        og_sum, og_sq = sem("og_sum"), sem("og_sq")
        gn_var, gn_rstd, gn_ready, gn_psum, gn_coef = (sem("gn_var"), sem("gn_rstd"), sem("gn_ready"), sem("gn_psum"),
                                                       sem("gn_coef"))
        y_aff, y_ready, wo_psum = sem("y_aff"), sem("y_ready"), sem("wo_psum")
        shift_ready, ln_ready = sem("shift_ready"), sem("ln_ready")
        h_ready = sem("h_ready")
        logit_psum, exp_in, exp_done = sem("logit_psum"), sem("exp_in"), sem("exp_done")
        onehot_ready, rank_psum, tables_ready = sem("onehot_ready"), sem("rank_psum"), sem("tables_ready")
        nm_out, at_ready, tile_hot_ready = sem("nm_out"), sem("at_ready"), sem("tile_hot_ready")
        one_tile_ready, numbers_ready = sem("one_tile_ready"), sem("numbers_ready")
        row_hot_ready, rows_psum = sem("row_hot_ready"), sem("rows_psum")
        src_ready, dest_ready, number_ready = sem("src_ready"), sem("dest_ready"), sem("number_ready")
        xg_in = [sem(f"xg_in{k}") for k in range(RG)]
        xgT_psum, xgT_ready = sem("xgT_psum"), sem("xgT_ready")
        gu_cur_ready, down_cur_ready = sem("gu_cur_ready"), sem("down_cur_ready")
        gu_psum, gate_done, hid_ready = sem("gu_psum"), sem("gate_done"), sem("hid_ready")
        down_psum, y_sb_ready = sem("down_psum"), sem("y_sb_ready")
        y_out = [sem(f"y_out{k}") for k in range(2)]
        y_back = [sem(f"y_back{g}") for g in range(G)]
        result_ready = sem("result_ready")

        block = ctx.enter_context(nc.Block())
        N_CONV, N_BIAS, N_EARLY, N_W = 4, 9, 3, 7

        x_v = x.rearrange("(b h p) f -> h p b f", h=NH, p=P)

        @block.sync
        def _(sp):
            for g in range(G):
                h, b0 = group(g)
                sp.dma_start(x_bh[:, b0:b0 + TG, h, :], x_v[h, :, b0:b0 + TG, :]).then_inc(x_in[g], 16)
                if g == 0:
                    sp.dma_start(conv_r, conv_rows.partition_broadcast(P)).then_inc(w_conv, 16)
                    for i, w in enumerate((Wq, Wk, Wv)):
                        sp.dma_start(w_proj[:, i, :], w).then_inc(w_conv, 16)
                if g == 1:
                    sp.dma_start(w_proj[:, 3, :], Wg).then_inc(w_early, 16)
                    sp.dma_start(w_ab[:, 0:H], Wa).then_inc(w_early, 16)
                    sp.dma_start(w_ab[:, H:2 * H], Wb).then_inc(w_early, 16)
            col = lambda v: v.rearrange("(p a) -> p a", a=1)
            sp.dma_start(gn_sb[:, 0:1], col(gn_scale)).then_inc(w_in, 16)
            sp.dma_start(gn_sb[:, 1:2], col(gn_bias)).then_inc(w_in, 16)
            sp.dma_start(w_o[:, :], Wo).then_inc(w_in, 16)
            sp.dma_start(normw_sb[:, :], col(norm_w)).then_inc(w_in, 16)
            sp.dma_start(w_router[:, :], router_t).then_inc(w_in, 16)
            sp.dma_start(bo_all[:, :], bo.partition_broadcast(P)).then_inc(w_in, 16)
            sp.dma_start(alpha_sb[:, :], res_alpha.partition_broadcast(P)).then_inc(w_in, 16)
            sp.dma_start(h_mask[:, :], head_mask).then_inc(row_in, 16)
            sp.dma_start(b_mask[:, :], batch_mask).then_inc(row_in, 16)
            for g in range(G):
                h, b0 = group(g)
                for w in range(3):
                    sp.wait_ge(silu_ready, 3 * g + w + 1)
                    sp.dma_start(qkv_d[h, w, b0:b0 + TG].rearrange("b p t -> p b t"),
                                 qs[:, g % 2, w, :, :]).then_inc(qs_out[g], 16)
                if g % 2:
                    sp.wait_ge(qs_out[g - 1], 3 * 16)
                    sp.wait_ge(qs_out[g], 3 * 16)
                    for w in (0, 1):
                        sp.dma_start(raw[:, h, w, :, :], qkv_d[h, w].rearrange("b (h d) t -> (b h) d t", h=H)
                                     ).then_inc(raw_in[h], 16)
                    sp.dma_start(raw[:, h, 2, :, :], qkv_d[h, 2].rearrange("b (h d) t -> (b h) d t", h=H)
                                 ).then_inc(v_in[h], 16)
            sp.wait_ge(u_ready, NH)
            sp.dma_start(gu_w, gu_t).then_inc(gu_in, 16)
            def back(n):
                sp.wait_ge(og_out[n], 16)
                sp.dma_start(gT[:, n], o_d[n].rearrange("b p t -> p b t")).then_inc(gT_in, 16)

            for n in range(NB):
                sp.wait_ge(og_sum, n + 1)
                sp.dma_start(o_d[n].rearrange("b (h d) t -> (b h) d t", h=H), og[:, n]).then_inc(og_out[n], 16)
                if n >= 2:
                    back(n - 2)
            back(NB - 2)
            back(NB - 1)
            for q, (h0, m) in enumerate(HC):
                sp.dma_start(down_w[0:m, :, q, :], down_t[:, h0:h0 + m, :].rearrange("e p n -> p e n")).then_inc(down_in, 16)
            for g in range(G):
                sp.wait_ge(xn_ready, (G + g + 1) * TG)
                sp.dma_start(nm_d.rearrange("(i p) f -> p i f", p=P)[:, g * TG:(g + 1) * TG],
                             nm[:, g * TG:(g + 1) * TG, :]).then_inc(nm_out, 16)
            for k in range(2):
                sp.wait_ge(y_out[k], 16 * ((NT + 1 - k) // 2))
            for g in range(G):
                sp.dma_start(y_in[g], y_d[0:2 * B * S, :].rearrange("(i p k) f -> p i k f", p=P, k=2)[:, g * TG:(g + 1) * TG]
                             ).then_inc(y_back[g], 16)
            for g in range(G):
                sp.wait_ge(result_ready, g + 1)
                sp.dma_start(out.rearrange("(i p) f -> p i f", p=P)[:, g * TG:(g + 1) * TG, :],
                             x_all[:, g * TG:(g + 1) * TG, :]).then_inc(out_done, 16)
            sp.wait_ge(out_done, G * 16)

        @block.scalar
        def _(act):
            col = lambda v: v.rearrange("(p a) -> p a", a=1)
            for i, v in enumerate((q_conv, k_conv, v_conv)):
                act.dma_start(conv_w[:, i, :], v).then_inc(w_bias, 16)
            for i, v in enumerate((bq, bk, bv, bg)):
                act.dma_start(bias_qkvg[:, i:i + 1], col(v)).then_inc(w_bias, 16)
            act.dma_start(bias_ab[0:H, :], col(ba)).then_inc(w_bias, 16)
            act.dma_start(bias_ab[H:2 * H, :], col(bb)).then_inc(w_bias, 16)

            def squares(h):
                act.wait_ge(raw_in[h], 2 * 16)
                nc.scalar.activation(square, raw[:, h, 0:2].rearrange("p w d t -> p (w d t)"),
                                     ACT.Square).then_inc(sq_ready, 1)
                act.wait_ge(ss_ready, h + 1)
                if h:
                    act.wait_ge(kq_ready, 2 * h)
                nc.scalar.activation(rn[:, :, :].rearrange("p w t -> p (w t)"), banks[:, 3, 0:2 * SH] if h else
                                     ss[:, :, :].rearrange("p w t -> p (w t)"), ACT.Sqrt).then_inc(root_ready, 1)

            def move_aq(h):
                act.wait_ge(qk_psum, h + 1)
                nc.scalar.copy(aq_low[:, :, h * CH:(h + 1) * CH],
                               banks[:, 6, 0:NLOW * CH].rearrange("p (m c) -> p m c", m=NLOW)).then_inc(aq_moved, 1)
                nc.scalar.copy(aq_diag[:, :, h * CH:(h + 1) * CH],
                               banks[:, 7, 0:C * CH].rearrange("p (m c) -> p m c", m=C)).then_inc(aq_moved, 1)

            def pad(g):
                h, b0 = group(g)
                act.wait_ge(xT_psum, g + 1)
                nc.scalar.copy(x_pad[:, b0:b0 + TG, KW - 1 + h * SH:KW - 1 + (h + 1) * SH],
                               banks[:, 0, :].rearrange("p (b t) -> p b t", b=TG)).then_inc(xnT_ready, 1)

            pad(0)
            pad(1)
            act.wait_ge(biases_ready, 1)
            act.wait_ge(w_bias, N_BIAS * 16)
            for g in range(G):
                h, b0 = group(g)
                if 0 < g < G - 1:
                    pad(g + 1)
                if g >= 2:
                    act.wait_ge(qs_out[g - 2], 3 * 16)
                for w in range(3):
                    act.wait_ge(proj_psum, 4 * g + w + 1)
                    if h == 0:
                        act.wait_ge(edge_ready, (3 * g + w + 1) * (KW - 1))
                    nc.scalar.activation(qs[:, g % 2, w].rearrange("p j t -> p (j t)"), banks[:, 1 + w, :], ACT.Silu,
                                         bias=conv_b[:, w, KW - 1:KW]).then_inc(silu_ready, 1)
                    if g == 2 and w == 1:
                        squares(0)
                act.wait_ge(proj_psum, 4 * g + 4)
                if g == 2:
                    act.wait_ge(ab_out[0], 32)
                nc.scalar.activation(ab_sb[:, b0:b0 + TG, :], banks[0:2 * H, 5, :].rearrange("p (b t) -> p b t", b=TG),
                                     ACT.Identity, bias=bias_ab[:, 0:1]).then_inc(ab_moved, 1)
                if g % 2:
                    act.wait_ge(ab_moved, g + 1)
                    nc.scalar.activation(ab_sb[:, :, :], ab_sb[:, :, :], ACT.Sigmoid).then_inc(ab_sig, 1)
                    act.wait_ge(ab_sig, h + 1)
                    for k in range(2):
                        act.dma_start(ab_d[h, k].rearrange("b h t -> h b t"),
                                      ab_sb[k * H:(k + 1) * H, :, :]).then_inc(ab_out[h], 16)
            for g in range(G):
                h, b0 = group(g)
                act.wait_ge(gate_psum, g + 1)
                nc.scalar.activation(gateT[:, b0:b0 + TG, h * SH:(h + 1) * SH],
                                     banks[:, 4 + g % 2, :].rearrange("p (b t) -> p b t", b=TG), ACT.Silu,
                                     bias=bias_qkvg[:, 3:4]).then_inc(gate_ready, 1)
            squares(1)
            for h in range(NH):
                move_aq(h)
            act.wait_ge(decay_ready, NH)
            act.wait_ge(u_ready, NH)
            with act.Fori(0, NC // (2 * RING)) as it:
                for k in range(2 * RING):
                    if k % RING == 0:
                        act.wait_ge(scan, it * (8 * 2 * RING) + (8 * max(k - RING, 0) + 2 if k else 1))
                        nc.scalar.copy(ws[:, k:k + RING, :, :, D].rearrange("p c r d -> p (c r) d"),
                                       us[:, bass.ds(it * (2 * RING * C) + k * C, RING * C), :]).then_inc(ring_ready, 1)
                    c = it * (2 * RING) + k
                    act.wait_ge(scan, it * (8 * 2 * RING) + (8 * k + 2))
                    nc.scalar.activation(outer[:, k % 2, :, C], states[:, bass.ds(c, 1), :].rearrange("p a n -> p (a n)"),
                                         ACT.Copy, scale=gc[:, C - 1, bass.ds(c, 1)]).then_inc(carry_ready, 1)
            for n in range(NB):
                act.wait_ge(slots_used, (n + 1) * SLOTS)
                nc.scalar.activation(og[:, n], banks[:, n, 0:DB * D].rearrange("p (t d) -> p d t", d=D),
                                     ACT.Copy, accum_out=gn_part[:, 0, n:n + 1]).then_inc(og_sum, 1)
                if n >= 2:
                    act.wait_ge(og_sq, n - 1)
                nc.scalar.activation(sq_dump[:, n % 2, 0:DB * D], banks[:, n, 0:DB * D], ACT.Square,
                                     accum_out=gn_part[:, 1, n:n + 1]).then_inc(og_sq, 1)
            act.wait_ge(gT_in, NB * 16)
            act.wait_ge(gn_coef, 2)
            for b in range(B):
                nc.scalar.activation(yT[:, b, :].rearrange("p (n t) -> p n t", n=NB), gT[:, :, b, :], ACT.Identity,
                                     scale=gn_ab[:, 0, b:b + 1], bias=gn_ab[:, 1, b:b + 1]).then_inc(y_aff, 1)

            for g in range(G):
                act.wait_ge(shift_ready, g + 1)
                if g >= 2:
                    act.wait_ge(ln_used, g - 1)
                for j in range(TG):
                    i = g * TG + j
                    nc.scalar.activation(xn[:, g % 2, j, :], banks[:, 4 + g, j * P:(j + 1) * P], ACT.Identity,
                                         scale=rstd[:, i:i + 1], bias=shift[:, i:i + 1]).then_inc(ln_ready, 1)
            act.wait_ge(w_in, N_W * 16)
            for g in range(G):
                act.wait_ge(xT_psum, G + g + 1)
                nc.scalar.activation(xnT[:, g * N:(g + 1) * N], banks[:, g, :], ACT.Copy,
                                     scale=normw_sb[:, 0:1]).then_inc(xnT_ready, 1)
            act.wait_ge(exp_in, 2)
            nc.scalar.activation(r_p[:, :, :], r_c[:, :, :], ACT.Exp).then_inc(exp_done, 1)
            nc.scalar.activation(r_s[:, 3, :], r_s[:, 2, :], ACT.Exp).then_inc(exp_done, 1)

            def rows(j, k, first=False):
                act.wait_ge(xgT_psum, j + 1)
                if not first:
                    act.wait_ge(gu_psum, j - 1)
                nc.scalar.activation(xgT[:, k, :], banks[:, 7 * k, 0:P], ACT.Copy,
                                     scale=normw_sb[:, 0:1]).then_inc(xgT_ready, 1)

            def gate(j, k, first=False):
                act.wait_ge(gu_psum, j + 1)
                if not first:
                    act.wait_ge(down_psum, j - 1)
                nc.scalar.activation(hidden[:, k, :], banks[:, 1 + k, 0:3 * P], ACT.Silu).then_inc(gate_done, 1)

            def result(j, k, sent_rows=None):
                act.wait_ge(down_psum, j + 1)
                if sent_rows is not None:
                    act.wait_ge(y_out[k], sent_rows)
                nc.scalar.copy(y_sb[:, k, :], banks[:, 5 + k, 0:P]).then_inc(y_sb_ready, 1)

            rows(0, 0, True)
            rows(1, 1, True)
            gate(0, 0, True)
            rows(2, 0)
            gate(1, 1, True)
            result(0, 0)
            rows(3, 1)
            gate(2, 0)
            result(1, 1)
            with act.Fori(0, (NT - 5) // 2) as it:
                for k in (1, 0):
                    j = it * 2 + (3 if k else 4)
                    rows(j + 1, 1 - k)
                    gate(j, k)
                    result(j - 1, 1 - k, it * 16 + 16)
            rows(NT - 1, 0)
            gate(NT - 2, 1)
            result(NT - 3, 0, 16 * ((NT - 3) // 2))
            gate(NT - 1, 0)
            result(NT - 2, 1, 16 * ((NT - 3) // 2))
            result(NT - 1, 0, 16 * (NT // 2))
            for g in range(G):
                act.wait_ge(shift_ready, G + g + 1)
                for j in range(TG):
                    i = g * TG + j
                    nc.scalar.activation(nm_all[:, i, :], h_all[:, i, :], ACT.Identity,
                                         scale=rstd[:, i:i + 1], bias=shift[:, i:i + 1]).then_inc(ln_ready, 1)

        @block.gpsimd
        def _(pool):
            own = Steps(pool, pool_s)
            gp = nc.gpsimd
            own.step(gp.memset(mhalf[:, :], -0.5))
            own.link(gp.memset(ident[:, :], 0.0))
            gp.affine_select(out=ident[:, :], in_=ident[:, :], compare_op=ALU.not_equal, fill=1.0, base=0,
                             pattern=[[-1, P]], channel_multiplier=1).then_inc(const_ready, 1)
            gp.memset(x_pad[:, :, 0:KW - 1], 0.0).then_inc(const_ready, 1)

            def root(n):
                pool.wait_ge(var_ready, n + 1)
                k = (n % G) * TG
                gp.tensor_tensor(rstd[:, k:k + TG], mv[:, k:k + TG, 1], mhalf[:, :], ALU.pow).then_inc(rstd_ready, 1)

            root(0)
            root(1)
            gp.memset(states[:, 0, 0:D * DL], 0.0).then_inc(scan, 1)
            gp.memset(states[:, 0, D * DL:D * D], 0.0).then_inc(scan, 1)
            gp.iota(ranks[:, :], pattern=[[-1, NE]], base=NE, channel_multiplier=0,
                    allow_small_or_imprecise_dtypes=True).then_inc(const_ready, 1)
            gp.memset(all_ones[:, :], 1.0).then_inc(const_ready, 1)
            gp.memset(ones_16[:, :], 1.0).then_inc(const_ready, 1)
            own.step(gp.memset(zeros[:, :], 0.0))
            own.step(gp.memset(l_tri[:, :], 1.0))
            gp.iota(col_no[:, :], pattern=[[1, P]], base=0, channel_multiplier=0,
                    allow_small_or_imprecise_dtypes=True).then_inc(const_ready, 1)
            gp.iota(column_no[:, :, :], pattern=[[2 * P, T], [0, 2]], base=2 * P, channel_multiplier=0,
                    allow_small_or_imprecise_dtypes=True).then_inc(tables_ready, 1)
            gp.iota(in_column[:, :, :], pattern=[[0, T], [1, 2]], base=0, channel_multiplier=2,
                    allow_small_or_imprecise_dtypes=True).then_inc(tables_ready, 1)
            gp.iota(past_no[:, :], pattern=[[P, NT]], base=2 * B * S + 2 * P, channel_multiplier=1,
                    allow_small_or_imprecise_dtypes=True).then_inc(tables_ready, 1)
            root(2)
            root(3)
            own.wait()
            gp.affine_select(out=l_tri[:, :], in_=l_tri[:, :], compare_op=ALU.is_gt, fill=0.0, base=0,
                             pattern=[[1, P]], channel_multiplier=-1).then_inc(const_ready, 1)
            k4 = kn[:, :, :].rearrange("p (c r) e -> p r c e", r=C)
            q4 = qn[:, :, :].rearrange("p (c r) e -> p r c e", r=C)
            for h in range(NH):
                c0, c1 = h * CH, (h + 1) * CH
                pool.wait_ge(ab_out[h], 32)
                pool.dma_start(ab_bh[:, h, :, :], ab_d[h].rearrange("k b h t -> (b h) k t")).then_inc(ab_in[h], 16)
                pool.wait_ge(ab_in[h], 16)
                al = ab_bh[:, h, 0, :].rearrange("p (c r) -> p r c", r=C)
                pool.wait_ge(v_in[h], 16)
                gp.tensor_tensor(us[:, h * SH:(h + 1) * SH, :].rearrange("p t d -> p d t"), raw[:, h, 2],
                                 ab_bh[:, h, 1:2, :].broadcast_to([P, D, SH]), ALU.mult).then_inc(v_scaled, 1)
                for i in range(C - 1):
                    own.step(gp.tensor_copy(dec[:, LOW[i], c0:c1], al[:, i + 1, :]))
                own.step(gp.tensor_copy(gc[:, 0, c0:c1], al[:, 0, :]))
                own.wait()
                for i in range(C - 3, -1, -1):
                    n = C - 2 - i
                    own.link(gp.tensor_tensor(dec[:, LOW[i] + 1:LOW[i] + 1 + n, c0:c1],
                                              dec[:, LOW[i + 1]:LOW[i + 1] + n, c0:c1],
                                              al[:, i + 1:i + 2, :].broadcast_to([P, n, CH]), ALU.mult))
                gp.tensor_tensor(gc[:, 1:C, c0:c1], dec[:, 0:C - 1, c0:c1],
                                 al[:, 0:1, :].broadcast_to([P, C - 1, CH]), ALU.mult).then_inc(decay_ready, 1)
                pool.wait_ge(kq_ready, 2 * (h + 1))
                if h:
                    pool.wait_ge(qk_psum, h)
                for i in range(C - 1):
                    n = C - 1 - i
                    gp.tensor_tensor(qk[:, LOW[i]:LOW[i] + n], q4[:, i + 1:C, c0:c1],
                                     k4[:, i:i + 1, c0:c1].broadcast_to([P, n, CH, D]), ALU.mult).then_inc(qk_ready, 1)
                gp.tensor_tensor(qk[:, NLOW:NLOW + C], q4[:, :, c0:c1], k4[:, :, c0:c1], ALU.mult).then_inc(qk_ready, 1)
                for i in range(C - 1):
                    own.step(gp.tensor_copy(tail[:, i, :], dec[:, LOW[i] + C - 2 - i, c0:c1]))
                own.wait()
                pool.wait_ge(qk_ready, C * (h + 1))
                pool.wait_ge(kk_ready, (C - 1) * (h + 1))
                gp.tensor_tensor(k4[:, 0:C - 1, c0:c1], k4[:, 0:C - 1, c0:c1],
                                 tail[:, :, :].unsqueeze(3).broadcast_to([P, C - 1, CH, D]), ALU.mult).then_inc(kd_ready, 1)
                gp.tensor_tensor(q4[:, :, c0:c1], q4[:, :, c0:c1],
                                 gc[:, :, c0:c1].unsqueeze(3).broadcast_to([P, C, CH, D]), ALU.mult).then_inc(qg_ready, 1)
                pool.wait_ge(kd_ready, h + 1)
            for h in range(NH):
                c0, c1 = h * CH, (h + 1) * CH
                pool.wait_ge(aq_moved, 2 * (h + 1))
                gp.tensor_tensor(aq_low[:, :, c0:c1], aq_low[:, :, c0:c1], dec[:, :, c0:c1], ALU.mult).then_inc(aq_ready, 1)
            pool.wait_ge(qk_psum, NH)
            for i in range(1, C):
                own.step(gp.memset(slots[:, D + i].rearrange("p (c r) d -> p c r d", r=C)[:, :, 0:i], 0.0))
            own.wait()
            pool.wait_ge(qg_ready, NH)
            pool.wait_ge(aq_ready, NH)
            for n in range(NB):
                pool.wait_ge(scan, 8 * CB * (n + 1) + 2)
                for s in range(SLOTS):
                    if n == NB - 1 and s in SLOTS_DVE:
                        continue
                    if n:
                        pool.wait_ge(slots_used, (n - 1) * SLOTS + s + 1)
                    out_product(gp, slots, s, n, qn, states, us, aq_low, aq_diag, slots_pool)
            pool.wait_ge(gn_var, 1)
            gp.tensor_tensor(gn_s[:, 4:5], gn_s[:, 3:4], mhalf[:, 0:1], ALU.pow).then_inc(gn_rstd, 1)
            for g in range(G):
                root(G + g)
            for g in range(G):
                pool.wait_ge(var_ready, 2 * G + g + 1)
                k = g * TG
                gp.tensor_tensor(factor[:, :, k:k + TG], spread[:, :, k:k + TG],
                                 mhalf[:, :].unsqueeze(1).broadcast_to([P, 2, TG]), ALU.pow).then_inc(rstd_ready, 1)
            pool.wait_ge(rstd_ready, 3 * G)
            for i in range(T):
                gp.tensor_scalar(h_all[:, i, :], x_all[:, i, :], mv[:, i, 0:1], factor[:, 0, i:i + 1],
                                 ALU.subtract, ALU.mult).then_inc(h_ready, 1)
            pool.wait_ge(tables_ready, 3)
            pool.wait_ge(one_tile_ready, 1)
            gp.tensor_tensor(tile_hot[:, :, 0, :], tile_one,
                             column_no[:, :, :].rearrange("p i k -> p (i k)").unsqueeze(2).broadcast_to([P, FT, NT]),
                             ALU.mult).then_inc(numbers_ready, 1)
            pool.wait_ge(nm_out, G * 16)
            pool.wait_ge(src_ready, 1)
            for j in range(NT + RG - 1):
                if j < NT:
                    if j >= RG:
                        pool.wait_ge(xgT_psum, j - RG + 1)
                    gp.indirect_dma_start(out=xg[:, j % RG, :], out_offset=None, in_=nm_d,
                                          in_offset=bass.IndirectOffsetOnAxis(ap=src[:, j:j + 1], axis=0)
                                          ).then_inc(xg_in[j % RG], 16)
                i = j - (RG - 1)
                if i >= 0:
                    if i == 0:
                        pool.wait_ge(dest_ready, 1)
                    pool.wait_ge(y_sb_ready, i + 1)
                    gp.indirect_dma_start(out=y_d, out_offset=bass.IndirectOffsetOnAxis(ap=dest[:, i:i + 1], axis=0),
                                          in_=y_sb[:, i % 2, :], in_offset=None).then_inc(y_out[i % 2], 16)
            for g in range(G):
                root(3 * G + g)

        @block.vector
        def _(dve):
            own = Steps(dve, vec)
            v = nc.vector
            roots = [0]

            def moments(g, src):
                for j in range(TG):
                    own.step(v.bn_stats(stats[:, g * TG + j, :], src(j)))
                own.wait()
                for j in range(TG):
                    own.step(v.bn_aggr(mv[:, g * TG + j, :], stats[:, g * TG + j, :]))
                own.wait()

            def statistics(g, src):
                moments(g, src)
                k = slice(g * TG, (g + 1) * TG)
                v.tensor_scalar(mv[:, k, 1], mv[:, k, 1], LN_EPS, None, ALU.add).then_inc(var_ready, 1)

            def await_root():
                roots[0] += 1
                dve.wait_ge(rstd_ready, roots[0])

            def scale_shift(g):
                await_root()
                k = slice(g * TG, (g + 1) * TG)
                v.scalar_tensor_tensor(shift[:, k], mv[:, k, 0], -1.0, rstd[:, k], ALU.mult, ALU.mult).then_inc(shift_ready, 1)

            dve.wait_ge(x_in[0], 16)
            statistics(0, lambda j: x_bh[:, j, 0, :])
            await_root()
            for j in range(TG):
                v.tensor_scalar(xn[:, 0, j, :], x_bh[:, j, 0, :], mv[:, j, 0:1], rstd[:, j:j + 1],
                                ALU.subtract, ALU.mult).then_inc(xn_ready, 1)
            for w in range(3):
                dve.wait_ge(w_conv, N_CONV * 16)
                v.tensor_tensor(w_tap[:, w], w_proj[:, w:w + 1, :].broadcast_to([P, KW, P]), conv_r[:, w],
                                ALU.mult).then_inc(tap_ready, 1)
            dve.wait_ge(w_bias, N_BIAS * 16)
            for k in range(1, KW):
                own.link(v.tensor_tensor(conv_w[:, :, k], conv_w[:, :, k], conv_w[:, :, k - 1], ALU.add))
            v.tensor_tensor(conv_b[:, :, :], conv_w[:, :, :], bias_qkvg[:, 0:3].unsqueeze(2).broadcast_to([P, 3, KW]),
                            ALU.mult).then_inc(biases_ready, 1)
            dve.wait_ge(biases_ready, 1)

            def ln_in(g):
                h, b0 = group(g)
                k = g * TG
                dve.wait_ge(x_in[g], 16)
                statistics(g, lambda j: x_bh[:, b0 + j, h, :])
                await_root()
                if g >= 2:
                    dve.wait_ge(xT_psum, g - 1)
                for j in range(TG):
                    v.tensor_scalar(xn[:, g % 2, j, :], x_bh[:, b0 + j, h, :], mv[:, k + j, 0:1], rstd[:, k + j:k + j + 1],
                                    ALU.subtract, ALU.mult).then_inc(xn_ready, 1)

            def edges(g):
                for w in range(3):
                    dve.wait_ge(proj_psum, 4 * g + w + 1)
                    for t in range(KW - 1):
                        col = banks[:, 1 + w, :].rearrange("p (b t) -> p b t", b=TG)[:, :, t]
                        v.tensor_scalar(col, col, conv_b[:, w, KW - 2 - t:KW - 1 - t], None,
                                        ALU.subtract).then_inc(edge_ready, 1)

            ln_in(1)
            edges(0)
            ln_in(2)
            edges(1)
            ln_in(3)

            k4 = kn[:, :, :].rearrange("p (c r) e -> p r c e", r=C)
            w4 = wx[:, :, :].rearrange("p (c r) e -> p r c e", r=C)
            u4 = us[:, :, :].rearrange("p (c r) e -> p r c e", r=C)
            for h in range(NH):
                c0, c1 = h * CH, (h + 1) * CH
                t0, t1 = h * SH, (h + 1) * SH
                if h == 0:
                    dve.wait_ge(sq_ready, 1)
                    v.tensor_reduce(ss[:, :, :], square.rearrange("p (w d t) -> p w t d", w=2, d=D),
                                    AX.X, ALU.add).then_inc(ss_ready, 1)
                dve.wait_ge(root_ready, h + 1)
                own.link(v.tensor_scalar(rn[:, :, :], rn[:, :, :], QK_EPS, None, ALU.add))
                own.link(v.reciprocal(rn[:, :, :], rn[:, :, :]))

                def normed(w, dst):
                    v.tensor_tensor(dst[:, t0:t1, :].rearrange("p t d -> p d t"), raw[:, h, w],
                                    rn[:, w:w + 1, :].broadcast_to([P, D, SH]), ALU.mult).then_inc(kq_ready, 1)

                normed(1, kn)
                dve.wait_ge(kq_ready, 2 * h + 1)
                dve.wait_ge(ab_in[h], 16)
                be = ab_bh[:, h, 1, :]
                own.link(v.tensor_tensor(wx[:, t0:t1, :], kn[:, t0:t1, :], be.unsqueeze(2).broadcast_to([P, SH, D]), ALU.mult))
                for i in range(C - 1):
                    n = C - 1 - i
                    v.tensor_tensor(kk[:, LOW[i]:LOW[i] + n], w4[:, i + 1:C, c0:c1],
                                    k4[:, i:i + 1, c0:c1].broadcast_to([P, n, CH, D]), ALU.mult).then_inc(kk_ready, 1)
                normed(0, qn)
                dve.wait_ge(decay_ready, h + 1)
                own.step(v.tensor_scalar(gc_neg[:, :, :], gc[:, :, c0:c1], -1.0, None, ALU.mult))
                own.wait()
                dve.wait_ge(kk_ready, (C - 1) * (h + 1))
                own.step(v.tensor_tensor(w4[:, :, c0:c1], w4[:, :, c0:c1],
                                         gc_neg[:, :, :].unsqueeze(3).broadcast_to([P, C, CH, D]), ALU.mult))
                dve.wait_ge(gram_psum, h + 1)
                v.tensor_tensor(gram[:, :, :], banks[:, 0, 0:NLOW * CH].rearrange("p (m c) -> p m c", m=NLOW),
                                dec[:, :, c0:c1], ALU.mult).then_inc(gram_used, 1)
                dve.wait_ge(gram_used, h + 1)
                own.wait()
                dve.wait_ge(v_scaled, h + 1)
                for i in range(C - 1):
                    n = C - 1 - i
                    m = gram[:, LOW[i]:LOW[i] + n, :].unsqueeze(3).broadcast_to([P, n, CH, D])
                    tw = w_tmp[:, 0:n * CH * D].rearrange("p (r c e) -> p r c e", r=n, c=CH)
                    tu = u_tmp[:, 0:n * CH * D].rearrange("p (r c e) -> p r c e", r=n, c=CH)
                    own.step(v.tensor_tensor(tw, m, w4[:, i:i + 1, c0:c1].broadcast_to([P, n, CH, D]), ALU.mult))
                    own.step(v.tensor_tensor(tu, m, u4[:, i:i + 1, c0:c1].broadcast_to([P, n, CH, D]), ALU.mult))
                    dve.wait_ge(vec, own.n - 1)
                    own.step(v.tensor_tensor(w4[:, i + 1:C, c0:c1], w4[:, i + 1:C, c0:c1], tw, ALU.subtract))
                    dve.wait_ge(vec, own.n - 1)
                    ins = v.tensor_tensor(u4[:, i + 1:C, c0:c1], u4[:, i + 1:C, c0:c1], tu, ALU.subtract)
                    if i < C - 2:
                        own.link(ins)
                    else:
                        ins.then_inc(u_ready, 1)
                own.wait()
                dve.wait_ge(u_ready, h + 1)

            dve.wait_ge(kd_ready, NH)
            with dve.Fori(0, NC // (2 * RING)) as it:
                for k in range(2 * RING):
                    c = it * (2 * RING) + k
                    tok = bass.ds(it * (2 * RING * C) + k * C, C)
                    base = it * (8 * 2 * RING)

                    for a in range(2):
                        rows = slice(a * DL, (a + 1) * DL)
                        dve.wait_ge(scan, base + (8 * k + 1 + a))
                        v.tensor_tensor(
                            ws[:, k, :, rows, 0:D],
                            wx[:, tok, :].unsqueeze(2).broadcast_to([P, C, DL, D]),
                            states[:, bass.ds(c, 1), :].rearrange("p a (d e) -> p a d e", d=D)[:, :, rows, :]
                            .broadcast_to([P, C, DL, D]), ALU.mult).then_inc(scan, 1)
                    if k % RING == 0:
                        dve.wait_ge(ring_ready, it * 2 + (k // RING + 1))
                    for a in range(2):
                        rows = slice(a * DL, (a + 1) * DL)
                        dve.wait_ge(scan, base + (8 * k + 3 + a))
                        v.tensor_reduce(us[:, tok, rows], ws[:, k, :, rows, :], AX.X, ALU.add).then_inc(scan, 1)
                    for a in range(2):
                        rows = slice(a * DL, (a + 1) * DL)
                        dve.wait_ge(scan, base + (8 * k + 5 + a))
                        v.tensor_tensor(
                            outer[:, k % 2, a * DL * D:(a + 1) * DL * D, 0:C].rearrange("p (d e) i -> p d e i", d=DL),
                            kn[:, tok, :].rearrange("p i e -> p e i").unsqueeze(1).broadcast_to([P, DL, D, C]),
                            us[:, tok, rows].rearrange("p i d -> p d i").unsqueeze(2).broadcast_to([P, DL, D, C]),
                            ALU.mult).then_inc(scan, 1)
                    dve.wait_ge(carry_ready, it * (2 * RING) + (k + 1))
                    for a in range(2):
                        half = slice(a * DL * D, (a + 1) * DL * D)
                        dve.wait_ge(scan, base + (8 * k + 7 + a))
                        v.tensor_reduce(states[:, bass.ds(c + 1, 1), half].rearrange("p a n -> p (a n)"),
                                        outer[:, k % 2, half, :], AX.X, ALU.add).then_inc(scan, 1)

            dve.wait_ge(scan, 8 * NC + 2)
            dve.wait_ge(qg_ready, NH)
            dve.wait_ge(aq_ready, NH)
            for s in SLOTS_DVE:
                dve.wait_ge(slots_used, (NB - 2) * SLOTS + s + 1)
                out_product(v, slots, s, NB - 1, qn, states, us, aq_low, aq_diag, slots_dve)

            dve.wait_ge(og_sum, NB)
            dve.wait_ge(og_sq, NB)
            own.link(v.tensor_reduce(gn_s[:, 0:2], gn_part[:, :, :], AX.X, ALU.add))
            own.link(v.tensor_scalar(gn_s[:, 0:2], gn_s[:, 0:2], 1.0 / (S * D), None, ALU.mult))
            own.link(v.tensor_tensor(gn_s[:, 2:3], gn_s[:, 0:1], gn_s[:, 0:1], ALU.mult))
            v.scalar_tensor_tensor(gn_s[:, 3:4], gn_s[:, 1:2], GN_EPS, gn_s[:, 2:3], ALU.add,
                                   ALU.subtract).then_inc(gn_var, 1)
            dve.wait_ge(gn_rstd, 1)
            own.link(v.scalar_tensor_tensor(gn_s[:, 5:6], gn_s[:, 0:1], -1.0, gn_s[:, 4:5], ALU.mult, ALU.mult))
            dve.wait_ge(row_in, 2 * 16)
            dve.wait_ge(w_in, N_W * 16)
            for k in range(2):
                v.tensor_scalar(gn_rhs[:, k, :], b_mask[:, :], gn_s[:, 4 + k:5 + k], None, ALU.mult).then_inc(gn_ready, 1)
            dve.wait_ge(gn_psum, 1)
            ab = banks[:, 4, 0:2 * B].rearrange("p (k b) -> p k b", k=2)
            v.tensor_scalar(gn_ab[:, 0, :], ab[:, 0, :], gn_sb[:, 0:1], None, ALU.mult).then_inc(gn_coef, 1)
            v.tensor_scalar(gn_ab[:, 1, :], ab[:, 1, :], gn_sb[:, 0:1], gn_sb[:, 1:2], ALU.mult, ALU.add).then_inc(gn_coef, 1)
            dve.wait_ge(gate_ready, G)
            for b in range(B):
                dve.wait_ge(y_aff, b + 1)
                v.tensor_tensor(yT[:, b, :], yT[:, b, :], gateT[:, b, :], ALU.mult).then_inc(y_ready, 1)

            for g in range(G):
                dve.wait_ge(wo_psum, g + 1)
                attn = banks[:, 4 + g, :].rearrange("p (j f) -> p j f", j=TG)
                own.link(v.tensor_tensor(attn, attn, bo_all[:, :].unsqueeze(1).broadcast_to([P, TG, P]), ALU.add))
                statistics(g, lambda j: banks[:, 4 + g, j * P:(j + 1) * P])
                if g:
                    scale_shift(g - 1)
            scale_shift(G - 1)
            for g in range(G):
                tl = slice(g * TG, (g + 1) * TG)
                dve.wait_ge(ln_ready, (g + 1) * TG)
                v.tensor_tensor(x_all[:, tl, :], x_all[:, tl, :], xn[:, g % 2], ALU.add).then_inc(ln_used, 1)
                dve.wait_ge(ln_used, g + 1)
                moments(g, lambda j: x_all[:, g * TG + j, :])
                k = slice(g * TG, (g + 1) * TG)
                own.step(v.tensor_scalar(spread[:, 0, k], mv[:, k, 1], LN_EPS, None, ALU.add))
                own.wait()
                v.tensor_scalar(spread[:, 1, k], mv[:, k, 1], 1.0 + RMS_EPS, LN_EPS * RMS_EPS, ALU.mult,
                                ALU.add).then_inc(var_ready, 1)
            for g in range(G):
                await_root()
                for j in range(TG):
                    i = g * TG + j
                    v.tensor_scalar(nm[:, i, :], x_all[:, i, :], mv[:, i, 0:1], factor[:, 1, i:i + 1],
                                    ALU.subtract, ALU.mult).then_inc(xn_ready, 1)

            dve.wait_ge(logit_psum, 1)
            dve.wait_ge(const_ready, 7)
            lg = banks[:, 4, 0:T * NE].rearrange("p (i e) -> p i e", e=NE)
            bc = lambda k: r_s[:, k, :].unsqueeze(2).broadcast_to([P, T, NE])
            chosen = lambda k: onehot[:, :, :, k].rearrange("p e i -> p i e")
            for k, scores in ((0, lg), (1, r_b[:, :, :])):
                own.link(v.tensor_reduce(r_s[:, k, :], scores, AX.X, ALU.max))
                own.link(v.tensor_tensor(r_a[:, :, :], scores, bc(k), ALU.is_equal))
                own.link(v.tensor_tensor(r_a[:, :, :], r_a[:, :, :],
                                         ranks[:, :].unsqueeze(1).broadcast_to([P, T, NE]), ALU.mult))
                own.link(v.tensor_reduce(r_s[:, 4, :], r_a[:, :, :], AX.X, ALU.max))
                v.tensor_tensor(chosen(k), r_a[:, :, :], bc(4), ALU.is_equal).then_inc(onehot_ready, 1)
                dve.wait_ge(onehot_ready, k + 1)
                if k == 0:
                    own.link(v.scalar_tensor_tensor(r_b[:, :, :], chosen(0), -3e38, lg, ALU.mult, ALU.add))
            v.tensor_tensor(r_c[:, :, :], lg, bc(0), ALU.subtract).then_inc(exp_in, 1)
            v.tensor_tensor(r_s[:, 2, :], r_s[:, 1, :], r_s[:, 0, :], ALU.subtract).then_inc(exp_in, 1)
            flat = lambda a: a[:, :, :, :].rearrange("p e i k -> p (e i k)")
            dve.wait_ge(rank_psum, 1)
            prefix, total = banks[:, 5, 0:2 * P], banks[:, 6, 0:2 * P]
            own.link(v.tensor_tensor_scan(flat(incl), all_ones[:, :], total, 0.0, ALU.mult, ALU.add))
            own.link(v.tensor_tensor(flat(place), flat(incl), total, ALU.subtract))
            start, count, tiles, first, shift_e, last = (r_e[:, k, :] for k in range(6))
            own.step(v.tensor_copy(start, place[:, :, 0, 0]))
            own.step(v.tensor_tensor(count, incl[:, :, T - 1, 1], place[:, :, 0, 0], ALU.subtract))
            own.wait()
            own.step(v.tensor_tensor(flat(place), flat(place), prefix, ALU.add))
            own.link(v.tensor_scalar(tiles, count, 1.0 / P, (P - 1.0) / P - 0.5 + 0.5 / P, ALU.mult, ALU.add))
            own.link(v.tensor_scalar(tiles, tiles, ROUND, None, ALU.add))
            own.link(v.tensor_scalar(tiles, tiles, ROUND, None, ALU.subtract))
            own.link(v.tensor_tensor_scan(last, all_ones[:, 0:NE], tiles, 0.0, ALU.mult, ALU.add))
            own.link(v.tensor_tensor(first, last, tiles, ALU.subtract))
            own.link(v.scalar_tensor_tensor(shift_e, first, float(P), start, ALU.mult, ALU.subtract))
            own.link(v.tensor_tensor(place[:, :, :, :].rearrange("p e i k -> p e (i k)"),
                                     place[:, :, :, :].rearrange("p e i k -> p e (i k)"),
                                     shift_e.unsqueeze(2).broadcast_to([P, NE, 2 * T]), ALU.add))
            own.link(v.tensor_tensor(flat(place), flat(place), flat(onehot), ALU.mult))
            own.link(v.tensor_reduce(slot_f[:, :, :], place[:, :, :, :].rearrange("p e i k -> p i k e"), AX.X, ALU.add))
            flat_ik = lambda a: a[:, :, :].rearrange("p i k -> p (i k)")
            own.link(v.tensor_scalar(tile_of[:, :, :], slot_f[:, :, :], 1.0 / P, (1.0 - P) / (2 * P), ALU.mult, ALU.add))
            own.link(v.tensor_scalar(tile_of[:, :, :], tile_of[:, :, :], ROUND, None, ALU.add))
            own.link(v.tensor_scalar(tile_of[:, :, :], tile_of[:, :, :], ROUND, None, ALU.subtract))
            v.scalar_tensor_tensor(row_of[:, :, :], tile_of[:, :, :], -float(P), slot_f[:, :, :],
                                   ALU.mult, ALU.add).then_inc(at_ready, 2)
            dve.wait_ge(tables_ready, 3)
            dve.wait_ge(at_ready, 2)
            wide = [P, FT, NT]
            v.tensor_tensor(tile_one, tile_no[:, 0:NT].unsqueeze(1).broadcast_to(wide),
                            flat_ik(tile_of).unsqueeze(2).broadcast_to(wide), ALU.is_equal).then_inc(one_tile_ready, 1)
            for q in range(4):
                c0, c1 = q * FT // 4, (q + 1) * FT // 4
                v.tensor_tensor(row_hot[:, c0:c1, :], col_no[:, :].unsqueeze(1).broadcast_to([P, c1 - c0, P]),
                                flat_ik(row_of)[:, c0:c1].unsqueeze(2).broadcast_to([P, c1 - c0, P]),
                                ALU.is_equal).then_inc(row_hot_ready, 1)
                if q == 0:
                    dve.wait_ge(one_tile_ready, 1)
                    v.tensor_tensor(tile_hot[:, :, 1, :], tile_one, flat_ik(in_column).unsqueeze(2).broadcast_to(wide),
                                    ALU.mult).then_inc(tile_hot_ready, 1)
            dve.wait_ge(exp_done, 2)
            own.link(v.tensor_reduce(r_s[:, 5, :], r_p[:, :, :], AX.X, ALU.add))
            own.link(v.reciprocal(r_s[:, 5, :], r_s[:, 5, :]))
            own.link(v.tensor_tensor(r_s[:, 3, :], r_s[:, 3, :], r_s[:, 5, :], ALU.mult))
            own.link(v.tensor_tensor(r_s[:, 4, :], r_s[:, 5, :], r_s[:, 3, :], ALU.add))
            own.link(v.reciprocal(r_s[:, 4, :], r_s[:, 4, :]))
            own.link(v.tensor_scalar(alpha_sb[:, :], alpha_sb[:, :], -0.5, 2.0, ALU.max, ALU.min))
            own.link(v.tensor_scalar(r_s[:, 4, :], r_s[:, 4, :], alpha_sb[:, 0:1], None, ALU.mult))
            for k, probability in ((0, 5), (1, 3)):
                own.step(v.tensor_tensor(weight[:, :, k], r_s[:, probability, :], r_s[:, 4, :], ALU.mult))
            own.link(v.tensor_tensor(tile_cmp[:, :, :], tile_no[:, :].unsqueeze(2).broadcast_to([P, NT + 1, NE]),
                                     last.unsqueeze(1).broadcast_to([P, NT + 1, NE]), ALU.is_ge))
            own.link(v.tensor_reduce(tile_e[:, :], tile_cmp[:, :, :], AX.X, ALU.add))
            own.link(v.tensor_scalar(tile_e[:, :], tile_e[:, :], NE - 1.0, None, ALU.min))
            own.link(v.tensor_copy(tile_ei[:, :], tile_e[:, :]))

            def expert(j):
                return dve.value_load(tile_ei[0:1, bass.ds(j, 1)], min_val=0, max_val=NE - 1)

            dve.wait_ge(rows_psum, 1)
            v.tensor_copy(dest_f[:, :], banks[:, 7, 0:NT]).then_inc(number_ready, 1)
            dve.wait_ge(number_ready, 1)
            v.tensor_tensor(dest_f[:, :], dest_f[:, :], banks[:, 7, NT:2 * NT], ALU.add).then_inc(number_ready, 1)
            dve.wait_ge(number_ready, 2)
            own.link(v.tensor_scalar(src_f[:, :], dest_f[:, :], 0.5, -P - 0.25, ALU.mult, ALU.add))
            own.link(v.tensor_scalar(src_f[:, :], src_f[:, :], ROUND, None, ALU.add))
            own.link(v.tensor_scalar(src_f[:, :], src_f[:, :], ROUND, 0.0, ALU.subtract, ALU.max))
            v.tensor_copy(src[:, :], src_f[:, :]).then_inc(src_ready, 1)
            dve.wait_ge(src_ready, 1)
            own.link(v.scalar_tensor_tensor(src_f[:, :], dest_f[:, :], 0.0, past_no[:, :], ALU.is_equal, ALU.mult))
            own.link(v.scalar_tensor_tensor(dest_f[:, :], dest_f[:, :], -2.0 * P, src_f[:, :], ALU.add, ALU.add))
            v.tensor_copy(dest[:, :], dest_f[:, :]).then_inc(dest_ready, 1)

            def copy_gu(j, k, e):
                v.tensor_scalar(gu_cur[:, k, :], gu_w[:, bass.ds(e, 1), :].rearrange("p a n -> p (a n)"), 1.0, None,
                                ALU.mult).then_inc(gu_cur_ready, 1)

            def copy_down(j, k, e):
                v.tensor_scalar(down_cur[:, k].rearrange("p j n -> p (j n)"),
                                down_w[:, bass.ds(e, 1)].rearrange("p a j n -> p (a j n)"), 1.0, None,
                                ALU.mult).then_inc(down_cur_ready, 1)

            def hide(j, k):
                dve.wait_ge(gate_done, j + 1)
                v.tensor_tensor(hidden[:, k, :], hidden[:, k, :], banks[:, 3 + k, 0:3 * P], ALU.mult).then_inc(hid_ready, 1)

            dve.wait_ge(gu_in, 16)
            dve.wait_ge(down_in, 48)
            dve.wait_ge(qk_psum, NH)
            e0, e1 = expert(0), expert(1)
            copy_gu(0, 0, e0)
            copy_down(0, 0, e0)
            copy_gu(1, 1, e1)
            hide(0, 0)
            copy_gu(2, 0, expert(2))
            copy_down(1, 1, e1)
            with dve.Fori(0, (NT - 3) // 2) as it:
                for k in (1, 0):
                    j = it * 2 + (2 - k)
                    e_gu, e_down = expert(j + 2), expert(j + 1)
                    hide(j, k)
                    copy_gu(j + 2, k, e_gu)
                    dve.wait_ge(down_psum, j)
                    copy_down(j + 1, 1 - k, e_down)
            e_last = expert(NT - 1)
            hide(NT - 2, 1)
            dve.wait_ge(down_psum, NT - 2)
            copy_down(NT - 1, 0, e_last)
            hide(NT - 1, 0)

            dve.wait_ge(h_ready, T)
            for g in range(G):
                dve.wait_ge(y_back[g], 16)
                for k in range(2):
                    for j in range(TG):
                        i = g * TG + j
                        own.step(v.scalar_tensor_tensor(h_all[:, i, :], y_in[g][:, j, k, :], weight[:, i, k:k + 1],
                                                        h_all[:, i, :], ALU.mult, ALU.add))
                    own.wait()

            for g in range(G):
                statistics(g, lambda j: h_all[:, g * TG + j, :])
                if g:
                    scale_shift(g - 1)
            scale_shift(G - 1)
            for g in range(G):
                tl = slice(g * TG, (g + 1) * TG)
                dve.wait_ge(ln_ready, (G + g + 1) * TG)
                v.tensor_tensor(x_all[:, tl, :], x_all[:, tl, :], nm_all[:, tl, :], ALU.add).then_inc(result_ready, 1)

        @block.tensor
        def _(pe):
            mm = nc.tensor.matmul
            pe.wait_ge(const_ready, 2)

            def transpose(g):
                pe.wait_ge(xn_ready, (g + 1) * TG)
                if g:
                    pe.wait_ge(xnT_ready, g)
                for j in range(TG):
                    ins = nc.tensor.transpose(banks[:, 0, j * P:(j + 1) * P], xn[:, g % 2, j, :], ident[:, :])
                ins.then_inc(xT_psum, 1)

            def sum_qk(h):
                pe.wait_ge(qk_ready, C * (h + 1))
                if h:
                    pe.wait_ge(aq_moved, 2 * h)
                for m0, m1, bank in ((0, NLOW, 6), (NLOW, NLOW + C, 7)):
                    for e in range(D):
                        ins = mm(banks[:, bank, 0:(m1 - m0) * CH], ident[:, :], qk[:, m0:m1, :, e],
                                 start=(e == 0), stop=(e == D - 1))
                ins.then_inc(qk_psum, 1)

            transpose(0)
            for g in range(G):
                h, b0 = group(g)
                pe.wait_ge(xnT_ready, g + 1)
                for w in range(3):
                    if w == 1 and g + 1 < G:
                        transpose(g + 1)
                    pe.wait_ge(tap_ready, w + 1)
                    if g:
                        pe.wait_ge(silu_ready, 3 * (g - 1) + w + 1)
                    for k in range(KW):
                        ins = mm(banks[:, 1 + w, :], w_tap[:, w, k, :],
                                 x_pad[:, b0:b0 + TG, k + h * SH:k + (h + 1) * SH], start=(k == 0), stop=(k == KW - 1))
                    ins.then_inc(proj_psum, 1)
                rhs = x_pad[:, b0:b0 + TG, KW - 1 + h * SH:KW - 1 + (h + 1) * SH]
                if g == 0:
                    pe.wait_ge(w_early, N_EARLY * 16)
                else:
                    pe.wait_ge(ab_moved, g)
                mm(banks[0:2 * H, 5, :], w_ab[:, :], rhs, start=True, stop=True).then_inc(proj_psum, 1)
            def sum_gram(h):
                for i0, i1 in ((0, 1), (1, 2), (2, C - 1)):
                    pe.wait_ge(kk_ready, h * (C - 1) + i1)
                    m0, m1 = LOW[i0], LOW[i1 - 1] + C - i1
                    for e in range(D):
                        ins = mm(banks[:, 0, m0 * CH:m1 * CH], ident[:, :], kk[:, m0:m1, :, e],
                                 start=(e == 0), stop=(e == D - 1))
                ins.then_inc(gram_psum, 1)

            pe.wait_ge(xnT_ready, G)
            sum_gram(0)
            for g in range(G):
                h, b0 = group(g)
                if g < 2:
                    pe.wait_ge(ab_moved, G)
                else:
                    pe.wait_ge(gate_ready, g - 1)
                mm(banks[:, 4 + g % 2, :], w_proj[:, 3, :],
                   x_pad[:, b0:b0 + TG, KW - 1 + h * SH:KW - 1 + (h + 1) * SH], start=True, stop=True).then_inc(gate_psum, 1)
            pe.wait_ge(sq_ready, NH)
            pe.wait_ge(silu_ready, 3 * G)
            for d in range(D):
                ins = mm(banks[:, 3, 0:2 * SH], ident[:, :],
                         square.rearrange("p (w d t) -> p w d t", w=2, d=D)[:, :, d, :], start=(d == 0), stop=(d == D - 1))
            ins.then_inc(ss_ready, 1)
            sum_qk(0)
            pe.wait_ge(gram_used, 1)
            sum_gram(1)
            sum_qk(1)
            pe.wait_ge(silu_ready, 3 * G)
            pe.wait_ge(xnT_ready, G)
            pe.wait_ge(gate_ready, G)
            pe.wait_ge(ab_moved, G)
            pe.wait_ge(aq_moved, 2 * NH)
            pe.wait_ge(gram_used, NH)
            pe.wait_ge(root_ready, NH)
            by_pool, by_dve = 0, 0
            for n in range(NB):
                for s in range(SLOTS):
                    if n == NB - 1 and s in SLOTS_DVE:
                        by_dve += products(s)
                        pe.wait_ge(slots_dve, by_dve)
                    else:
                        by_pool += products(s)
                        pe.wait_ge(slots_pool, by_pool)
                    mm(banks[:, n, 0:DB * D], ident[:, :], slots[:, s].rearrange("p t d -> p (t d)"),
                       start=(s == 0), stop=(s == SLOTS - 1)).then_inc(slots_used, 1)
            pe.wait_ge(gn_ready, 2)
            pe.wait_ge(gate_ready, G)
            mm(banks[:, 4, 0:2 * B], h_mask[:, :], gn_rhs[:, :, :].rearrange("p k b -> p (k b)"),
               start=True, stop=True).then_inc(gn_psum, 1)
            pe.wait_ge(ab_moved, G)
            pe.wait_ge(aq_moved, 2 * NH)
            pe.wait_ge(gn_coef, 2)
            pe.wait_ge(w_in, N_W * 16)
            for g in range(G):
                for j in range(TG):
                    i = g * TG + j
                    pe.wait_ge(y_ready, i // NH + 1)
                    dst = banks[:, 4 + g, j * P:(j + 1) * P]
                    ins = mm(dst, yT[:, i // NH, (i % NH) * P:(i % NH + 1) * P], w_o[:, :], start=True, stop=True)
                ins.then_inc(wo_psum, 1)
            for g in range(G):
                pe.wait_ge(xn_ready, (G + g + 1) * TG)
                for j in range(TG):
                    ins = nc.tensor.transpose(banks[:, g, j * P:(j + 1) * P], nm[:, g * TG + j, :], ident[:, :])
                ins.then_inc(xT_psum, 1)
            pe.wait_ge(xnT_ready, 2 * G)
            for i in range(T):
                ins = mm(banks[:, 4, i * NE:(i + 1) * NE], xnT[:, i * P:(i + 1) * P], w_router[:, :], start=True, stop=True)
            ins.then_inc(logit_psum, 1)
            pe.wait_ge(onehot_ready, 2)
            pe.wait_ge(const_ready, 7)
            oh = onehot[:, :, :, :].rearrange("p e i k -> p (e i k)")
            mm(banks[:, 5, 0:2 * P], l_tri[:, :], oh, start=True, stop=True)
            mm(banks[:, 6, 0:2 * P], ones_16[:, :], oh, start=True, stop=True).then_inc(rank_psum, 1)
            pe.wait_ge(exp_in, 1)
            for k in range(2):
                for bank in (1 + k, 3 + k):
                    mm(banks[:, bank, 0:3 * P], zeros[:, :], ident[:, 0:1].broadcast_to([P, 3 * P]), start=True, stop=True)
            pe.wait_ge(tile_hot_ready, 1)
            pe.wait_ge(numbers_ready, 1)
            for c in range(FT):
                if c % (FT // 4) == 0:
                    pe.wait_ge(row_hot_ready, c // (FT // 4) + 1)
                ins = mm(banks[:, 7, 0:2 * NT], row_hot[:, c, :], tile_hot[:, c].rearrange("p w t -> p (w t)"),
                         start=(c == 0), stop=(c == FT - 1))
            ins.then_inc(rows_psum, 1)

            def turn(j, k, slot, loads, first=False):
                pe.wait_ge(xg_in[slot], loads)
                if not first:
                    pe.wait_ge(xgT_ready, j - 1)
                nc.tensor.transpose(banks[:, 7 * k, 0:P], xg[:, slot, :], ident[:, :]).then_inc(xgT_psum, 1)

            def gate_up(j, k, first=False):
                pe.wait_ge(gu_cur_ready, j + 1)
                pe.wait_ge(xgT_ready, j + 1)
                if not first:
                    pe.wait_ge(hid_ready, j - 1)
                rhs = xgT[:, k, :]
                for bank, at in ((1 + k, 0), (3 + k, HID)):
                    for q, (h0, m) in enumerate(HC):
                        ins = mm(banks[0:m, bank, q * P:(q + 1) * P], gu_cur[:, k, at + h0:at + h0 + m], rhs,
                                 start=True, stop=True)
                ins.then_inc(gu_psum, 1)

            def down(j, k, first=False):
                pe.wait_ge(down_cur_ready, j + 1)
                pe.wait_ge(hid_ready, j + 1)
                if not first:
                    pe.wait_ge(y_sb_ready, j - 1)
                for q, (_, m) in enumerate(HC):
                    ins = mm(banks[:, 5 + k, 0:P], hidden[0:m, k, q * P:(q + 1) * P], down_cur[0:m, k, q, :],
                             start=(q == 0), stop=(q == 2))
                ins.then_inc(down_psum, 1)

            pe.wait_ge(number_ready, 2)
            turn(0, 0, 0, 16, True)
            turn(1, 1, 1, 16, True)
            gate_up(0, 0, True)
            turn(2, 0, 2, 16)
            gate_up(1, 1, True)
            down(0, 0, True)
            turn(3, 1, 3, 16)
            gate_up(2, 0)
            down(1, 1, True)
            with pe.Fori(0, (NT - 3) // RG) as it:
                for q in range(RG):
                    j, k = it * RG + (3 + q), (3 + q) % 2
                    turn(j + 1, 1 - k, (4 + q) % RG, it * 16 + ((4 + q) // RG + 1) * 16)
                    gate_up(j, k)
                    down(j - 1, 1 - k)
            for j in range(3 + (NT - 3) // RG * RG, NT):
                if j + 1 < NT:
                    turn(j + 1, (j + 1) % 2, (j + 1) % RG, 16 * ((j + 1) // RG + 1))
                gate_up(j, j % 2)
                down(j - 1, (j - 1) % 2)
            down(NT - 1, 0)


_INS = ['L0_attn_x', 'L0_attn_Wq', 'L0_attn_bq', 'L0_attn_Wk', 'L0_attn_bk', 'L0_attn_Wv', 'L0_attn_bv',
        'L0_attn_q_conv', 'L0_attn_k_conv', 'L0_attn_v_conv', 'L0_attn_Wa', 'L0_attn_ba', 'L0_attn_Wb', 'L0_attn_bb',
        'L0_attn_Wg', 'L0_attn_bg', 'L0_attn_gn_scale', 'L0_attn_gn_bias', 'L0_attn_Wo', 'L0_attn_bo',
        'L0_ffn_norm_weight', 'L0_ffn_router_weight', 'L0_ffn_gate_up_weight', 'L0_ffn_down_weight',
        'L0_ffn_residual_alpha']


def kernel(**inputs):
    import numpy as _np
    import concourse.bacc as _bacc
    from concourse import mybir as _mybir
    from concourse.bass_utils import run_bass_kernel_spmd as _run

    nc = _bacc.Bacc("TRN2", target_bir_lowering=False, num_devices=1)
    laid = {n: _np.asarray(inputs[n]) for n in _INS}
    laid['L0_attn_x'] = laid['L0_attn_x'].reshape(B * S, P)
    laid['L0_ffn_router_weight'] = laid['L0_ffn_router_weight'].T
    laid['L0_ffn_gate_up_weight'] = laid['L0_ffn_gate_up_weight'].transpose(2, 0, 1)
    laid['L0_ffn_down_weight'] = laid['L0_ffn_down_weight'].transpose(0, 2, 1)
    laid['L0_ffn_residual_alpha'] = laid['L0_ffn_residual_alpha'].reshape(1)
    arrays, args = {}, []
    for name in _INS:
        a = _np.ascontiguousarray(laid[name])
        arrays[f"in_{name}_dram"] = a
        args.append(nc.dram_tensor(f"in_{name}_dram", a.shape, _mybir.dt.from_np(a.dtype), kind="ExternalInput").ap())
    bh = _np.arange(P)
    masks = {"conv_rows": _np.ascontiguousarray(_np.stack(
                 [_np.asarray(inputs[f'L0_attn_{n}_conv']).T for n in 'qkv'])),
             "head_mask": (bh[:, None] % H == bh[None, :] // D).astype(_np.float32),
             "batch_mask": (bh[:, None] // H == _np.arange(B)[None, :]).astype(_np.float32)}
    for name, a in masks.items():
        arrays[f"in_{name}_dram"] = a
        args.append(nc.dram_tensor(f"in_{name}_dram", a.shape, _mybir.dt.from_np(a.dtype), kind="ExternalInput").ap())
    res = nc.dram_tensor("out_0_dram", (B * S, P), F32, kind="ExternalOutput").ap()
    build(nc, *args, res)
    r = _run(nc, [arrays], core_ids=[0])
    return r.results[0]["out_0_dram"].reshape(B, S, P)
```

```python
import concourse.bass as bass
from concourse import mybir
from contextlib import ExitStack

F32 = mybir.dt.float32
I32 = mybir.dt.int32
BF16 = mybir.dt.bfloat16
ALU = mybir.AluOpType
ACT = mybir.ActivationFunctionType
AX = mybir.AxisListType

P = 128
B, S = 8, 256
H, D = 16, 8
NE, HID = 8, 352
C = 8
NH = 2
SH = S // NH
CH = SH // C
NC = S // C
T = B * S // P
G = 4
TG = T // G
N = TG * P
KW = 4
PAD = S + KW - 1
LN_EPS, GN_EPS, RMS_EPS, QK_EPS = 1e-5, 1e-5, 1e-6, 1e-6
HC = [(0, 128), (128, 128), (256, 96)]
NLOW = C * (C - 1) // 2
LOW = [sum(C - 1 - k for k in range(i)) for i in range(C)]
DB = 32
NB = S // DB
CB = DB // C
SLOTS = D + C
RING = 4
NU = [4, CH]
WU = sum(1 + (nu < CH) for nu in NU)
DL = D // 2
ROUND = 1.5 * 2 ** 23
NT = (B * S * 2 + NE * (P - 1)) // P
RG = 8
PAIRS = [(1, 2), (3, 5), (7, 8), (9, 10), (11, 12)]
SLOTS_DVE = [s for pair in PAIRS for s in pair]


Q, K, V, AB = range(4)
ORDER = [(g, w) for h in range(NH) for g, w in (
    (2 * h, Q), (2 * h, K), (2 * h + 1, Q), (2 * h + 1, K), (2 * h, AB), (2 * h + 1, AB), (2 * h, V), (2 * h + 1, V))]
CONVOLVED = [p for p in ORDER if p[1] != AB]


def nth(p):
    return ORDER.index(p) + 1


def bank_of(g, w):
    return 4 if w == V and g % 2 else 1 + w


def nth_convolved(p):
    return CONVOLVED.index(p) + 1


class Steps:

    def __init__(self, eng, sem):
        self.eng, self.sem, self.n = eng, sem, 0

    def step(self, ins):
        ins.then_inc(self.sem, 1)
        self.n = self.n + 1

    def link(self, ins):
        self.step(ins)
        self.eng.wait_ge(self.sem, self.n)

    def wait(self):
        self.eng.wait_ge(self.sem, self.n)


def group(g):
    return g // 2, TG * (g % 2)


def out_product(eng, slots, s, n, qn, states, us, aq_low, aq_diag, signal):
    dst = slots[:, s].rearrange("p (c r) d -> p r c d", r=C)
    c0, c1 = n * CB, (n + 1) * CB
    if s < D:
        eng.tensor_tensor(
            slots[:, s].rearrange("p (c r) d -> p c r d", r=C),
            states[:, c0:c1, :].rearrange("p c (d e) -> p c d e", d=D)[:, :, :, s].unsqueeze(2).broadcast_to([P, CB, C, D]),
            qn[:, n * DB:(n + 1) * DB, s:s + 1].rearrange("p (c r) a -> p c r a", r=C).broadcast_to([P, CB, C, D]),
            ALU.mult).then_inc(signal, 1)
        return
    i = s - D
    u = us[:, n * DB:(n + 1) * DB, :].rearrange("p (c r) d -> p r c d", r=C)
    eng.tensor_tensor(dst[:, i], u[:, i], aq_diag[:, i, c0:c1].unsqueeze(2).broadcast_to([P, CB, D]),
                      ALU.mult).then_inc(signal, 1)
    if i < C - 1:
        m = C - 1 - i
        eng.tensor_tensor(dst[:, i + 1:C], u[:, i:i + 1].broadcast_to([P, m, CB, D]),
                          aq_low[:, LOW[i]:LOW[i] + m, c0:c1].unsqueeze(3).broadcast_to([P, m, CB, D]),
                          ALU.mult).then_inc(signal, 1)


def products(s):
    return 2 if D <= s < SLOTS - 1 else 1


def build(nc, x, Wq, bq, Wk, bk, Wv, bv, q_conv, k_conv, v_conv, Wa, ba, Wb, bb, Wg, bg,
          gn_scale, gn_bias, Wo, bo, norm_w, router_t, gu_t, down_t, res_alpha, conv_rows, head_mask, batch_mask, out):
    ctx = ExitStack()
    with ctx:
        def sb(name, shape):
            return ctx.enter_context(nc.sbuf_tensor(name, shape, F32))

        def sem(name):
            return ctx.enter_context(nc.semaphore(name))

        qkv_d = nc.dram_tensor("qkv_scratch", [NH, 3, B, P, SH], F32, kind="Internal").ap()
        ab_d = nc.dram_tensor("ab_scratch", [NH, 2, B, H, SH], F32, kind="Internal").ap()
        o_d = nc.dram_tensor("o_scratch", [NB, B, P, DB], F32, kind="Internal").ap()

        nm_d = nc.dram_tensor("expert_inputs", [B * S, P], F32, kind="Internal").ap()
        y_d = nc.dram_tensor("expert_rows", [2 * B * S + NT * P, P], F32, kind="Internal").ap()

        w_proj = sb("w_proj", [P, 4, P])
        w_tap = sb("w_tap", [P, 3, KW, P])
        w_ab = sb("w_ab", [P, 2 * H])
        w_o = sb("w_o", [P, P])
        w_router = sb("w_router", [P, NE])
        conv_w = sb("conv_w", [P, 3, KW])
        conv_b = sb("conv_b", [P, 3, KW])
        bias_qkvg = sb("bias_qkvg", [P, 4])
        bias_ab = sb("bias_ab", [2 * H, 1])
        gn_sb = sb("gn_sb", [P, 2])
        normw_sb = sb("normw_sb", [P, 1])
        alpha_sb = sb("alpha_sb", [P, 1])
        bo_row = sb("bo_row", [1, P])
        zeros = sb("zeros", [P, P])
        ident = sb("ident", [P, P])
        h_mask = sb("h_mask", [P, P])
        b_mask = sb("b_mask", [P, B])
        mhalf = sb("mhalf", [P, TG])
        ranks = sb("ranks", [P, NE])

        x_all = sb("x_all", [P, T, P])
        x_bh = x_all[:, :, :].rearrange("p (b h) f -> p b h f", h=NH)
        xn = sb("xn", [P, 2, TG, P])
        x_pad = sb("x_pad", [P, B, PAD])
        gateT = sb("gateT", [P, B, S])
        qs = sb("qs", [P, 2, 3, TG, P])
        ab_sb = sb("ab_sb", [2 * H, B, SH])
        raw = sb("raw", [P, NH, 3, D, SH])
        ab_bh = sb("ab_bh", [P, NH, 2, SH])
        kn = sb("kn", [P, S, D])
        qn = sb("qn", [P, S, D])
        wx = sb("wx", [P, S, D])
        us = sb("us", [P, S, D])
        ring = sb("ring", [P, 2 * RING * C * D * (D + 1)])
        ws = ring[:, :].rearrange("p (c r d e) -> p c r d e", c=2 * RING, r=C, d=D)
        states = sb("states", [P, NC + 1, D * D])
        outer = sb("outer", [P, 2, D * D, C + 1])
        slots_buf = sb("slots_buf", [P, 8192])
        slots = slots_buf[:, 0:SLOTS * DB * D].rearrange("p (s t d) -> p s t d", s=SLOTS, t=DB)
        ss = sb("ss", [P, 2, SH])
        rn = sb("rn", [P, 2, SH])
        gram = sb("gram", [P, NH, NLOW, CH])
        aq_low = sb("aq_low", [P, NLOW, NC])
        aq_diag = sb("aq_diag", [P, C, NC])
        dec = sb("dec", [P, NLOW, NC])
        gc = sb("gc", [P, C, NC])
        gc_neg = sb("gc_neg", [P, C, CH])
        tail = sb("tail", [P, C - 1, CH])
        stats = sb("stats", [P, T, 6])
        mv = sb("mv", [P, T, 2])
        rstd = sb("rstd", [P, T])
        shift = sb("shift", [P, T])
        spread = sb("spread", [P, 2, T])
        factor = sb("factor", [P, 2, T])
        gn_part = sb("gn_part", [P, 2, NB])
        gn_s = sb("gn_s", [P, 8])
        gn_rhs = sb("gn_rhs", [P, 2, B])
        gn_ab = sb("gn_ab", [P, 2, B])
        l_tri = ctx.enter_context(nc.sbuf_tensor("l_tri", [P, P], BF16))
        all_ones = sb("all_ones", [P, 2 * P])
        ones_16 = ctx.enter_context(nc.sbuf_tensor("ones_16", [P, P], BF16))
        col_no = sb("col_no", [P, P])
        column_no = sb("column_no", [P, T, 2])
        in_column = sb("in_column", [P, T, 2])
        past_no = sb("past_no", [P, NT])
        tile_e = sb("tile_e", [P, NT + 1])
        tile_no = col_no[:, 0:NT + 1]
        tile_cmp = sb("tile_cmp", [P, NT + 1, NE])
        onehot = ctx.enter_context(nc.sbuf_tensor("onehot", [P, NE, T, 2], BF16))
        incl = sb("incl", [P, NE, T, 2])
        place = sb("place", [P, NE, T, 2])
        r_e = sb("r_e", [P, 6, NE])
        weight = sb("weight", [P, T, 2])
        slot_f = sb("slot_f", [P, T, 2])
        tile_ei = ctx.enter_context(nc.sbuf_tensor("tile_ei", [P, NT + 1], I32))
        col_16 = ctx.enter_context(nc.sbuf_tensor("col_16", [P, P], BF16))
        in_column_16 = ctx.enter_context(nc.sbuf_tensor("in_column_16", [P, T, 2], BF16))
        tile_of_16 = ctx.enter_context(nc.sbuf_tensor("tile_of_16", [P, T, 2], BF16))
        row_of_16 = ctx.enter_context(nc.sbuf_tensor("row_of_16", [P, T, 2], BF16))
        tile_of = sb("tile_of", [P, T, 2])
        dest_f = sb("dest_f", [P, NT])
        src_f = sb("src_f", [P, NT])
        dest = ctx.enter_context(nc.sbuf_tensor("dest", [P, NT], I32))
        src = ctx.enter_context(nc.sbuf_tensor("src", [P, NT], I32))
        r_a = sb("r_a", [P, T, NE])
        r_b = sb("r_b", [P, T, NE])
        r_c = sb("r_c", [P, T, NE])
        r_p = sb("r_p", [P, T, NE])
        r_s = sb("r_s", [P, 6, T])

        conv_r = slots_buf[:, 0:3 * KW * P].rearrange("p (w k f) -> p w k f", w=3, k=KW)
        QK = (NLOW + C) * CH * D
        square = slots_buf[:, QK:QK + 2 * D * SH]
        kk = ring[:, 0:NLOW * CH * D].rearrange("p (m c e) -> p m c e", m=NLOW, c=CH)
        TMP = (C - 1) * CH * D
        w_tmp, u_tmp = ring[:, 0:TMP], ring[:, TMP:2 * TMP]
        u_tmp_pool = slots_buf[:, QK + 2 * D * SH:QK + 2 * D * SH + (C - 1) * max(NU) * D]
        qk = slots_buf[:, 0:QK].rearrange("p (m c e) -> p m c e", m=NLOW + C, c=CH)
        og = qs[:, :, :, :, :].rearrange("p a w j t -> p (a w j t)")[:, 0:S * D].rearrange(
            "p (n d t) -> p n d t", n=NB, d=D)
        sq_dump = xn[:, :, :, :].rearrange("p a j t -> p a (j t)")
        gu_w = raw[:, :, :, :, :].rearrange("p a w d t -> p (a w d t)")[:, 0:NE * 2 * HID].rearrange("p (e n) -> p e n", e=NE)
        down_w = ring[:, 0:NE * 3 * P].rearrange("p (e j n) -> p e j n", e=NE, j=3)
        gT = slots_buf[:, SLOTS * DB * D:SLOTS * DB * D + B * S].rearrange("p (n b t) -> p n b t", n=NB, b=B)
        yT = wx[:, :, :].rearrange("p t d -> p (t d)").rearrange("p (b t) -> p b t", b=B)
        h_all = kn[:, :, :].rearrange("p t d -> p (t d)").rearrange("p (i f) -> p i f", i=T)
        nm = qs[:, :, :, :, :].rearrange("p a w j t -> p (a w j t)")[:, 0:T * P].rearrange("p (i f) -> p i f", i=T)
        nm_all = us[:, :, :].rearrange("p t d -> p (t d)").rearrange("p (i f) -> p i f", i=T)
        xnT = qn[:, :, :].rearrange("p t d -> p (t d)")
        GU = 2 * HID
        FT = 2 * T
        row_hot = slots_buf[:, 0:FT * P // 2].bitcast(BF16).rearrange("p (c r) -> p c r", c=FT)
        tile_hot = slots_buf[:, FT * P // 2:FT * (P // 2 + NT)].bitcast(BF16).rearrange("p (c w t) -> p c w t", c=FT, w=2)
        tile_one = slots_buf[:, FT * (P // 2 + NT):FT * (P // 2 + 2 * NT)].bitcast(BF16)[:, 0:FT * NT].rearrange(
            "p (c t) -> p c t", c=FT)
        o1 = FT * (P // 2 + 2 * NT)
        hidden = slots_buf[:, o1:o1 + 6 * P].rearrange("p (k n) -> p k n", k=2)
        states_flat = states[:, :, :].rearrange("p c f -> p (c f)")
        xgT = states_flat[:, 0:2 * P].rearrange("p (k n) -> p k n", k=2)
        gu_cur = states_flat[:, 2 * P:2 * P + 2 * GU].rearrange("p (k n) -> p k n", k=2)
        down_cur = wx[:, :, :].rearrange("p t d -> p (t d)")[:, 0:6 * P].rearrange("p (k j n) -> p k j n", k=2, j=3)
        y_sb = wx[:, :, :].rearrange("p t d -> p (t d)")[:, 6 * P:8 * P].rearrange("p (k n) -> p k n", k=2)
        xg = us[:, :, :].rearrange("p t d -> p (t d)")[:, 0:RG * P].rearrange("p (k f) -> p k f", k=RG)
        y_in = [m.rearrange("p (j k f) -> p j k f", j=TG, k=2) for m in (
            gateT[:, :, :].rearrange("p b t -> p (b t)")[:, 0:2 * N], gateT[:, :, :].rearrange("p b t -> p (b t)")[:, 2 * N:4 * N],
            xnT[:, 0:2 * N], xnT[:, 2 * N:4 * N])]

        banks = ctx.enter_context(nc.psum_tensor("banks", [P, 8, N], F32))

        x_in = [sem(f"x_in{g}") for g in range(G)]
        w_conv, w_bias = sem("w_conv"), sem("w_bias")
        w_early, w_in, row_in = sem("w_early"), sem("w_in"), sem("row_in")
        gu_in, down_in = sem("gu_in"), sem("down_in")
        qk_out = [sem(f"qk_out{h}") for h in range(NH)]
        v_out = [sem(f"v_out{h}") for h in range(NH)]
        ab_out = [sem(f"ab_out{h}") for h in range(NH)]
        raw_in = [sem(f"raw_in{h}") for h in range(NH)]
        v_in = [sem(f"v_in{h}") for h in range(NH)]
        ab_in = [sem(f"ab_in{h}") for h in range(NH)]
        og_out = [sem(f"og_out{n}") for n in range(NB)]
        gT_in = sem("gT_in")
        out_done = sem("out_done")
        vec, pool_s = sem("vec_steps"), sem("pool_steps")
        const_ready, tap_ready, biases_ready = sem("const_ready"), sem("tap_ready"), sem("biases_ready")
        var_ready, rstd_ready = sem("var_ready"), sem("rstd_ready")
        xn_ready, xT_psum, xnT_ready = sem("xn_ready"), sem("xT_psum"), sem("xnT_ready")
        proj_psum, edge_ready, silu_ready = sem("proj_psum"), sem("edge_ready"), sem("silu_ready")
        gate_psum, gram_psum, kk_ready = sem("gate_psum"), sem("gram_psum"), sem("kk_ready")
        v_scaled, gram_used = sem("v_scaled"), sem("gram_used")
        gate_ready, ab_moved, ab_sig = sem("gate_ready"), sem("ab_moved"), sem("ab_sig")
        sq_ready, ss_ready, root_ready = sem("sq_ready"), sem("ss_ready"), sem("root_ready")
        kq_ready = sem("kq_ready")
        decay_ready, kd_ready, qg_ready = sem("decay_ready"), sem("kd_ready"), sem("qg_ready")
        qk_ready, qk_psum, aq_moved = sem("qk_ready"), sem("qk_psum"), sem("aq_moved")
        wu_ready, u_pool, gram_head = sem("wu_ready"), sem("u_pool"), sem("gram_head")
        aq_ready, ln_used = sem("aq_ready"), sem("ln_used")
        ring_ready, carry_ready, scan = sem("ring_ready"), sem("carry_ready"), sem("scan_steps")
        slots_pool, slots_dve, slots_used = sem("slots_pool"), sem("slots_dve"), sem("slots_used")
        pair_ready = sem("pair_ready")
        og_sum, og_sq = sem("og_sum"), sem("og_sq")
        gn_var, gn_rstd, gn_ready, gn_psum, gn_coef = (sem("gn_var"), sem("gn_rstd"), sem("gn_ready"), sem("gn_psum"),
                                                       sem("gn_coef"))
        y_aff, y_ready, wo_psum = sem("y_aff"), sem("y_ready"), sem("wo_psum")
        shift_ready, ln_ready = sem("shift_ready"), sem("ln_ready")
        spread_ready, factor_ready = sem("spread_ready"), sem("factor_ready")
        h_factor_ready, h_ready = sem("h_factor_ready"), sem("h_ready")
        logit_psum, exp_in, exp_done = sem("logit_psum"), sem("exp_in"), sem("exp_done")
        onehot_ready, rank_psum, tables_ready = sem("onehot_ready"), sem("rank_psum"), sem("tables_ready")
        nm_out, at_ready, tile_hot_ready = sem("nm_out"), sem("at_ready"), sem("tile_hot_ready")
        tables_16 = sem("tables_16")
        one_tile_ready, numbers_ready = sem("one_tile_ready"), sem("numbers_ready")
        row_hot_ready, rows_psum = sem("row_hot_ready"), sem("rows_psum")
        src_ready, dest_ready, number_ready = sem("src_ready"), sem("dest_ready"), sem("number_ready")
        xg_in = [sem(f"xg_in{k}") for k in range(RG)]
        xgT_psum, xgT_ready = sem("xgT_psum"), sem("xgT_ready")
        gu_cur_ready, down_cur_ready = sem("gu_cur_ready"), sem("down_cur_ready")
        gu_psum, gate_done, hid_ready = sem("gu_psum"), sem("gate_done"), sem("hid_ready")
        down_psum, y_sb_ready = sem("down_psum"), sem("y_sb_ready")
        y_out = [sem(f"y_out{k}") for k in range(2)]
        y_back = [sem(f"y_back{g}") for g in range(G)]
        result_ready, weight_ready = sem("result_ready"), sem("weight_ready")
        last_result_ready = sem("last_result_ready")
        first_scaled, first_added = sem("first_scaled"), sem("first_added")

        block = ctx.enter_context(nc.Block())
        N_CONV, N_BIAS, N_EARLY, N_W = 4, 9, 3, 7

        x_v = x.rearrange("(b h p) f -> h p b f", h=NH, p=P)

        @block.sync
        def _(sp):
            for g in range(G):
                h, b0 = group(g)
                sp.dma_start(x_bh[:, b0:b0 + TG, h, :], x_v[h, :, b0:b0 + TG, :]).then_inc(x_in[g], 16)
                if g == 0:
                    sp.dma_start(conv_r, conv_rows.partition_broadcast(P)).then_inc(w_conv, 16)
                    for i, w in enumerate((Wq, Wk, Wv)):
                        sp.dma_start(w_proj[:, i, :], w).then_inc(w_conv, 16)
                if g == 1:
                    sp.dma_start(w_proj[:, 3, :], Wg).then_inc(w_early, 16)
                    sp.dma_start(w_ab[:, 0:H], Wa).then_inc(w_early, 16)
                    sp.dma_start(w_ab[:, H:2 * H], Wb).then_inc(w_early, 16)
            col = lambda v: v.rearrange("(p a) -> p a", a=1)
            sp.dma_start(gn_sb[:, 0:1], col(gn_scale)).then_inc(w_in, 16)
            sp.dma_start(gn_sb[:, 1:2], col(gn_bias)).then_inc(w_in, 16)
            sp.dma_start(w_o[:, :], Wo).then_inc(w_in, 16)
            sp.dma_start(normw_sb[:, :], col(norm_w)).then_inc(w_in, 16)
            sp.dma_start(w_router[:, :], router_t).then_inc(w_in, 16)
            sp.dma_start(bo_row[:, :], bo.unsqueeze(0)).then_inc(w_in, 16)
            sp.dma_start(alpha_sb[:, :], res_alpha.partition_broadcast(P)).then_inc(w_in, 16)
            sp.dma_start(h_mask[:, :], head_mask).then_inc(row_in, 16)
            sp.dma_start(b_mask[:, :], batch_mask).then_inc(row_in, 16)
            for g, w in CONVOLVED:
                h, b0 = group(g)
                sp.wait_ge(silu_ready, nth_convolved((g, w)))
                signal = v_out if w == V else qk_out
                sp.dma_start(qkv_d[h, w, b0:b0 + TG].rearrange("b p t -> p b t"), qs[:, g % 2, w, :, :]
                             ).then_inc(signal[h], 16)
                if g % 2 and w == K:
                    sp.wait_ge(qk_out[h], 4 * 16)
                    for u in (Q, K):
                        sp.dma_start(raw[:, h, u, :, :], qkv_d[h, u].rearrange("b (h d) t -> (b h) d t", h=H)
                                     ).then_inc(raw_in[h], 16)
                if g % 2 and w == V:
                    sp.wait_ge(v_out[h], 2 * 16)
                    sp.dma_start(raw[:, h, 2, :, :], qkv_d[h, 2].rearrange("b (h d) t -> (b h) d t", h=H)
                                 ).then_inc(v_in[h], 16)
            sp.wait_ge(wu_ready, WU)
            sp.dma_start(gu_w, gu_t).then_inc(gu_in, 16)
            def back(n):
                sp.wait_ge(og_out[n], 16)
                sp.dma_start(gT[:, n], o_d[n].rearrange("b p t -> p b t")).then_inc(gT_in, 16)

            for n in range(NB):
                sp.wait_ge(og_sum, n + 1)
                sp.dma_start(o_d[n].rearrange("b (h d) t -> (b h) d t", h=H), og[:, n]).then_inc(og_out[n], 16)
                if n >= 2:
                    back(n - 2)
            back(NB - 2)
            back(NB - 1)
            for q, (h0, m) in enumerate(HC):
                sp.dma_start(down_w[0:m, :, q, :], down_t[:, h0:h0 + m, :].rearrange("e p n -> p e n")).then_inc(down_in, 16)
            for g in range(G):
                sp.wait_ge(xn_ready, (G + g + 1) * TG)
                sp.dma_start(nm_d.rearrange("(i p) f -> p i f", p=P)[:, g * TG:(g + 1) * TG],
                             nm[:, g * TG:(g + 1) * TG, :]).then_inc(nm_out, 16)
            for k in range(2):
                sp.wait_ge(y_out[k], 16 * ((NT + 1 - k) // 2))
            for g in range(G):
                sp.dma_start(y_in[g], y_d[0:2 * B * S, :].rearrange("(i p k) f -> p i k f", p=P, k=2)[:, g * TG:(g + 1) * TG]
                             ).then_inc(y_back[g], 16)
            for g in range(G):
                if g < G - 1:
                    sp.wait_ge(result_ready, g + 1)
                else:
                    sp.wait_ge(last_result_ready, 1)
                sp.dma_start(out.rearrange("(i p) f -> p i f", p=P)[:, g * TG:(g + 1) * TG, :],
                             x_all[:, g * TG:(g + 1) * TG, :]).then_inc(out_done, 16)
            sp.wait_ge(out_done, G * 16)

        @block.scalar
        def _(act):
            col = lambda v: v.rearrange("(p a) -> p a", a=1)
            for i, v in enumerate((q_conv, k_conv, v_conv)):
                act.dma_start(conv_w[:, i, :], v).then_inc(w_bias, 16)
            for i, v in enumerate((bq, bk, bv, bg)):
                act.dma_start(bias_qkvg[:, i:i + 1], col(v)).then_inc(w_bias, 16)
            act.dma_start(bias_ab[0:H, :], col(ba)).then_inc(w_bias, 16)
            act.dma_start(bias_ab[H:2 * H, :], col(bb)).then_inc(w_bias, 16)

            def squares(h):
                act.wait_ge(raw_in[h], 2 * 16)
                nc.scalar.activation(square, raw[:, h, 0:2].rearrange("p w d t -> p (w d t)"),
                                     ACT.Square).then_inc(sq_ready, 1)
                act.wait_ge(ss_ready, h + 1)
                if h:
                    act.wait_ge(kq_ready, 2 * h)
                nc.scalar.activation(rn[:, :, :].rearrange("p w t -> p (w t)"), banks[:, 1, 0:2 * SH] if h else
                                     ss[:, :, :].rearrange("p w t -> p (w t)"), ACT.Sqrt).then_inc(root_ready, 1)

            def move_aq(h):
                act.wait_ge(qk_psum, h + 1)
                nc.scalar.copy(aq_low[:, :, h * CH:(h + 1) * CH],
                               banks[:, 6, 0:NLOW * CH].rearrange("p (m c) -> p m c", m=NLOW)).then_inc(aq_moved, 1)
                nc.scalar.copy(aq_diag[:, :, h * CH:(h + 1) * CH],
                               banks[:, 7, 0:C * CH].rearrange("p (m c) -> p m c", m=C)).then_inc(aq_moved, 1)

            def pad(g):
                h, b0 = group(g)
                act.wait_ge(xT_psum, g + 1)
                nc.scalar.copy(x_pad[:, b0:b0 + TG, KW - 1 + h * SH:KW - 1 + (h + 1) * SH],
                               banks[:, 0, :].rearrange("p (b t) -> p b t", b=TG)).then_inc(xnT_ready, 1)

            pad(0)
            pad(1)
            act.wait_ge(biases_ready, 1)
            act.wait_ge(w_bias, N_BIAS * 16)
            for g, w in ORDER:
                h, b0 = group(g)
                if (g, w) in ((0, AB), (0, V)):
                    pad(2 if w == AB else 3)
                if g % 2 == 0 and w == V:
                    squares(h)
                act.wait_ge(proj_psum, nth((g, w)))
                if w == AB:
                    if g == 2:
                        act.wait_ge(ab_out[0], 32)
                    nc.scalar.activation(ab_sb[:, b0:b0 + TG, :], banks[0:2 * H, 5, :].rearrange("p (b t) -> p b t", b=TG),
                                         ACT.Identity, bias=bias_ab[:, 0:1]).then_inc(ab_moved, 1)
                    if g % 2:
                        act.wait_ge(ab_moved, g + 1)
                        nc.scalar.activation(ab_sb[:, :, :], ab_sb[:, :, :], ACT.Sigmoid).then_inc(ab_sig, 1)
                        act.wait_ge(ab_sig, h + 1)
                        for k in range(2):
                            act.dma_start(ab_d[h, k].rearrange("b h t -> h b t"),
                                          ab_sb[k * H:(k + 1) * H, :, :]).then_inc(ab_out[h], 16)
                    continue
                if h:
                    act.wait_ge((v_out if w == V else qk_out)[0], (2 if w == V else 4) * 16)
                else:
                    act.wait_ge(edge_ready, nth_convolved((g, w)) * (KW - 1))
                nc.scalar.activation(qs[:, g % 2, w].rearrange("p j t -> p (j t)"), banks[:, bank_of(g, w), :], ACT.Silu,
                                     bias=conv_b[:, w, KW - 1:KW]).then_inc(silu_ready, 1)
            move_aq(0)
            for g in range(G):
                h, b0 = group(g)
                act.wait_ge(gate_psum, g + 1)
                nc.scalar.activation(gateT[:, b0:b0 + TG, h * SH:(h + 1) * SH],
                                     banks[:, 4 + g % 2, :].rearrange("p (b t) -> p b t", b=TG), ACT.Silu,
                                     bias=bias_qkvg[:, 3:4]).then_inc(gate_ready, 1)
            act.wait_ge(decay_ready, NH)
            act.wait_ge(wu_ready, WU)
            for h in range(NH):
                if h:
                    move_aq(h)
                act.wait_ge(u_pool, h + 1)
                with act.Fori(h * NC // (4 * RING), (h + 1) * NC // (4 * RING)) as it:
                    for k in range(2 * RING):
                        if k % RING == 0:
                            act.wait_ge(scan, it * (8 * 2 * RING) + (8 * max(k - RING, 0) + 2 if k else 1))
                            nc.scalar.copy(ws[:, k:k + RING, :, :, D].rearrange("p c r d -> p (c r) d"),
                                           us[:, bass.ds(it * (2 * RING * C) + k * C, RING * C), :]).then_inc(ring_ready, 1)
                        c = it * (2 * RING) + k
                        act.wait_ge(scan, it * (8 * 2 * RING) + (8 * k + 2))
                        nc.scalar.activation(outer[:, k % 2, :, C], states[:, bass.ds(c, 1), :].rearrange("p a n -> p (a n)"),
                                             ACT.Copy, scale=gc[:, C - 1, bass.ds(c, 1)]).then_inc(carry_ready, 1)
            for n in range(NB):
                act.wait_ge(slots_used, (n + 1) * SLOTS - (len(PAIRS) if n == NB - 1 else 0))
                nc.scalar.activation(og[:, n], banks[:, n, 0:DB * D].rearrange("p (t d) -> p d t", d=D),
                                     ACT.Copy, accum_out=gn_part[:, 0, n:n + 1]).then_inc(og_sum, 1)
                if n >= 2:
                    act.wait_ge(og_sq, n - 1)
                nc.scalar.activation(sq_dump[:, n % 2, 0:DB * D], banks[:, n, 0:DB * D], ACT.Square,
                                     accum_out=gn_part[:, 1, n:n + 1]).then_inc(og_sq, 1)
            act.wait_ge(gT_in, NB * 16)
            act.wait_ge(gn_coef, 2)
            for b in range(B):
                nc.scalar.activation(yT[:, b, :].rearrange("p (n t) -> p n t", n=NB), gT[:, :, b, :], ACT.Identity,
                                     scale=gn_ab[:, 0, b:b + 1], bias=gn_ab[:, 1, b:b + 1]).then_inc(y_aff, 1)

            for g in range(G):
                act.wait_ge(shift_ready, g + 1)
                if g >= 2:
                    act.wait_ge(ln_used, g - 1)
                for j in range(TG):
                    i = g * TG + j
                    nc.scalar.activation(xn[:, g % 2, j, :], banks[:, 4 + g, j * P:(j + 1) * P], ACT.Identity,
                                         scale=rstd[:, i:i + 1], bias=shift[:, i:i + 1]).then_inc(ln_ready, 1)
            act.wait_ge(w_in, N_W * 16)
            for g in range(G):
                act.wait_ge(xT_psum, G + g + 1)
                nc.scalar.activation(xnT[:, g * N:(g + 1) * N], banks[:, g, :], ACT.Copy,
                                     scale=normw_sb[:, 0:1]).then_inc(xnT_ready, 1)
            act.wait_ge(exp_in, 2)
            nc.scalar.activation(r_p[:, :, :], r_c[:, :, :], ACT.Exp).then_inc(exp_done, 1)
            nc.scalar.activation(r_s[:, 3, :], r_s[:, 2, :], ACT.Exp).then_inc(exp_done, 1)

            def rows(j, k, first=False):
                act.wait_ge(xgT_psum, j + 1)
                if not first:
                    act.wait_ge(gu_psum, j - 1)
                nc.scalar.activation(xgT[:, k, :], banks[:, 7 * k, 0:P], ACT.Copy,
                                     scale=normw_sb[:, 0:1]).then_inc(xgT_ready, 1)

            def gate(j, k, first=False):
                act.wait_ge(gu_psum, j + 1)
                if not first:
                    act.wait_ge(down_psum, j - 1)
                nc.scalar.activation(hidden[:, k, :], banks[:, 1 + k, 0:3 * P], ACT.Silu).then_inc(gate_done, 1)

            def result(j, k, sent_rows=None):
                act.wait_ge(down_psum, j + 1)
                if sent_rows is not None:
                    act.wait_ge(y_out[k], sent_rows)
                nc.scalar.copy(y_sb[:, k, :], banks[:, 5 + k, 0:P]).then_inc(y_sb_ready, 1)

            rows(0, 0, True)
            rows(1, 1, True)
            gate(0, 0, True)
            rows(2, 0)
            gate(1, 1, True)
            result(0, 0)
            rows(3, 1)
            gate(2, 0)
            result(1, 1)
            with act.Fori(0, (NT - 5) // 2) as it:
                for k in (1, 0):
                    j = it * 2 + (3 if k else 4)
                    rows(j + 1, 1 - k)
                    gate(j, k)
                    result(j - 1, 1 - k, it * 16 + 16)
            rows(NT - 1, 0)
            gate(NT - 2, 1)
            result(NT - 3, 0, 16 * ((NT - 3) // 2))
            gate(NT - 1, 0)
            result(NT - 2, 1, 16 * ((NT - 3) // 2))
            result(NT - 1, 0, 16 * (NT // 2))
            act.wait_ge(weight_ready, 2)
            for g in range(1, G):
                act.wait_ge(y_back[g], 16)
                for j in range(TG):
                    nc.scalar.activation(y_in[g][:, j, 0, :], y_in[g][:, j, 0, :], ACT.Copy,
                                         scale=weight[:, g * TG + j, 0:1]).then_inc(first_scaled, 1)
            for g in range(G):
                act.wait_ge(shift_ready, G + g + 1)
                for j in range(TG if g < G - 1 else TG // 2):
                    i = g * TG + j
                    nc.scalar.activation(nm_all[:, i, :], h_all[:, i, :], ACT.Identity,
                                         scale=rstd[:, i:i + 1], bias=shift[:, i:i + 1]).then_inc(ln_ready, 1)

        @block.gpsimd
        def _(pool):
            own = Steps(pool, pool_s)
            gp = nc.gpsimd
            own.step(gp.memset(mhalf[:, :], -0.5))
            own.link(gp.memset(ident[:, :], 0.0))
            gp.affine_select(out=ident[:, :], in_=ident[:, :], compare_op=ALU.not_equal, fill=1.0, base=0,
                             pattern=[[-1, P]], channel_multiplier=1).then_inc(const_ready, 1)
            gp.memset(x_pad[:, :, 0:KW - 1], 0.0).then_inc(const_ready, 1)

            def root(n):
                pool.wait_ge(var_ready, n + 1)
                k = (n % G) * TG
                gp.tensor_tensor(rstd[:, k:k + TG], mv[:, k:k + TG, 1], mhalf[:, :], ALU.pow).then_inc(rstd_ready, 1)

            root(0)
            root(1)
            gp.memset(states[:, 0, 0:D * DL], 0.0).then_inc(scan, 1)
            gp.memset(states[:, 0, D * DL:D * D], 0.0).then_inc(scan, 1)
            gp.iota(ranks[:, :], pattern=[[-1, NE]], base=NE, channel_multiplier=0,
                    allow_small_or_imprecise_dtypes=True).then_inc(const_ready, 1)
            gp.memset(all_ones[:, :], 1.0).then_inc(const_ready, 1)
            gp.memset(ones_16[:, :], 1.0).then_inc(const_ready, 1)
            own.step(gp.memset(zeros[:, :], 0.0))
            own.step(gp.memset(l_tri[:, :], 1.0))
            gp.iota(col_no[:, :], pattern=[[1, P]], base=0, channel_multiplier=0,
                    allow_small_or_imprecise_dtypes=True).then_inc(const_ready, 1)
            gp.iota(column_no[:, :, :], pattern=[[2 * P, T], [0, 2]], base=2 * P, channel_multiplier=0,
                    allow_small_or_imprecise_dtypes=True).then_inc(tables_ready, 1)
            gp.iota(in_column[:, :, :], pattern=[[0, T], [1, 2]], base=0, channel_multiplier=2,
                    allow_small_or_imprecise_dtypes=True).then_inc(tables_ready, 1)
            gp.iota(past_no[:, :], pattern=[[P, NT]], base=2 * B * S + 2 * P, channel_multiplier=1,
                    allow_small_or_imprecise_dtypes=True).then_inc(tables_ready, 1)
            root(2)
            root(3)
            own.wait()
            gp.affine_select(out=l_tri[:, :], in_=l_tri[:, :], compare_op=ALU.is_gt, fill=0.0, base=0,
                             pattern=[[1, P]], channel_multiplier=-1).then_inc(const_ready, 1)
            k4 = kn[:, :, :].rearrange("p (c r) e -> p r c e", r=C)
            q4 = qn[:, :, :].rearrange("p (c r) e -> p r c e", r=C)
            u4 = us[:, :, :].rearrange("p (c r) e -> p r c e", r=C)

            def solve_u(h):
                nu = NU[h]
                c0, c1 = (h + 1) * CH - nu, (h + 1) * CH
                pool.wait_ge(gram_head, h + 1)
                pool.wait_ge(gram_used, h + 1)
                pool.wait_ge(v_scaled, h + 1)
                for i in range(C - 1):
                    n = C - 1 - i
                    tu = u_tmp_pool[:, 0:n * nu * D].rearrange("p (r c e) -> p r c e", r=n, c=nu)
                    m = gram[:, h, LOW[i]:LOW[i] + n, CH - nu:CH].unsqueeze(3).broadcast_to([P, n, nu, D])
                    own.link(gp.tensor_tensor(tu, m, u4[:, i:i + 1, c0:c1].broadcast_to([P, n, nu, D]), ALU.mult))
                    ins = gp.tensor_tensor(u4[:, i + 1:C, c0:c1], u4[:, i + 1:C, c0:c1], tu, ALU.subtract)
                    if i < C - 2:
                        own.link(ins)
                    else:
                        ins.then_inc(u_pool, 1)

            for h in range(NH):
                c0, c1 = h * CH, (h + 1) * CH
                pool.wait_ge(ab_out[h], 32)
                pool.dma_start(ab_bh[:, h, :, :], ab_d[h].rearrange("k b h t -> (b h) k t")).then_inc(ab_in[h], 16)
                pool.wait_ge(ab_in[h], 16)
                al = ab_bh[:, h, 0, :].rearrange("p (c r) -> p r c", r=C)
                for i in range(C - 1):
                    own.step(gp.tensor_copy(dec[:, LOW[i], c0:c1], al[:, i + 1, :]))
                own.step(gp.tensor_copy(gc[:, 0, c0:c1], al[:, 0, :]))
                own.wait()
                for i in range(C - 3, -1, -1):
                    n = C - 2 - i
                    own.link(gp.tensor_tensor(dec[:, LOW[i] + 1:LOW[i] + 1 + n, c0:c1],
                                              dec[:, LOW[i + 1]:LOW[i + 1] + n, c0:c1],
                                              al[:, i + 1:i + 2, :].broadcast_to([P, n, CH]), ALU.mult))
                gp.tensor_tensor(gc[:, 1:C, c0:c1], dec[:, 0:C - 1, c0:c1],
                                 al[:, 0:1, :].broadcast_to([P, C - 1, CH]), ALU.mult).then_inc(decay_ready, 1)
                if h:
                    solve_u(0)
                pool.wait_ge(v_in[h], 16)
                gp.tensor_tensor(us[:, h * SH:(h + 1) * SH, :].rearrange("p t d -> p d t"), raw[:, h, 2],
                                 ab_bh[:, h, 1:2, :].broadcast_to([P, D, SH]), ALU.mult).then_inc(v_scaled, 1)
                pool.wait_ge(kq_ready, 2 * (h + 1))
                if h:
                    pool.wait_ge(qk_psum, h)
                for i in range(C - 1):
                    n = C - 1 - i
                    gp.tensor_tensor(qk[:, LOW[i]:LOW[i] + n], q4[:, i + 1:C, c0:c1],
                                     k4[:, i:i + 1, c0:c1].broadcast_to([P, n, CH, D]), ALU.mult).then_inc(qk_ready, 1)
                gp.tensor_tensor(qk[:, NLOW:NLOW + C], q4[:, :, c0:c1], k4[:, :, c0:c1], ALU.mult).then_inc(qk_ready, 1)
                for i in range(C - 1):
                    own.step(gp.tensor_copy(tail[:, i, :], dec[:, LOW[i] + C - 2 - i, c0:c1]))
                own.wait()
                pool.wait_ge(qk_ready, C * (h + 1))
                pool.wait_ge(kk_ready, (C - 1) * (h + 1))
                gp.tensor_tensor(k4[:, 0:C - 1, c0:c1], k4[:, 0:C - 1, c0:c1],
                                 tail[:, :, :].unsqueeze(3).broadcast_to([P, C - 1, CH, D]), ALU.mult).then_inc(kd_ready, 1)
                gp.tensor_tensor(q4[:, :, c0:c1], q4[:, :, c0:c1],
                                 gc[:, :, c0:c1].unsqueeze(3).broadcast_to([P, C, CH, D]), ALU.mult).then_inc(qg_ready, 1)
                pool.wait_ge(kd_ready, h + 1)

            def decay_aq(h):
                c0, c1 = h * CH, (h + 1) * CH
                pool.wait_ge(aq_moved, 2 * (h + 1))
                gp.tensor_tensor(aq_low[:, :, c0:c1], aq_low[:, :, c0:c1], dec[:, :, c0:c1], ALU.mult).then_inc(aq_ready, 1)
                pool.wait_ge(aq_ready, h + 1)

            decay_aq(0)
            solve_u(1)
            pool.wait_ge(qk_psum, NH)
            for i in range(1, C):
                own.step(gp.memset(slots[:, D + i].rearrange("p (c r) d -> p c r d", r=C)[:, :, 0:i], 0.0))
            own.wait()
            pool.wait_ge(qg_ready, NH)
            for n in range(NB):
                if n == NB // NH:
                    decay_aq(1)
                last_chunk = CB * (n + 1) - 1
                pool.wait_ge(scan, 8 * last_chunk + 2)
                for s in range(SLOTS):
                    if s == D:
                        pool.wait_ge(scan, 8 * last_chunk + 6)
                    if n == NB - 1 and s in SLOTS_DVE:
                        continue
                    if n:
                        pool.wait_ge(slots_used, (n - 1) * SLOTS + s + 1)
                    out_product(gp, slots, s, n, qn, states, us, aq_low, aq_diag, slots_pool)
            pool.wait_ge(gn_var, 1)
            gp.tensor_tensor(gn_s[:, 4:5], gn_s[:, 3:4], mhalf[:, 0:1], ALU.pow).then_inc(gn_rstd, 1)
            for g in range(G + 2):
                if g < G:
                    root(G + g)
                if g >= 2:
                    pool.wait_ge(spread_ready, g - 1)
                    k = (g - 2) * TG
                    for f, signal in ((1, factor_ready), (0, h_factor_ready)):
                        gp.tensor_tensor(factor[:, f, k:k + TG], spread[:, f, k:k + TG], mhalf[:, :],
                                         ALU.pow).then_inc(signal, 1)
            pool.wait_ge(h_factor_ready, G)
            for i in range(T):
                gp.tensor_scalar(h_all[:, i, :], x_all[:, i, :], mv[:, i, 0:1], factor[:, 0, i:i + 1],
                                 ALU.subtract, ALU.mult).then_inc(h_ready, 1)
            pool.wait_ge(tables_ready, 3)
            pool.wait_ge(one_tile_ready, 1)
            gp.tensor_tensor(tile_hot[:, :, 0, :], tile_one,
                             column_no[:, :, :].rearrange("p i k -> p (i k)").unsqueeze(2).broadcast_to([P, FT, NT]),
                             ALU.mult).then_inc(numbers_ready, 1)
            pool.wait_ge(nm_out, G * 16)
            pool.wait_ge(src_ready, 1)
            for j in range(NT + RG - 1):
                if j < NT:
                    if j >= RG:
                        pool.wait_ge(xgT_psum, j - RG + 1)
                    gp.indirect_dma_start(out=xg[:, j % RG, :], out_offset=None, in_=nm_d,
                                          in_offset=bass.IndirectOffsetOnAxis(ap=src[:, j:j + 1], axis=0)
                                          ).then_inc(xg_in[j % RG], 16)
                i = j - (RG - 1)
                if i >= 0:
                    if i == 0:
                        pool.wait_ge(dest_ready, 1)
                    pool.wait_ge(y_sb_ready, i + 1)
                    gp.indirect_dma_start(out=y_d, out_offset=bass.IndirectOffsetOnAxis(ap=dest[:, i:i + 1], axis=0),
                                          in_=y_sb[:, i % 2, :], in_offset=None).then_inc(y_out[i % 2], 16)
            pool.wait_ge(h_ready, T)
            for g in range(G + 1):
                if g + 1 < G:
                    tl = slice((g + 1) * TG, (g + 2) * TG)
                    pool.wait_ge(first_scaled, (g + 1) * TG)
                    gp.tensor_tensor(h_all[:, tl, :], h_all[:, tl, :], y_in[g + 1][:, :, 0, :],
                                     ALU.add).then_inc(first_added, 1)
                if g:
                    root(2 * G + g - 1)
                if g >= 2:
                    normed = slice((g - 2) * TG, (g - 1) * TG)
                    pool.wait_ge(ln_ready, (G + g - 1) * TG)
                    gp.tensor_tensor(x_all[:, normed, :], x_all[:, normed, :], nm_all[:, normed, :],
                                     ALU.add).then_inc(result_ready, 1)

        @block.vector
        def _(dve):
            own = Steps(dve, vec)
            v = nc.vector
            roots = [0]

            def moments(g, src):
                for j in range(TG):
                    own.step(v.bn_stats(stats[:, g * TG + j, :], src(j)))
                own.wait()
                for j in range(TG):
                    own.step(v.bn_aggr(mv[:, g * TG + j, :], stats[:, g * TG + j, :]))
                own.wait()

            def statistics(g, src):
                moments(g, src)
                k = slice(g * TG, (g + 1) * TG)
                v.tensor_scalar(mv[:, k, 1], mv[:, k, 1], LN_EPS, None, ALU.add).then_inc(var_ready, 1)

            def await_root():
                roots[0] += 1
                dve.wait_ge(rstd_ready, roots[0])

            def scale_shift(g):
                await_root()
                k = slice(g * TG, (g + 1) * TG)
                v.scalar_tensor_tensor(shift[:, k], mv[:, k, 0], -1.0, rstd[:, k], ALU.mult, ALU.mult).then_inc(shift_ready, 1)

            dve.wait_ge(x_in[0], 16)
            statistics(0, lambda j: x_bh[:, j, 0, :])
            await_root()
            for j in range(TG):
                v.tensor_scalar(xn[:, 0, j, :], x_bh[:, j, 0, :], mv[:, j, 0:1], rstd[:, j:j + 1],
                                ALU.subtract, ALU.mult).then_inc(xn_ready, 1)
            for w in range(3):
                dve.wait_ge(w_conv, N_CONV * 16)
                v.tensor_tensor(w_tap[:, w], w_proj[:, w:w + 1, :].broadcast_to([P, KW, P]), conv_r[:, w],
                                ALU.mult).then_inc(tap_ready, 1)
            dve.wait_ge(w_bias, N_BIAS * 16)
            for k in range(1, KW):
                own.link(v.tensor_tensor(conv_w[:, :, k], conv_w[:, :, k], conv_w[:, :, k - 1], ALU.add))
            v.tensor_tensor(conv_b[:, :, :], conv_w[:, :, :], bias_qkvg[:, 0:3].unsqueeze(2).broadcast_to([P, 3, KW]),
                            ALU.mult).then_inc(biases_ready, 1)
            dve.wait_ge(biases_ready, 1)

            def ln_in(g):
                h, b0 = group(g)
                k = g * TG
                dve.wait_ge(x_in[g], 16)
                statistics(g, lambda j: x_bh[:, b0 + j, h, :])
                await_root()
                if g >= 2:
                    dve.wait_ge(xT_psum, g - 1)
                for j in range(TG):
                    v.tensor_scalar(xn[:, g % 2, j, :], x_bh[:, b0 + j, h, :], mv[:, k + j, 0:1], rstd[:, k + j:k + j + 1],
                                    ALU.subtract, ALU.mult).then_inc(xn_ready, 1)

            def edges(g, which):
                for w in which:
                    dve.wait_ge(proj_psum, nth((g, w)))
                    for t in range(KW - 1):
                        col = banks[:, bank_of(g, w), :].rearrange("p (b t) -> p b t", b=TG)[:, :, t]
                        v.tensor_scalar(col, col, conv_b[:, w, KW - 2 - t:KW - 1 - t], None,
                                        ALU.subtract).then_inc(edge_ready, 1)

            ln_in(1)
            edges(0, (Q, K))
            ln_in(2)
            edges(1, (Q, K))
            ln_in(3)
            edges(0, (V,))
            edges(1, (V,))

            k4 = kn[:, :, :].rearrange("p (c r) e -> p r c e", r=C)
            w4 = wx[:, :, :].rearrange("p (c r) e -> p r c e", r=C)
            u4 = us[:, :, :].rearrange("p (c r) e -> p r c e", r=C)
            for h in range(NH):
                c0, c1 = h * CH, (h + 1) * CH
                t0, t1 = h * SH, (h + 1) * SH
                if h == 0:
                    dve.wait_ge(sq_ready, 1)
                    v.tensor_reduce(ss[:, :, :], square.rearrange("p (w d t) -> p w t d", w=2, d=D),
                                    AX.X, ALU.add).then_inc(ss_ready, 1)
                dve.wait_ge(root_ready, h + 1)
                own.link(v.tensor_scalar(rn[:, :, :], rn[:, :, :], QK_EPS, None, ALU.add))
                own.link(v.reciprocal(rn[:, :, :], rn[:, :, :]))

                def normed(w, dst):
                    v.tensor_tensor(dst[:, t0:t1, :].rearrange("p t d -> p d t"), raw[:, h, w],
                                    rn[:, w:w + 1, :].broadcast_to([P, D, SH]), ALU.mult).then_inc(kq_ready, 1)

                normed(1, kn)
                dve.wait_ge(kq_ready, 2 * h + 1)
                dve.wait_ge(ab_in[h], 16)
                be = ab_bh[:, h, 1, :]
                own.link(v.tensor_tensor(wx[:, t0:t1, :], kn[:, t0:t1, :], be.unsqueeze(2).broadcast_to([P, SH, D]), ALU.mult))
                for i in (*range(1, C - 1), 0):
                    n = C - 1 - i
                    v.tensor_tensor(kk[:, LOW[i]:LOW[i] + n], w4[:, i + 1:C, c0:c1],
                                    k4[:, i:i + 1, c0:c1].broadcast_to([P, n, CH, D]), ALU.mult).then_inc(kk_ready, 1)
                dve.wait_ge(kk_ready, (C - 1) * (h + 1))
                own.step(v.tensor_reduce(gram[:, h, 0:C - 1, :], kk[:, 0:C - 1], AX.X, ALU.add))
                normed(0, qn)
                dve.wait_ge(decay_ready, h + 1)
                own.step(v.tensor_scalar(gc_neg[:, :, :], gc[:, :, c0:c1], -1.0, None, ALU.mult))
                own.wait()
                own.step(v.tensor_tensor(w4[:, :, c0:c1], w4[:, :, c0:c1],
                                         gc_neg[:, :, :].unsqueeze(3).broadcast_to([P, C, CH, D]), ALU.mult))
                dve.wait_ge(vec, own.n - 1)
                v.tensor_tensor(gram[:, h, 0:C - 1, :], gram[:, h, 0:C - 1, :], dec[:, 0:C - 1, c0:c1],
                                ALU.mult).then_inc(gram_head, 1)
                dve.wait_ge(gram_psum, h + 1)
                v.tensor_tensor(gram[:, h, C - 1:NLOW, :],
                                banks[:, 0, (C - 1) * CH:NLOW * CH].rearrange("p (m c) -> p m c", c=CH),
                                dec[:, C - 1:NLOW, c0:c1], ALU.mult).then_inc(gram_used, 1)
                dve.wait_ge(gram_head, h + 1)
                dve.wait_ge(gram_used, h + 1)
                own.wait()
                dve.wait_ge(v_scaled, h + 1)
                nu = CH - NU[h]
                for i in range(C - 1):
                    n = C - 1 - i
                    m = gram[:, h, LOW[i]:LOW[i] + n, :].unsqueeze(3).broadcast_to([P, n, CH, D])
                    tw = w_tmp[:, 0:n * CH * D].rearrange("p (r c e) -> p r c e", r=n, c=CH)
                    last = own.step if i < C - 2 else lambda ins: ins.then_inc(wu_ready, 1)
                    own.step(v.tensor_tensor(tw, m, w4[:, i:i + 1, c0:c1].broadcast_to([P, n, CH, D]), ALU.mult))
                    if nu:
                        tu = u_tmp[:, 0:n * nu * D].rearrange("p (r c e) -> p r c e", r=n, c=nu)
                        own.step(v.tensor_tensor(tu, m[:, :, 0:nu], u4[:, i:i + 1, c0:c0 + nu].broadcast_to([P, n, nu, D]),
                                                 ALU.mult))
                    dve.wait_ge(vec, own.n - (1 if nu else 0))
                    last(v.tensor_tensor(w4[:, i + 1:C, c0:c1], w4[:, i + 1:C, c0:c1], tw, ALU.subtract))
                    if nu:
                        dve.wait_ge(vec, own.n - (1 if i < C - 2 else 0))
                        last(v.tensor_tensor(u4[:, i + 1:C, c0:c0 + nu], u4[:, i + 1:C, c0:c0 + nu], tu, ALU.subtract))
                    own.wait()
                dve.wait_ge(wu_ready, WU if h else 2)

            for h in range(NH):
                dve.wait_ge(kd_ready, h + 1)
                with dve.Fori(h * NC // (4 * RING), (h + 1) * NC // (4 * RING)) as it:
                    for k in range(2 * RING):
                        c = it * (2 * RING) + k
                        tok = bass.ds(it * (2 * RING * C) + k * C, C)
                        base = it * (8 * 2 * RING)

                        for a in range(2):
                            rows = slice(a * DL, (a + 1) * DL)
                            dve.wait_ge(scan, base + (8 * k + 1 + a))
                            v.tensor_tensor(
                                ws[:, k, :, rows, 0:D],
                                wx[:, tok, :].unsqueeze(2).broadcast_to([P, C, DL, D]),
                                states[:, bass.ds(c, 1), :].rearrange("p a (d e) -> p a d e", d=D)[:, :, rows, :]
                                .broadcast_to([P, C, DL, D]), ALU.mult).then_inc(scan, 1)
                        if k % RING == 0:
                            dve.wait_ge(ring_ready, it * 2 + (k // RING + 1))
                        for a in range(2):
                            rows = slice(a * DL, (a + 1) * DL)
                            dve.wait_ge(scan, base + (8 * k + 3 + a))
                            v.tensor_reduce(us[:, tok, rows], ws[:, k, :, rows, :], AX.X, ALU.add).then_inc(scan, 1)
                        for a in range(2):
                            rows = slice(a * DL, (a + 1) * DL)
                            dve.wait_ge(scan, base + (8 * k + 5 + a))
                            v.tensor_tensor(
                                outer[:, k % 2, a * DL * D:(a + 1) * DL * D, 0:C].rearrange("p (d e) i -> p d e i", d=DL),
                                kn[:, tok, :].rearrange("p i e -> p e i").unsqueeze(1).broadcast_to([P, DL, D, C]),
                                us[:, tok, rows].rearrange("p i d -> p d i").unsqueeze(2).broadcast_to([P, DL, D, C]),
                                ALU.mult).then_inc(scan, 1)
                        dve.wait_ge(carry_ready, it * (2 * RING) + (k + 1))
                        for a in range(2):
                            half = slice(a * DL * D, (a + 1) * DL * D)
                            dve.wait_ge(scan, base + (8 * k + 7 + a))
                            v.tensor_reduce(states[:, bass.ds(c + 1, 1), half].rearrange("p a n -> p (a n)"),
                                            outer[:, k % 2, half, :], AX.X, ALU.add).then_inc(scan, 1)

            dve.wait_ge(scan, 8 * (NC - 1) + 6)
            dve.wait_ge(qg_ready, NH)
            dve.wait_ge(aq_ready, NH)
            formed = [0]
            for k in range(len(PAIRS) + 1):
                if k < len(PAIRS):
                    for s in PAIRS[k]:
                        dve.wait_ge(slots_used, (NB - 2) * SLOTS + s + 1)
                        out_product(v, slots, s, NB - 1, qn, states, us, aq_low, aq_diag, slots_dve)
                    formed.append(formed[-1] + sum(products(s) for s in PAIRS[k]))
                if k:
                    a, b = PAIRS[k - 1]
                    dve.wait_ge(slots_dve, formed[k])
                    v.tensor_tensor(slots[:, a], slots[:, a], slots[:, b], ALU.add).then_inc(pair_ready, 1)

            dve.wait_ge(og_sum, NB)
            dve.wait_ge(og_sq, NB)
            own.link(v.tensor_reduce(gn_s[:, 0:2], gn_part[:, :, :], AX.X, ALU.add))
            own.link(v.tensor_scalar(gn_s[:, 0:2], gn_s[:, 0:2], 1.0 / (S * D), None, ALU.mult))
            own.link(v.tensor_tensor(gn_s[:, 2:3], gn_s[:, 0:1], gn_s[:, 0:1], ALU.mult))
            v.scalar_tensor_tensor(gn_s[:, 3:4], gn_s[:, 1:2], GN_EPS, gn_s[:, 2:3], ALU.add,
                                   ALU.subtract).then_inc(gn_var, 1)
            dve.wait_ge(gn_rstd, 1)
            own.link(v.scalar_tensor_tensor(gn_s[:, 5:6], gn_s[:, 0:1], -1.0, gn_s[:, 4:5], ALU.mult, ALU.mult))
            dve.wait_ge(row_in, 2 * 16)
            dve.wait_ge(w_in, N_W * 16)
            for k in range(2):
                v.tensor_scalar(gn_rhs[:, k, :], b_mask[:, :], gn_s[:, 4 + k:5 + k], None, ALU.mult).then_inc(gn_ready, 1)
            dve.wait_ge(gn_psum, 1)
            ab = banks[:, 0, 0:2 * B].rearrange("p (k b) -> p k b", k=2)
            v.tensor_scalar(gn_ab[:, 0, :], ab[:, 0, :], gn_sb[:, 0:1], None, ALU.mult).then_inc(gn_coef, 1)
            v.tensor_scalar(gn_ab[:, 1, :], ab[:, 1, :], gn_sb[:, 0:1], gn_sb[:, 1:2], ALU.mult, ALU.add).then_inc(gn_coef, 1)
            dve.wait_ge(gate_ready, G)
            for b in range(B):
                dve.wait_ge(y_aff, b + 1)
                v.tensor_tensor(yT[:, b, :], yT[:, b, :], gateT[:, b, :], ALU.mult).then_inc(y_ready, 1)

            def residual(g):
                tl = slice(g * TG, (g + 1) * TG)
                dve.wait_ge(ln_ready, (g + 1) * TG)
                v.tensor_tensor(x_all[:, tl, :], x_all[:, tl, :], xn[:, g % 2], ALU.add).then_inc(ln_used, 1)
                dve.wait_ge(ln_used, g + 1)
                moments(g, lambda j: x_all[:, g * TG + j, :])
                own.step(v.tensor_scalar(spread[:, 0, tl], mv[:, tl, 1], LN_EPS, None, ALU.add))
                own.wait()
                v.tensor_scalar(spread[:, 1, tl], mv[:, tl, 1], 1.0 + RMS_EPS, LN_EPS * RMS_EPS, ALU.mult,
                                ALU.add).then_inc(spread_ready, 1)

            def expert_input(g):
                dve.wait_ge(factor_ready, g + 1)
                for i in range(g * TG, (g + 1) * TG):
                    v.tensor_scalar(nm[:, i, :], x_all[:, i, :], mv[:, i, 0:1], factor[:, 1, i:i + 1],
                                    ALU.subtract, ALU.mult).then_inc(xn_ready, 1)

            for g in range(G + 3):
                if g < G:
                    dve.wait_ge(wo_psum, g + 1)
                    statistics(g, lambda j: banks[:, 4 + g, j * P:(j + 1) * P])
                if 1 <= g <= G:
                    scale_shift(g - 1)
                if 2 <= g < G + 2:
                    residual(g - 2)
                if g >= 3:
                    expert_input(g - 3)

            dve.wait_ge(tables_ready, 3)
            v.tensor_copy(col_16[:, :], col_no[:, :]).then_inc(tables_16, 1)
            v.tensor_copy(in_column_16[:, :, :], in_column[:, :, :]).then_inc(tables_16, 1)
            dve.wait_ge(logit_psum, 1)
            dve.wait_ge(const_ready, 7)
            lg = banks[:, 4, 0:T * NE].rearrange("p (i e) -> p i e", e=NE)
            bc = lambda k: r_s[:, k, :].unsqueeze(2).broadcast_to([P, T, NE])
            chosen = lambda k: onehot[:, :, :, k].rearrange("p e i -> p i e")
            for k, scores in ((0, lg), (1, r_b[:, :, :])):
                own.link(v.tensor_reduce(r_s[:, k, :], scores, AX.X, ALU.max))
                own.link(v.tensor_tensor(r_a[:, :, :], scores, bc(k), ALU.is_equal))
                own.link(v.tensor_tensor(r_a[:, :, :], r_a[:, :, :],
                                         ranks[:, :].unsqueeze(1).broadcast_to([P, T, NE]), ALU.mult))
                own.link(v.tensor_reduce(r_s[:, 4, :], r_a[:, :, :], AX.X, ALU.max))
                v.tensor_tensor(chosen(k), r_a[:, :, :], bc(4), ALU.is_equal).then_inc(onehot_ready, 1)
                dve.wait_ge(onehot_ready, k + 1)
                if k == 0:
                    own.link(v.scalar_tensor_tensor(r_b[:, :, :], chosen(0), -3e38, lg, ALU.mult, ALU.add))
            v.tensor_tensor(r_c[:, :, :], lg, bc(0), ALU.subtract).then_inc(exp_in, 1)
            v.tensor_tensor(r_s[:, 2, :], r_s[:, 1, :], r_s[:, 0, :], ALU.subtract).then_inc(exp_in, 1)
            flat = lambda a: a[:, :, :, :].rearrange("p e i k -> p (e i k)")
            dve.wait_ge(rank_psum, 1)
            prefix, total = banks[:, 5, 0:2 * P], banks[:, 6, 0:2 * P]
            own.link(v.tensor_tensor_scan(flat(incl), all_ones[:, :], total, 0.0, ALU.mult, ALU.add))
            own.link(v.tensor_tensor(flat(place), flat(incl), total, ALU.subtract))
            start, count, tiles, first, shift_e, last = (r_e[:, k, :] for k in range(6))
            own.step(v.tensor_copy(start, place[:, :, 0, 0]))
            own.step(v.tensor_tensor(count, incl[:, :, T - 1, 1], place[:, :, 0, 0], ALU.subtract))
            own.wait()
            own.step(v.tensor_tensor(flat(place), flat(place), prefix, ALU.add))
            own.link(v.tensor_scalar(tiles, count, 1.0 / P, (P - 1.0) / P - 0.5 + 0.5 / P, ALU.mult, ALU.add))
            own.link(v.tensor_scalar(tiles, tiles, ROUND, None, ALU.add))
            own.link(v.tensor_scalar(tiles, tiles, ROUND, None, ALU.subtract))
            own.link(v.tensor_tensor_scan(last, all_ones[:, 0:NE], tiles, 0.0, ALU.mult, ALU.add))
            own.link(v.tensor_tensor(first, last, tiles, ALU.subtract))
            own.link(v.scalar_tensor_tensor(shift_e, first, float(P), start, ALU.mult, ALU.subtract))
            own.link(v.tensor_tensor(place[:, :, :, :].rearrange("p e i k -> p e (i k)"),
                                     place[:, :, :, :].rearrange("p e i k -> p e (i k)"),
                                     shift_e.unsqueeze(2).broadcast_to([P, NE, 2 * T]), ALU.add))
            own.link(v.tensor_tensor(flat(place), flat(place), flat(onehot), ALU.mult))
            own.link(v.tensor_reduce(slot_f[:, :, :], place[:, :, :, :].rearrange("p e i k -> p i k e"), AX.X, ALU.add))
            flat_ik = lambda a: a[:, :, :].rearrange("p i k -> p (i k)")
            own.link(v.tensor_scalar(tile_of[:, :, :], slot_f[:, :, :], 1.0 / P, (1.0 - P) / (2 * P), ALU.mult, ALU.add))
            own.link(v.tensor_scalar(tile_of[:, :, :], tile_of[:, :, :], ROUND, None, ALU.add))
            own.link(v.tensor_scalar(tile_of[:, :, :], tile_of[:, :, :], ROUND, None, ALU.subtract))
            v.tensor_copy(tile_of_16[:, :, :], tile_of[:, :, :]).then_inc(at_ready, 1)
            v.scalar_tensor_tensor(row_of_16[:, :, :], tile_of[:, :, :], -float(P), slot_f[:, :, :],
                                   ALU.mult, ALU.add).then_inc(at_ready, 1)
            dve.wait_ge(tables_16, 2)
            dve.wait_ge(tables_ready, 3)
            dve.wait_ge(at_ready, 2)
            wide = [P, FT, NT]
            v.tensor_tensor(tile_one, col_16[:, 0:NT].unsqueeze(1).broadcast_to(wide),
                            flat_ik(tile_of_16).unsqueeze(2).broadcast_to(wide), ALU.is_equal).then_inc(one_tile_ready, 1)
            for q in range(4):
                c0, c1 = q * FT // 4, (q + 1) * FT // 4
                v.tensor_tensor(row_hot[:, c0:c1, :], col_16[:, :].unsqueeze(1).broadcast_to([P, c1 - c0, P]),
                                flat_ik(row_of_16)[:, c0:c1].unsqueeze(2).broadcast_to([P, c1 - c0, P]),
                                ALU.is_equal).then_inc(row_hot_ready, 1)
                if q == 0:
                    dve.wait_ge(one_tile_ready, 1)
                    v.tensor_tensor(tile_hot[:, :, 1, :], tile_one, flat_ik(in_column_16).unsqueeze(2).broadcast_to(wide),
                                    ALU.mult).then_inc(tile_hot_ready, 1)
            own.link(v.tensor_tensor(tile_cmp[:, :, :], tile_no[:, :].unsqueeze(2).broadcast_to([P, NT + 1, NE]),
                                     last.unsqueeze(1).broadcast_to([P, NT + 1, NE]), ALU.is_ge))
            own.link(v.tensor_reduce(tile_e[:, :], tile_cmp[:, :, :], AX.X, ALU.add))
            own.link(v.tensor_scalar(tile_e[:, :], tile_e[:, :], NE - 1.0, None, ALU.min))
            own.link(v.tensor_copy(tile_ei[:, :], tile_e[:, :]))

            def expert(j):
                return dve.value_load(tile_ei[0:1, bass.ds(j, 1)], min_val=0, max_val=NE - 1)

            dve.wait_ge(rows_psum, 1)
            v.tensor_copy(dest_f[:, :], banks[:, 7, 0:NT]).then_inc(number_ready, 1)
            dve.wait_ge(number_ready, 1)
            v.tensor_tensor(dest_f[:, :], dest_f[:, :], banks[:, 7, NT:2 * NT], ALU.add).then_inc(number_ready, 1)
            dve.wait_ge(number_ready, 2)
            own.link(v.tensor_scalar(src_f[:, :], dest_f[:, :], 0.5, -P - 0.25, ALU.mult, ALU.add))
            own.link(v.tensor_scalar(src_f[:, :], src_f[:, :], ROUND, None, ALU.add))
            own.link(v.tensor_scalar(src_f[:, :], src_f[:, :], ROUND, 0.0, ALU.subtract, ALU.max))
            v.tensor_copy(src[:, :], src_f[:, :]).then_inc(src_ready, 1)
            dve.wait_ge(src_ready, 1)
            own.link(v.scalar_tensor_tensor(src_f[:, :], dest_f[:, :], 0.0, past_no[:, :], ALU.is_equal, ALU.mult))
            own.link(v.scalar_tensor_tensor(dest_f[:, :], dest_f[:, :], -2.0 * P, src_f[:, :], ALU.add, ALU.add))
            v.tensor_copy(dest[:, :], dest_f[:, :]).then_inc(dest_ready, 1)

            def copy_gu(j, k, e):
                v.tensor_scalar(gu_cur[:, k, :], gu_w[:, bass.ds(e, 1), :].rearrange("p a n -> p (a n)"), 1.0, None,
                                ALU.mult).then_inc(gu_cur_ready, 1)

            def copy_down(j, k, e):
                v.tensor_scalar(down_cur[:, k].rearrange("p j n -> p (j n)"),
                                down_w[:, bass.ds(e, 1)].rearrange("p a j n -> p (a j n)"), 1.0, None,
                                ALU.mult).then_inc(down_cur_ready, 1)

            def hide(j, k):
                dve.wait_ge(gate_done, j + 1)
                v.tensor_tensor(hidden[:, k, :], hidden[:, k, :], banks[:, 3 + k, 0:3 * P], ALU.mult).then_inc(hid_ready, 1)

            dve.wait_ge(gu_in, 16)
            dve.wait_ge(down_in, 48)
            dve.wait_ge(qk_psum, NH)
            e0, e1 = expert(0), expert(1)
            copy_gu(0, 0, e0)
            copy_down(0, 0, e0)
            copy_gu(1, 1, e1)
            hide(0, 0)
            copy_gu(2, 0, expert(2))
            copy_down(1, 1, e1)
            with dve.Fori(0, (NT - 3) // 2) as it:
                for k in (1, 0):
                    j = it * 2 + (2 - k)
                    e_gu, e_down = expert(j + 2), expert(j + 1)
                    hide(j, k)
                    copy_gu(j + 2, k, e_gu)
                    dve.wait_ge(down_psum, j)
                    copy_down(j + 1, 1 - k, e_down)
            e_last = expert(NT - 1)
            hide(NT - 2, 1)
            dve.wait_ge(down_psum, NT - 2)
            copy_down(NT - 1, 0, e_last)
            hide(NT - 1, 0)

            dve.wait_ge(exp_done, 2)
            own.link(v.tensor_reduce(r_s[:, 5, :], r_p[:, :, :], AX.X, ALU.add))
            own.link(v.reciprocal(r_s[:, 5, :], r_s[:, 5, :]))
            own.link(v.tensor_tensor(r_s[:, 3, :], r_s[:, 3, :], r_s[:, 5, :], ALU.mult))
            own.link(v.tensor_tensor(r_s[:, 4, :], r_s[:, 5, :], r_s[:, 3, :], ALU.add))
            own.link(v.reciprocal(r_s[:, 4, :], r_s[:, 4, :]))
            own.link(v.tensor_scalar(alpha_sb[:, :], alpha_sb[:, :], -0.5, 2.0, ALU.max, ALU.min))
            own.link(v.tensor_scalar(r_s[:, 4, :], r_s[:, 4, :], alpha_sb[:, 0:1], None, ALU.mult))
            for k, probability in ((0, 5), (1, 3)):
                v.tensor_tensor(weight[:, :, k], r_s[:, probability, :], r_s[:, 4, :], ALU.mult).then_inc(weight_ready, 1)
            dve.wait_ge(weight_ready, 2)
            dve.wait_ge(h_ready, T)
            for g in range(G):
                dve.wait_ge(y_back[g], 16)
                if g:
                    dve.wait_ge(first_added, g)
                for k in range(1 if g else 0, 2):
                    for j in range(TG):
                        i = g * TG + j
                        own.step(v.scalar_tensor_tensor(h_all[:, i, :], y_in[g][:, j, k, :], weight[:, i, k:k + 1],
                                                        h_all[:, i, :], ALU.mult, ALU.add))
                    own.wait()
                statistics(g, lambda j: h_all[:, g * TG + j, :])
                if g:
                    scale_shift(g - 1)
            scale_shift(G - 1)
            dve.wait_ge(shift_ready, 2 * G)
            for i in range(T - TG // 2, T):
                own.step(v.tensor_scalar(nm_all[:, i, :], h_all[:, i, :], rstd[:, i:i + 1], shift[:, i:i + 1],
                                         ALU.mult, ALU.add))
            own.wait()
            tl = slice((G - 1) * TG, T)
            dve.wait_ge(ln_ready, 2 * G * TG - TG // 2)
            v.tensor_tensor(x_all[:, tl, :], x_all[:, tl, :], nm_all[:, tl, :], ALU.add).then_inc(last_result_ready, 1)

        @block.tensor
        def _(pe):
            mm = nc.tensor.matmul
            pe.wait_ge(const_ready, 2)

            def transpose(g):
                pe.wait_ge(xn_ready, (g + 1) * TG)
                if g:
                    pe.wait_ge(xnT_ready, g)
                for j in range(TG):
                    ins = nc.tensor.transpose(banks[:, 0, j * P:(j + 1) * P], xn[:, g % 2, j, :], ident[:, :])
                ins.then_inc(xT_psum, 1)

            def sum_qk(h):
                pe.wait_ge(qk_ready, C * (h + 1))
                if h:
                    pe.wait_ge(aq_moved, 2 * h)
                for m0, m1, bank in ((0, NLOW, 6), (NLOW, NLOW + C, 7)):
                    for e in range(D):
                        ins = mm(banks[:, bank, 0:(m1 - m0) * CH], ident[:, :], qk[:, m0:m1, :, e],
                                 start=(e == 0), stop=(e == D - 1))
                ins.then_inc(qk_psum, 1)

            def sum_gram(h):
                for i0, i1 in ((1, 3), (3, C - 1)):
                    pe.wait_ge(kk_ready, h * (C - 1) + i1 - 1)
                    m0, m1 = LOW[i0], LOW[i1 - 1] + C - i1
                    for e in range(D):
                        ins = mm(banks[:, 0, m0 * CH:m1 * CH], ident[:, :], kk[:, m0:m1, :, e],
                                 start=(e == 0), stop=(e == D - 1))
                ins.then_inc(gram_psum, 1)

            transpose(0)
            for g, w in ORDER:
                h, b0 = group(g)
                if (g, w) in ((0, K), (0, AB), (0, V)):
                    transpose({K: 1, AB: 2, V: 3}[w])
                if (g, w) == (3, K):
                    pe.wait_ge(xnT_ready, G)
                    sum_gram(0)
                pe.wait_ge(xnT_ready, g + 1)
                if w == AB:
                    if g == 0:
                        pe.wait_ge(w_early, N_EARLY * 16)
                    else:
                        pe.wait_ge(ab_moved, g)
                    mm(banks[0:2 * H, 5, :], w_ab[:, :], x_pad[:, b0:b0 + TG, KW - 1 + h * SH:KW - 1 + (h + 1) * SH],
                       start=True, stop=True).then_inc(proj_psum, 1)
                    continue
                pe.wait_ge(tap_ready, w + 1)
                before = [p for p in CONVOLVED[:CONVOLVED.index((g, w))] if bank_of(*p) == bank_of(g, w)]
                if before:
                    pe.wait_ge(silu_ready, nth_convolved(before[-1]))
                for k in range(KW):
                    ins = mm(banks[:, bank_of(g, w), :], w_tap[:, w, k, :],
                             x_pad[:, b0:b0 + TG, k + h * SH:k + (h + 1) * SH], start=(k == 0), stop=(k == KW - 1))
                ins.then_inc(proj_psum, 1)
            pe.wait_ge(sq_ready, NH)
            pe.wait_ge(silu_ready, nth_convolved((3, Q)))
            for d in range(D):
                ins = mm(banks[:, 1, 0:2 * SH], ident[:, :],
                         square.rearrange("p (w d t) -> p w d t", w=2, d=D)[:, :, d, :], start=(d == 0), stop=(d == D - 1))
            ins.then_inc(ss_ready, 1)
            sum_qk(0)
            pe.wait_ge(silu_ready, 3 * G)
            for g in range(G):
                h, b0 = group(g)
                if g < 2:
                    pe.wait_ge(ab_moved, G)
                else:
                    pe.wait_ge(gate_ready, g - 1)
                mm(banks[:, 4 + g % 2, :], w_proj[:, 3, :],
                   x_pad[:, b0:b0 + TG, KW - 1 + h * SH:KW - 1 + (h + 1) * SH], start=True, stop=True).then_inc(gate_psum, 1)
            pe.wait_ge(gram_used, 1)
            sum_gram(1)
            sum_qk(1)
            pe.wait_ge(silu_ready, 3 * G)
            pe.wait_ge(xnT_ready, G)
            pe.wait_ge(gate_ready, G)
            pe.wait_ge(ab_moved, G)
            pe.wait_ge(gram_used, NH)
            pe.wait_ge(root_ready, NH)
            by_pool = 0
            for n in range(NB):
                if n == NB // NH:
                    pe.wait_ge(aq_moved, 2 * NH)
                last_block = n == NB - 1
                formed_by_pool = [s for s in range(SLOTS) if not (last_block and s in SLOTS_DVE)]
                for s in formed_by_pool:
                    by_pool += products(s)
                    pe.wait_ge(slots_pool, by_pool)
                    mm(banks[:, n, 0:DB * D], ident[:, :], slots[:, s].rearrange("p t d -> p (t d)"),
                       start=(s == 0), stop=(not last_block and s == SLOTS - 1)).then_inc(slots_used, 1)
            for k, (a, _) in enumerate(PAIRS):
                pe.wait_ge(pair_ready, k + 1)
                mm(banks[:, NB - 1, 0:DB * D], ident[:, :], slots[:, a].rearrange("p t d -> p (t d)"),
                   start=False, stop=(k == len(PAIRS) - 1)).then_inc(slots_used, 1)
            def output_bias(g):
                mm(banks[:, 4 + g, :], all_ones[0:1, 0:P], bo_row[:, :].unsqueeze(1).broadcast_to([1, TG, P]),
                   start=True, stop=False)

            pe.wait_ge(const_ready, 7)
            pe.wait_ge(row_in, 2 * 16)
            pe.wait_ge(w_in, N_W * 16)
            for g in range(G - 1):
                pe.wait_ge(og_sum, 4 + g + 1)
                pe.wait_ge(og_sq, 4 + g + 1)
                output_bias(g)
            pe.wait_ge(gn_ready, 2)
            mm(banks[:, 0, 0:2 * B], h_mask[:, :], gn_rhs[:, :, :].rearrange("p k b -> p (k b)"),
               start=True, stop=True).then_inc(gn_psum, 1)
            output_bias(G - 1)
            pe.wait_ge(aq_moved, 2 * NH)
            for g in range(G):
                for j in range(TG):
                    i = g * TG + j
                    pe.wait_ge(y_ready, i // NH + 1)
                    dst = banks[:, 4 + g, j * P:(j + 1) * P]
                    ins = mm(dst, yT[:, i // NH, (i % NH) * P:(i % NH + 1) * P], w_o[:, :],
                             start=False, stop=(j == TG - 1))
                ins.then_inc(wo_psum, 1)
            for g in range(G + 1):
                if g < G:
                    pe.wait_ge(xn_ready, (G + g + 1) * TG)
                    for j in range(TG):
                        ins = nc.tensor.transpose(banks[:, g, j * P:(j + 1) * P], nm[:, g * TG + j, :], ident[:, :])
                    ins.then_inc(xT_psum, 1)
                if g:
                    pe.wait_ge(xnT_ready, G + g)
                    for i in range((g - 1) * TG, g * TG):
                        ins = mm(banks[:, 4, i * NE:(i + 1) * NE], xnT[:, i * P:(i + 1) * P], w_router[:, :],
                                 start=True, stop=True)
            ins.then_inc(logit_psum, 1)
            pe.wait_ge(onehot_ready, 2)
            pe.wait_ge(const_ready, 7)
            oh = onehot[:, :, :, :].rearrange("p e i k -> p (e i k)")
            mm(banks[:, 5, 0:2 * P], l_tri[:, :], oh, start=True, stop=True)
            mm(banks[:, 6, 0:2 * P], ones_16[:, :], oh, start=True, stop=True).then_inc(rank_psum, 1)
            pe.wait_ge(exp_in, 1)
            for k in range(2):
                for bank in (1 + k, 3 + k):
                    mm(banks[:, bank, 0:3 * P], zeros[:, :], ident[:, 0:1].broadcast_to([P, 3 * P]), start=True, stop=True)
            pe.wait_ge(tile_hot_ready, 1)
            pe.wait_ge(numbers_ready, 1)
            for c in range(FT):
                if c % (FT // 4) == 0:
                    pe.wait_ge(row_hot_ready, c // (FT // 4) + 1)
                ins = mm(banks[:, 7, 0:2 * NT], row_hot[:, c, :], tile_hot[:, c].rearrange("p w t -> p (w t)"),
                         start=(c == 0), stop=(c == FT - 1))
            ins.then_inc(rows_psum, 1)

            def turn(j, k, slot, loads, first=False):
                pe.wait_ge(xg_in[slot], loads)
                if not first:
                    pe.wait_ge(xgT_ready, j - 1)
                nc.tensor.transpose(banks[:, 7 * k, 0:P], xg[:, slot, :], ident[:, :]).then_inc(xgT_psum, 1)

            def gate_up(j, k, first=False):
                pe.wait_ge(gu_cur_ready, j + 1)
                pe.wait_ge(xgT_ready, j + 1)
                if not first:
                    pe.wait_ge(hid_ready, j - 1)
                rhs = xgT[:, k, :]
                for bank, at in ((1 + k, 0), (3 + k, HID)):
                    for q, (h0, m) in enumerate(HC):
                        ins = mm(banks[0:m, bank, q * P:(q + 1) * P], gu_cur[:, k, at + h0:at + h0 + m], rhs,
                                 start=True, stop=True)
                ins.then_inc(gu_psum, 1)

            def down(j, k, first=False):
                pe.wait_ge(down_cur_ready, j + 1)
                pe.wait_ge(hid_ready, j + 1)
                if not first:
                    pe.wait_ge(y_sb_ready, j - 1)
                for q, (_, m) in enumerate(HC):
                    ins = mm(banks[:, 5 + k, 0:P], hidden[0:m, k, q * P:(q + 1) * P], down_cur[0:m, k, q, :],
                             start=(q == 0), stop=(q == 2))
                ins.then_inc(down_psum, 1)

            pe.wait_ge(number_ready, 2)
            turn(0, 0, 0, 16, True)
            turn(1, 1, 1, 16, True)
            gate_up(0, 0, True)
            turn(2, 0, 2, 16)
            gate_up(1, 1, True)
            down(0, 0, True)
            turn(3, 1, 3, 16)
            gate_up(2, 0)
            down(1, 1, True)
            with pe.Fori(0, (NT - 3) // RG) as it:
                for q in range(RG):
                    j, k = it * RG + (3 + q), (3 + q) % 2
                    turn(j + 1, 1 - k, (4 + q) % RG, it * 16 + ((4 + q) // RG + 1) * 16)
                    gate_up(j, k)
                    down(j - 1, 1 - k)
            for j in range(3 + (NT - 3) // RG * RG, NT):
                if j + 1 < NT:
                    turn(j + 1, (j + 1) % 2, (j + 1) % RG, 16 * ((j + 1) // RG + 1))
                gate_up(j, j % 2)
                down(j - 1, (j - 1) % 2)
            down(NT - 1, 0)


_INS = ['L0_attn_x', 'L0_attn_Wq', 'L0_attn_bq', 'L0_attn_Wk', 'L0_attn_bk', 'L0_attn_Wv', 'L0_attn_bv',
        'L0_attn_q_conv', 'L0_attn_k_conv', 'L0_attn_v_conv', 'L0_attn_Wa', 'L0_attn_ba', 'L0_attn_Wb', 'L0_attn_bb',
        'L0_attn_Wg', 'L0_attn_bg', 'L0_attn_gn_scale', 'L0_attn_gn_bias', 'L0_attn_Wo', 'L0_attn_bo',
        'L0_ffn_norm_weight', 'L0_ffn_router_weight', 'L0_ffn_gate_up_weight', 'L0_ffn_down_weight',
        'L0_ffn_residual_alpha']


def kernel(**inputs):
    import numpy as _np
    import concourse.bacc as _bacc
    from concourse import mybir as _mybir
    from concourse.bass_utils import run_bass_kernel_spmd as _run

    nc = _bacc.Bacc("TRN2", target_bir_lowering=False, num_devices=1)
    laid = {n: _np.asarray(inputs[n]) for n in _INS}
    laid['L0_attn_x'] = laid['L0_attn_x'].reshape(B * S, P)
    laid['L0_ffn_router_weight'] = laid['L0_ffn_router_weight'].T
    laid['L0_ffn_gate_up_weight'] = laid['L0_ffn_gate_up_weight'].transpose(2, 0, 1)
    laid['L0_ffn_down_weight'] = laid['L0_ffn_down_weight'].transpose(0, 2, 1)
    laid['L0_ffn_residual_alpha'] = laid['L0_ffn_residual_alpha'].reshape(1)
    arrays, args = {}, []
    for name in _INS:
        a = _np.ascontiguousarray(laid[name])
        arrays[f"in_{name}_dram"] = a
        args.append(nc.dram_tensor(f"in_{name}_dram", a.shape, _mybir.dt.from_np(a.dtype), kind="ExternalInput").ap())
    bh = _np.arange(P)
    masks = {"conv_rows": _np.ascontiguousarray(_np.stack(
                 [_np.asarray(inputs[f'L0_attn_{n}_conv']).T for n in 'qkv'])),
             "head_mask": (bh[:, None] % H == bh[None, :] // D).astype(_np.float32),
             "batch_mask": (bh[:, None] // H == _np.arange(B)[None, :]).astype(_np.float32)}
    for name, a in masks.items():
        arrays[f"in_{name}_dram"] = a
        args.append(nc.dram_tensor(f"in_{name}_dram", a.shape, _mybir.dt.from_np(a.dtype), kind="ExternalInput").ap())
    res = nc.dram_tensor("out_0_dram", (B * S, P), F32, kind="ExternalOutput").ap()
    build(nc, *args, res)
    r = _run(nc, [arrays], core_ids=[0])
    return r.results[0]["out_0_dram"].reshape(B, S, P)
```
